# Optimizing a Trainium2 kernel written in Bass

```python
import numpy as np
import jax
import jax.numpy as jnp

def _softmax(x, axis=-1):
    return jax.nn.softmax(x, axis=axis)
def _gelu(x):
    return jax.nn.gelu(x, approximate=True)
def _silu(x):
    return jax.nn.silu(x)
def _sigmoid(x):
    return jax.nn.sigmoid(x)
def _layernorm(x, axis=-1, eps=1e-5):
    m = jnp.mean(x, axis=axis, keepdims=True)
    v = jnp.var(x, axis=axis, keepdims=True)
    return (x - m) / jnp.sqrt(v + eps)
def _scatter_add(tgt, idx, src, axis=0):
    return tgt.at[idx].add(src)
def _segment_sum(src, seg, n):
    return jax.ops.segment_sum(src, seg, n)

kernel_name = 'mk_conv_seq_d2_conv_nchw192_f1c970'

def setup_inputs(seed: int = 0):
    np.random.seed(seed)
    _w = jnp.asarray
    def _rec_inputs():
        import jax
        import jax.numpy as jnp
        _gk = jax.random.key(seed)
        x = -0.0005058 + 1 * jax.random.normal(jax.random.fold_in(_gk, 1), (8, 192, 48, 48), jnp.float32)
        return x
    x = _rec_inputs()
    def _L0_conv_setup():
        import jax, jax.numpy as jnp
        import numpy as np
        import math
        D_MODEL = 192
        D_STATE = 16
        D_CONV = 3
        D_INNER = 2 * D_MODEL
        DT_RANK = math.ceil(D_MODEL / 16)
        BATCH, HH, WW = (8, 48, 48)
        DT_MIN, DT_MAX = (0.001, 0.1)
        EPS = 1e-05

        def _silu(v):
            return v * jax.nn.sigmoid(v)

        def _selective_scan(u, delta, A, Bp, Cp, D_param):
            deltaA = jnp.exp(delta[..., None] * A)
            deltaBu = (delta * u)[..., None] * Bp[:, :, None, :]
            a_seq = jnp.moveaxis(deltaA, 1, 0)
            b_seq = jnp.moveaxis(deltaBu, 1, 0)
            c_seq = jnp.moveaxis(Cp, 1, 0)

            def step(h, abc):
                a_t, b_t, c_t = abc
                h = a_t * h + b_t
                y = jnp.einsum('bds,bs->bd', h, c_t)
                return (h, y)
            h0 = jnp.zeros(u.shape[:1] + (u.shape[2], A.shape[1]), dtype=u.dtype)
            _, ys = jax.lax.scan(step, h0, (a_seq, b_seq, c_seq))
            return jnp.moveaxis(ys, 0, 1) + u * D_param
        key = jax.random.key(seed)
        ks = jax.random.split(key, 10)
        x = jax.random.normal(ks[0], (BATCH, D_MODEL, HH, WW), dtype=jnp.float32)
        in_proj_w = jax.random.normal(ks[1], (2 * D_INNER, D_MODEL), dtype=jnp.float32) * D_MODEL ** (-0.5)
        conv_w = jax.random.normal(ks[2], (D_INNER, 1, D_CONV, D_CONV), dtype=jnp.float32) * (1.0 / 3.0)
        conv_b = jnp.zeros((D_INNER,), dtype=jnp.float32)
        x_proj_w = jax.random.normal(ks[3], (DT_RANK + 2 * D_STATE, D_INNER), dtype=jnp.float32) * D_INNER ** (-0.5)
        dt_std = DT_RANK ** (-0.5)
        dt_proj_w = jax.random.uniform(ks[4], (D_INNER, DT_RANK), dtype=jnp.float32, minval=-dt_std, maxval=dt_std)
        u = jax.random.uniform(ks[5], (D_INNER,), dtype=jnp.float32)
        dt_proj_b = jnp.exp(u * (math.log(DT_MAX) - math.log(DT_MIN)) + math.log(DT_MIN))
        A_log = jnp.log(jnp.tile(jnp.arange(1, D_STATE + 1, dtype=jnp.float32)[None, :], (D_INNER, 1)))
        D_param = jnp.ones((D_INNER,), dtype=jnp.float32)
        ln_g = jnp.ones((D_INNER,), dtype=jnp.float32)
        ln_b = jnp.zeros((D_INNER,), dtype=jnp.float32)
        out_proj_w = jax.random.normal(ks[6], (D_MODEL, D_INNER), dtype=jnp.float32) * D_INNER ** (-0.5)
        fuse_w = jax.random.normal(ks[7], (D_MODEL, D_MODEL, 1, 1), dtype=jnp.float32) * D_MODEL ** (-0.5)
        fuse_b = jnp.zeros((D_MODEL,), dtype=jnp.float32)
        return dict(x=x, in_proj_w=in_proj_w, conv_w=conv_w, conv_b=conv_b, x_proj_w=x_proj_w, dt_proj_w=dt_proj_w, dt_proj_b=dt_proj_b, A_log=A_log, D_param=D_param, ln_g=ln_g, ln_b=ln_b, out_proj_w=out_proj_w, fuse_w=fuse_w, fuse_b=fuse_b)
    _L0_conv_all = _L0_conv_setup()
    _L0_conv_in = {k: v for k, v in _L0_conv_all.items() if k in ('in_proj_w', 'conv_w', 'conv_b', 'x_proj_w', 'dt_proj_w', 'dt_proj_b', 'A_log', 'D_param', 'ln_g', 'ln_b', 'out_proj_w', 'fuse_w', 'fuse_b', )}
    del _L0_conv_all

    def _L1_conv_setup():
        import jax, jax.numpy as jnp
        import numpy as np
        B, DIM, H, W = (2, 192, 256, 256)
        WIN = 4
        EPS = 1e-05

        def _cd_conj(x):
            if len(x) == 1:
                return x
            h = len(x) // 2
            return np.concatenate([_cd_conj(x[:h]), -x[h:]])

        def _cd_mult(a, b):
            n = len(a)
            if n == 1:
                return a * b
            h = n // 2
            a1, a2, b1, b2 = (a[:h], a[h:], b[:h], b[h:])
            c1 = _cd_mult(a1, b1) - _cd_mult(_cd_conj(b2), a2)
            c2 = _cd_mult(b2, a1) + _cd_mult(a2, _cd_conj(b1))
            return np.concatenate([c1, c2])

        def _sedenion_table(n=16):
            eye = np.eye(n, dtype=np.float32)
            M = np.zeros((n, n, n), dtype=np.float32)
            for i in range(n):
                for j in range(n):
                    M[i, j] = _cd_mult(eye[i], eye[j])
            return M
        SED_TABLE = jnp.asarray(_sedenion_table(16))

        def layer_norm(x, g, b):
            m = x.mean(-1, keepdims=True)
            v = ((x - m) ** 2).mean(-1, keepdims=True)
            return (x - m) * jax.lax.rsqrt(v + EPS) * g + b

        def get_window(x):
            b, c, h, w = x.shape
            x = x.reshape(b, c, h // WIN, WIN, w // WIN, WIN)
            x = x.transpose(0, 2, 4, 3, 5, 1)
            return x.reshape(b, h // WIN, w // WIN, WIN * WIN * c)

        def reverse_window(x, c):
            b, hh, ww, _ = x.shape
            x = x.reshape(b, hh, ww, WIN, WIN, c)
            x = x.transpose(0, 5, 1, 3, 2, 4)
            return x.reshape(b, c, hh * WIN, ww * WIN)

        def sedenion_full_weight(w_sed):
            d = w_sed.shape[1]
            wf = jnp.einsum('ijk,jde->idke', SED_TABLE, w_sed)
            return wf.reshape(16 * d, 16 * w_sed.shape[2])
        key = jax.random.key(seed)
        ks = jax.random.split(key, 8)
        d, dh = (DIM, 4 * DIM)
        s = 0.02
        return {'x': jax.random.normal(ks[0], (B, DIM, H, W), jnp.float32), 'norm1_g': jnp.ones((d,), jnp.float32), 'norm1_b': jnp.zeros((d,), jnp.float32), 'w_sed': jax.random.normal(ks[1], (16, d, d), jnp.float32) * s, 'proj_w': jax.random.normal(ks[2], (d, d), jnp.float32) * s, 'proj_b': jnp.zeros((d,), jnp.float32), 'norm2_g': jnp.ones((d,), jnp.float32), 'norm2_b': jnp.zeros((d,), jnp.float32), 'fc1_w': jax.random.normal(ks[3], (d, dh), jnp.float32) * s, 'fc1_b': jnp.zeros((dh,), jnp.float32), 'fc2_w': jax.random.normal(ks[4], (dh, d), jnp.float32) * s, 'fc2_b': jnp.zeros((d,), jnp.float32)}
    _L1_conv_all = _L1_conv_setup()
    _L1_conv_in = {k: v for k, v in _L1_conv_all.items() if k in ('norm1_g', 'norm1_b', 'w_sed', 'proj_w', 'proj_b', 'norm2_g', 'norm2_b', 'fc1_w', 'fc1_b', 'fc2_w', 'fc2_b', )}
    del _L1_conv_all

    return {
        "x": x,
        "L0_conv_in_proj_w": _L0_conv_in["in_proj_w"],
        "L0_conv_conv_w": _L0_conv_in["conv_w"],
        "L0_conv_conv_b": _L0_conv_in["conv_b"],
        "L0_conv_x_proj_w": _L0_conv_in["x_proj_w"],
        "L0_conv_dt_proj_w": _L0_conv_in["dt_proj_w"],
        "L0_conv_dt_proj_b": _L0_conv_in["dt_proj_b"],
        "L0_conv_A_log": _L0_conv_in["A_log"],
        "L0_conv_D_param": _L0_conv_in["D_param"],
        "L0_conv_ln_g": _L0_conv_in["ln_g"],
        "L0_conv_ln_b": _L0_conv_in["ln_b"],
        "L0_conv_out_proj_w": _L0_conv_in["out_proj_w"],
        "L0_conv_fuse_w": _L0_conv_in["fuse_w"],
        "L0_conv_fuse_b": _L0_conv_in["fuse_b"],
        "L1_conv_norm1_g": _L1_conv_in["norm1_g"],
        "L1_conv_norm1_b": _L1_conv_in["norm1_b"],
        "L1_conv_w_sed": _L1_conv_in["w_sed"],
        "L1_conv_proj_w": _L1_conv_in["proj_w"],
        "L1_conv_proj_b": _L1_conv_in["proj_b"],
        "L1_conv_norm2_g": _L1_conv_in["norm2_g"],
        "L1_conv_norm2_b": _L1_conv_in["norm2_b"],
        "L1_conv_fc1_w": _L1_conv_in["fc1_w"],
        "L1_conv_fc1_b": _L1_conv_in["fc1_b"],
        "L1_conv_fc2_w": _L1_conv_in["fc2_w"],
        "L1_conv_fc2_b": _L1_conv_in["fc2_b"],
    }

def reference(x, L0_conv_in_proj_w, L0_conv_conv_w, L0_conv_conv_b, L0_conv_x_proj_w, L0_conv_dt_proj_w, L0_conv_dt_proj_b, L0_conv_A_log, L0_conv_D_param, L0_conv_ln_g, L0_conv_ln_b, L0_conv_out_proj_w, L0_conv_fuse_w, L0_conv_fuse_b, L1_conv_norm1_g, L1_conv_norm1_b, L1_conv_w_sed, L1_conv_proj_w, L1_conv_proj_b, L1_conv_norm2_g, L1_conv_norm2_b, L1_conv_fc1_w, L1_conv_fc1_b, L1_conv_fc2_w, L1_conv_fc2_b):
    import jax
    import jax.numpy as jnp
    def _L0_conv_ref(x, in_proj_w, conv_w, conv_b, x_proj_w, dt_proj_w, dt_proj_b, A_log, D_param, ln_g, ln_b, out_proj_w, fuse_w, fuse_b):
        import jax, jax.numpy as jnp
        import numpy as np
        import math
        D_MODEL = 192
        D_STATE = 16
        D_CONV = 3
        D_INNER = 2 * D_MODEL
        DT_RANK = math.ceil(D_MODEL / 16)
        BATCH, HH, WW = (8, 48, 48)
        DT_MIN, DT_MAX = (0.001, 0.1)
        EPS = 1e-05

        def _silu(v):
            return v * jax.nn.sigmoid(v)

        def _selective_scan(u, delta, A, Bp, Cp, D_param):
            deltaA = jnp.exp(delta[..., None] * A)
            deltaBu = (delta * u)[..., None] * Bp[:, :, None, :]
            a_seq = jnp.moveaxis(deltaA, 1, 0)
            b_seq = jnp.moveaxis(deltaBu, 1, 0)
            c_seq = jnp.moveaxis(Cp, 1, 0)

            def step(h, abc):
                a_t, b_t, c_t = abc
                h = a_t * h + b_t
                y = jnp.einsum('bds,bs->bd', h, c_t)
                return (h, y)
            h0 = jnp.zeros(u.shape[:1] + (u.shape[2], A.shape[1]), dtype=u.dtype)
            _, ys = jax.lax.scan(step, h0, (a_seq, b_seq, c_seq))
            return jnp.moveaxis(ys, 0, 1) + u * D_param
        Bn, C, H, W = x.shape
        L = H * W
        x_hwc = jnp.transpose(x, (0, 2, 3, 1))
        xz = jnp.einsum('bhwc,oc->bhwo', x_hwc, in_proj_w)
        xin, z = jnp.split(xz, 2, axis=-1)
        xin_c = jnp.transpose(xin, (0, 3, 1, 2))
        conv = jax.lax.conv_general_dilated(xin_c, conv_w, window_strides=(1, 1), padding='SAME', feature_group_count=D_INNER, dimension_numbers=('NCHW', 'OIHW', 'NCHW')) + conv_b[None, :, None, None]
        xact = _silu(conv)
        x_flat = jnp.transpose(xact.reshape(Bn, D_INNER, L), (0, 2, 1))
        xp = jnp.einsum('bld,od->blo', x_flat, x_proj_w)
        dt_low = xp[..., :DT_RANK]
        Bp = xp[..., DT_RANK:DT_RANK + D_STATE]
        Cp = xp[..., DT_RANK + D_STATE:]
        dt = jnp.einsum('blr,dr->bld', dt_low, dt_proj_w)
        delta = jax.nn.softplus(dt + dt_proj_b)
        A = -jnp.exp(A_log)
        y = _selective_scan(x_flat, delta, A, Bp, Cp, D_param)
        out = y.reshape(Bn, H, W, D_INNER)
        mu = out.mean(axis=-1, keepdims=True)
        var = out.var(axis=-1, keepdims=True)
        out = (out - mu) * jax.lax.rsqrt(var + EPS) * ln_g + ln_b
        out = out * _silu(z)
        out = jnp.einsum('bhwd,od->bhwo', out, out_proj_w)
        out_c = jnp.transpose(out, (0, 3, 1, 2))
        fused = jnp.einsum('bchw,oc->bohw', out_c, fuse_w[:, :, 0, 0]) + fuse_b[None, :, None, None]
        m = fused.mean(axis=(2, 3), keepdims=True)
        v = fused.var(axis=(2, 3), keepdims=True)
        normed = (fused - m) * jax.lax.rsqrt(v + EPS)
        return x + normed

    def _L1_conv_ref(x, norm1_g, norm1_b, w_sed, proj_w, proj_b, norm2_g, norm2_b, fc1_w, fc1_b, fc2_w, fc2_b):
        import jax, jax.numpy as jnp
        import numpy as np
        B, DIM, H, W = (2, 192, 256, 256)
        WIN = 4
        EPS = 1e-05

        def _cd_conj(x):
            if len(x) == 1:
                return x
            h = len(x) // 2
            return np.concatenate([_cd_conj(x[:h]), -x[h:]])

        def _cd_mult(a, b):
            n = len(a)
            if n == 1:
                return a * b
            h = n // 2
            a1, a2, b1, b2 = (a[:h], a[h:], b[:h], b[h:])
            c1 = _cd_mult(a1, b1) - _cd_mult(_cd_conj(b2), a2)
            c2 = _cd_mult(b2, a1) + _cd_mult(a2, _cd_conj(b1))
            return np.concatenate([c1, c2])

        def _sedenion_table(n=16):
            eye = np.eye(n, dtype=np.float32)
            M = np.zeros((n, n, n), dtype=np.float32)
            for i in range(n):
                for j in range(n):
                    M[i, j] = _cd_mult(eye[i], eye[j])
            return M
        SED_TABLE = jnp.asarray(_sedenion_table(16))

        def layer_norm(x, g, b):
            m = x.mean(-1, keepdims=True)
            v = ((x - m) ** 2).mean(-1, keepdims=True)
            return (x - m) * jax.lax.rsqrt(v + EPS) * g + b

        def get_window(x):
            b, c, h, w = x.shape
            x = x.reshape(b, c, h // WIN, WIN, w // WIN, WIN)
            x = x.transpose(0, 2, 4, 3, 5, 1)
            return x.reshape(b, h // WIN, w // WIN, WIN * WIN * c)

        def reverse_window(x, c):
            b, hh, ww, _ = x.shape
            x = x.reshape(b, hh, ww, WIN, WIN, c)
            x = x.transpose(0, 5, 1, 3, 2, 4)
            return x.reshape(b, c, hh * WIN, ww * WIN)

        def sedenion_full_weight(w_sed):
            d = w_sed.shape[1]
            wf = jnp.einsum('ijk,jde->idke', SED_TABLE, w_sed)
            return wf.reshape(16 * d, 16 * w_sed.shape[2])
        b, c, h, w = x.shape
        xn = layer_norm(x.transpose(0, 2, 3, 1), norm1_g, norm1_b).transpose(0, 3, 1, 2)
        xw = get_window(xn)
        wf = sedenion_full_weight(w_sed)
        xw = xw @ wf
        x1 = reverse_window(xw, c)
        y = x1.transpose(0, 2, 3, 1)
        y = jax.nn.gelu(y, approximate=False)
        y = y @ proj_w + proj_b
        x = x + y.transpose(0, 3, 1, 2)
        hbr = layer_norm(x.transpose(0, 2, 3, 1), norm2_g, norm2_b)
        hbr = jax.nn.gelu(hbr @ fc1_w + fc1_b, approximate=False)
        hbr = hbr @ fc2_w + fc2_b
        x = x + hbr.transpose(0, 3, 1, 2)
        return x

    def _gn(v, G=32, eps=1e-5):
        B_, C_, H_, W_ = v.shape
        g = v.reshape(B_, G, C_ // G, H_, W_)
        m = jnp.mean(g, axis=(2, 3, 4), keepdims=True)
        s = jnp.var(g, axis=(2, 3, 4), keepdims=True)
        return ((g - m) / jnp.sqrt(s + eps)).reshape(v.shape)

    def _ln_c(v, eps=1e-6):
        m = jnp.mean(v, axis=1, keepdims=True)
        s = jnp.var(v, axis=1, keepdims=True)
        return (v - m) / jnp.sqrt(s + eps)

    def _ln_t(v, eps=1e-5):
        m = jnp.mean(v, axis=-1, keepdims=True)
        s = jnp.var(v, axis=-1, keepdims=True)
        return (v - m) / jnp.sqrt(s + eps)

    def _to_tokens(v):
        B_, C_, H_, W_ = v.shape
        return v.reshape(B_, C_, H_ * W_).transpose(0, 2, 1)
    def _from_tokens(t, like):
        B_, C_, H_, W_ = like.shape
        return t.transpose(0, 2, 1).reshape(B_, C_, H_, W_)

    x = _L0_conv_ref(x, L0_conv_in_proj_w, L0_conv_conv_w, L0_conv_conv_b, L0_conv_x_proj_w, L0_conv_dt_proj_w, L0_conv_dt_proj_b, L0_conv_A_log, L0_conv_D_param, L0_conv_ln_g, L0_conv_ln_b, L0_conv_out_proj_w, L0_conv_fuse_w, L0_conv_fuse_b)
    x = _L1_conv_ref(x, L1_conv_norm1_g, L1_conv_norm1_b, L1_conv_w_sed, L1_conv_proj_w, L1_conv_proj_b, L1_conv_norm2_g, L1_conv_norm2_b, L1_conv_fc1_w, L1_conv_fc1_b, L1_conv_fc2_w, L1_conv_fc2_b)
    return x


_drawn_inputs = setup_inputs


def setup_inputs(seed=0):
    import zlib

    import numpy as np

    out = dict(_drawn_inputs(seed))
    spreads = {'L0_conv_conv_b': (0.0, 0.1),
     'L0_conv_D_param': (1.0, 0.2),
     'L0_conv_ln_g': (1.0, 0.2),
     'L0_conv_ln_b': (0.0, 0.1),
     'L0_conv_fuse_b': (0.0, 0.8),
     'L1_conv_norm1_g': (1.0, 0.2),
     'L1_conv_norm1_b': (0.0, 0.612),
     'L1_conv_proj_b': (0.0, 0.1),
     'L1_conv_norm2_g': (1.0, 0.6),
     'L1_conv_norm2_b': (0.0, 0.8),
     'L1_conv_fc1_b': (0.0, 0.39),
     'L1_conv_fc2_b': (0.0, 0.1)}
    factors = {'L0_conv_dt_proj_b': 3.587}
    for name, (base, spread) in spreads.items():
        noise = np.random.default_rng([zlib.crc32(name.encode()), seed]).standard_normal(out[name].shape)
        drawn = base * np.exp(spread * noise) if base else spread * noise
        out[name] = jnp.asarray(drawn.astype(out[name].dtype))
    for name, factor in factors.items():
        out[name] = (out[name] * factor).astype(out[name].dtype)
    return out
```

```python
from contextlib import ExitStack

import numpy as np

import concourse.bass as bass
from concourse import mybir
from concourse.alu_op_type import AluOpType as ALU

F32 = mybir.dt.float32
F32R = mybir.dt.float32r
ACT = mybir.ActivationFunctionType
AX = mybir.AxisListType

P = 128
CH, HALF = 192, 64
IMG, SIDE = 8, 48
DI, ST, RANK = 384, 16, 12
ND = DI // P
ROWS = 8
TC = ROWS * SIDE
TH = (ROWS + 2) * SIDE
NCH = SIDE // ROWS
BANK = 512
RING = 4
EPS = 1e-5
TOK = SIDE * SIDE
WIN = 4
NW = SIDE // WIN
WT = NW * NW
NK = WIN * WIN
GT = 2 * WT
NG = NK // 2
BL, NB = 96, 3
HID = 4 * CH
NM = HID // P
TURN = 4



class At:

    def __init__(self, off, reg=None, mult=0):
        self.off, self.reg, self.mult = off, reg, mult

    def linear(self, k, c):
        c = k * self.off + c
        return c if self.reg is None else self.reg * (self.mult * k) + c

    def later(self):
        return self.reg is not None or self.off > 0

    def shift(self, d):
        return At(self.off + d, self.reg, self.mult)


class Count:

    def __init__(self, sem, when, events):
        self.sem, self.when, self.events = sem, when, events

    def _at(self, step, name, after):
        total, const = 0, 0
        inside, found = 0, False
        for ev, kind, w in self.events:
            first, last = self.when[kind]
            if step.reg is None:
                const += w * min(max(step.off - first, 0), last - first + 1)
                on = first <= step.off <= last
            else:
                total += w
                const -= w * first
                on = True
            if found:
                continue
            if ev == name:
                found = True
                inside += w if after and on else 0
            else:
                inside += w if on else 0
        assert found, name
        return const + inside if step.reg is None else step.linear(total, const + inside)

    def after(self, step, name):
        return self._at(step, name, True)

    def before(self, step, name):
        return self._at(step, name, False)


def held(eng, value):
    return value if isinstance(value, int) else eng.to_reg(value)


def layer0(nc, d, nimg):
    NS = nimg * NCH
    when = {"X": (-2, NS - 3), "A": (-1, NS - 2), "S": (0, NS - 1), "O": (1, NS)}
    ctx = ExitStack()
    with ctx:
        def sb(name, shape, dt=F32):
            return ctx.enter_context(nc.sbuf_tensor(name, shape, dt))

        def ps(name, shape):
            return ctx.enter_context(nc.psum_tensor(name, shape, F32))

        def sem(name):
            return ctx.enter_context(nc.semaphore(name))

        def count(name, events):
            return Count(sem(name), when, events)

        win_a, win_b = sb("win_a", [P, 2 * DI]), sb("win_b", [HALF, 2 * DI])
        cw, diag = sb("cw", [P, ND, 9]), sb("diag", [P, ND, 9, P])
        xpw = sb("xpw", [P, ND, RANK + 2 * ST])
        dtw = sb("dtw", [RANK, DI])
        opw_a, opw_b = sb("opw_a", [P, DI]), sb("opw_b", [HALF, DI])
        fuw_a, fuw_b = sb("fuw_a", [P, CH]), sb("fuw_b", [HALF, CH])
        wout = sb("wout", [P, ND, CH])
        vecs = sb("vecs", [P, 5, ND])
        fub = sb("fub", [P, 2])
        alog = sb("alog", [P, ND, ST])
        aneg = sb("aneg", [P, ND, ST])
        ident = sb("ident", [P, P])
        pick, pick_r = sb("pick", [4 * ST, 2 * ST]), sb("pick_r", [4 * ST, 2 * ST], F32R)
        keep = sb("keep", [P, NS * ND])
        mhalf = sb("mhalf", [P, ND])
        xc_a, xc_b = sb("xc_a", [P, TH]), sb("xc_b", [HALF, TH])
        xz_a, xz_b = sb("xz_a", [P, TC]), sb("xz_b", [HALF, TC])
        xin = sb("xin", [P, ND, ROWS + 2, SIDE + 2])
        pre, u = sb("pre", [P, ND, TC]), sb("u", [P, ND, TC])
        dtl = sb("dtl", [RANK, TC])
        soft = sb("soft", [P, ND, TC])
        soft2 = sb("soft2", [P, ND, TC])
        delta = sb("delta", [P, 2, ND, TC])
        du = sb("du", [P, 2, ND, TC])
        bc = sb("bc", [4 * ST, 2, TC], F32R)
        brow = sb("brow", [P, RING, TC])
        drive = sb("drive", [P, RING, ND, TC])
        hst = sb("hst", [P, RING, ND, TC])
        carry = sb("carry", [P, ST, ND])
        part = sb("part", [P, 6, ND, TC])
        ysum = sb("ysum", [P, ND, TC])
        zpre, sz = sb("zpre", [P, ND, TC]), sb("sz", [P, ND, TC])
        yt = sb("yt", [P, ND, DI])
        st6, mv = sb("st6", [P, ND, 6]), sb("mv", [P, ND, 2])
        rstd = sb("rstd", [P, 2, ND])
        og = sb("og", [P, ND, TC])
        fz = sb("fz", [P, 2, TC])
        decay = ps("decay", [P, ND, BANK])
        bps = ps("bps", [P, BANK])
        cps = ps("cps", [P, 2, BANK])
        fill = ps("fill", [P, 2, BANK])

        loaded, prepared, merged, mergedone = sem("loaded"), sem("prepared"), sem("merged"), sem("mergedone")
        alogged = sem("alogged")
        uses = [("conv0", "A", 0), ("yT0", "O", 1), ("yT1", "O", 1), ("conv1", "A", 0), ("yT2", "O", 1),
                ("conv2", "A", 0), ("xp", "A", 1), ("z0", "S", 0), ("dt0", "A", 1), ("dt1", "A", 0),
                ("dt2", "A", 1), ("back0", "O", 0), ("back1", "O", 1), ("back2", "O", 0), ("z1", "S", 1),
                ("xin0", "X", 0), ("z2", "S", 1), ("out0", "O", 0), ("xin1", "X", 1), ("out1", "O", 0),
                ("xin2", "X", 1)]
        bank_of = {name: bank for name, _, bank in uses}
        filled = count("filled", [(name, kind, 1) for name, kind, _ in uses])
        xc_in = count("xc_in", [("x", "X", 32)])
        xz_in = count("xz_in", [("x", "S", 32)])
        ahead = lambda k: [(f"{s}", "S", 1) for s in range(k, ST)] + [(f"{s}", "A", 1) for s in range(k)]
        b_spread, b_copied, driven = count("b_spread", ahead(5)), count("b_copied", ahead(4)), count("driven", ahead(3))
        c_spread = count("c_spread", [(f"{s}", "S", 1) for s in range(ST)])
        decayed = count("decayed", [(f"{s}.{m}", "S", 1) for s in range(ST) for m in range(ND)])
        scanned = count("scanned", [(f"{s}.{m}", "S", 1) for s in range(ST) for m in range(ND)])
        scaled = count("scaled", [(f"{s}", "S", 1) for s in range(ST)])
        summed = count("summed", [(f"{g}", "S", 1) for g in range(4)])
        carried = count("carried", [(f"{ST - 1}", "O", 1)] + [(f"{s}", "S", 1) for s in range(ST - 1)])
        xin_set = count("xin_set", [(f"{m}", "X", 1) for m in range(ND)])
        pre_set = count("pre_set", [(f"{m}", "A", 1) for m in range(ND)])
        u_set = count("u_set", [("u", "A", 1)])
        sz_set = count("sz_set", [("sz", "O", 1)])
        zpre_set = count("zpre_set", [(f"{m}", "S", 1) for m in range(ND)])
        bchi, bclo, dtl_set = count("bchi", [("x", "A", 1)]), count("bclo", [("x", "A", 1)]), count("dtl_set", [("x", "A", 1)])
        dt_set = count("dt_set", [(f"{m}", "A", 1) for m in range(ND)])
        abs_set = count("abs_set", [("x", "A", 1)])
        exp_set, ln_set = count("exp_set", [("x", "A", 1)]), count("ln_set", [("x", "A", 1)])
        relu_set = count("relu_set", [("x", "A", 1)])
        delta_set, du_set, ud_set = count("delta_set", [("x", "A", 1)]), count("du_set", [("x", "A", 1)]), count("ud_set", [("x", "A", 1)])
        yt_set = count("yt_set", [(f"{j}", "O", 1) for j in range(ND)])
        stat_set = count("stat_set", [(f"{j}", "O", 1) for j in range(ND)])
        mv_set = count("mv_set", [("x", "O", 1)])
        veps_set, rstd_set = count("veps_set", [("x", "O", 1)]), count("rstd_set", [("x", "O", 1)])
        normed = count("normed", [(f"{j}", "O", 1) for j in range(ND)])
        affined = count("affined", [(f"{m}", "O", 1) for m in range(ND)])
        gated = count("gated", [("x", "O", 1)])
        fz_set = count("fz_set", [("0", "O", 1), ("1", "O", 1)])
        stored = count("stored", [("x", "O", 32)])
        NLOADS = 16

        def readers(name):
            what, i = name.rstrip("012"), name[-1]
            return {"yT": [(yt_set, i)], "xin": [(xin_set, i)], "conv": [(pre_set, i)], "xp": [(dtl_set, "x"), (bclo, "x")],
                    "back": [(affined, i)], "dt": [(dt_set, i)], "out": [(fz_set, i)],
                    "z": [(zpre_set, i)]}[what]

        def before_it(n, name):
            names = [name for name, _, _ in uses]
            kinds = {name: kind for name, kind, _ in uses}
            for back in range(3):
                step = n.shift(-back)
                upto = names.index(name) if back == 0 else len(names)
                for other in reversed(names[:upto]):
                    if bank_of[other] == bank_of[name] and on(kinds[other], step):
                        return step, other
            return None

        def on(kind, n):
            return n.reg is not None or when[kind][0] <= n.off <= when[kind][1]

        def steps(eng, emit):
            for n in range(-2, 2):
                emit(At(n), n % 2)
            with eng.Fori(0, (NS - 4) // 2) as m:
                emit(At(2, m, 2), 0)
                emit(At(3, m, 2), 1)
            emit(At(NS - 2), NS % 2)
            emit(At(NS - 1), (NS - 1) % 2)
            emit(At(NS), NS % 2)

        block = ctx.enter_context(nc.Block())

        @block.sync
        def _(sp):
            for dst, src in [(win_a, d["win"][0:P]), (win_b, d["win"][P:CH]), (cw, d["cw"]), (xpw, d["xpw"]),
                             (dtw, d["dtw"]), (opw_a, d["opw"][0:P]), (opw_b, d["opw"][P:CH]),
                             (fuw_a, d["fuw"][0:P]), (fuw_b, d["fuw"][P:CH]), (vecs, d["vecs"]),
                             (alog, d["alog"]), (ident, d["ident"]), (pick, d["pick"]),
                             (keep, d["keep"])]:
                sp.dma_start(dst[:], src).then_inc(loaded, 16)
            sp.dma_start(fub[:, 0:1], d["fub"][0:P]).then_inc(loaded, 16)
            sp.dma_start(fub[0:HALF, 1:2], d["fub"][P:CH]).then_inc(loaded, 16)

            def emit(n, par):
                if on("X", n):
                    if n.reg is not None or n.off > -2:
                        xc_in_value = held(sp, xc_in.after(n.shift(-1), "x"))
                        filled_value = held(sp, filled.after(n.shift(-1), "xin2"))
                        sp.wait_ge(loaded, 16 * NLOADS)
                        sp.wait_ge(xc_in.sem, xc_in_value)
                        sp.wait_ge(filled.sem, filled_value)
                    j = n.linear(1, 2)
                    sp.dma_start(xc_a[:], d["xch"][j, 0:P, :]).then_inc(xc_in.sem, 16)
                    sp.dma_start(xc_b[:], d["xch"][j, P:CH, :]).then_inc(xc_in.sem, 16)
                if on("S", n):
                    if n.reg is not None or n.off > 0:
                        xz_in_value = held(sp, xz_in.after(n.shift(-1), "x"))
                        filled_value = held(sp, filled.after(n.shift(-1), "z2"))
                        sp.wait_ge(loaded, 16 * NLOADS)
                        sp.wait_ge(xz_in.sem, xz_in_value)
                        sp.wait_ge(filled.sem, filled_value)
                    j = n.linear(1, 0)
                    sp.dma_start(xz_a[:], d["xch"][j, 0:P, SIDE:SIDE + TC]).then_inc(xz_in.sem, 16)
                    sp.dma_start(xz_b[:], d["xch"][j, P:CH, SIDE:SIDE + TC]).then_inc(xz_in.sem, 16)
                if on("O", n):
                    sp.wait_ge(fz_set.sem, fz_set.after(n, "1"))
                    j = n.linear(1, -1)
                    sp.dma_start(d["fz"][j, 0:P, :], fz[:, 0, :]).then_inc(stored.sem, 16)
                    sp.dma_start(d["fz"][j, P:CH, :], fz[0:HALF, 1, :]).then_inc(stored.sem, 16)

            steps(sp, emit)
            sp.wait_ge(stored.sem, stored.after(At(NS), "x"))

        @block.tensor
        def _(pe):
            pe.wait_ge(loaded, 16 * NLOADS)
            for m in range(ND):
                if m >= 2:
                    pe.wait_ge(mergedone, m - 1)
                o = fill[:, m % 2, 0:CH]
                nc.tensor.matmul(o, opw_a[:, bass.ts(m, P)], fuw_a[:], start=True, stop=False)
                nc.tensor.matmul(o, opw_b[:, bass.ts(m, P)], fuw_b[:], start=False, stop=True).then_inc(merged, 1)
            pe.wait_ge(mergedone, ND)
            pe.wait_ge(prepared, 3)

            def use(n, name):
                held = before_it(n, name)
                for c, event in readers(held[1]) if held else []:
                    pe.wait_ge(c.sem, c.after(held[0], event))
                return fill[:, bank_of[name], :]

            def y_back(n, j):
                o = use(n, f"yT{j}")
                for m in range(ND):
                    last = nc.tensor.transpose(o[:, bass.ts(m, P)], ysum[:, m, bass.ts(j, P)], ident[:])
                last.then_inc(filled.sem, 1)

            def x_in(n, m):
                o = use(n, f"xin{m}")[:, 0:TH]
                nc.tensor.matmul(o, win_a[:, bass.ts(m, P)], xc_a[:], start=True, stop=False)
                nc.tensor.matmul(o, win_b[:, bass.ts(m, P)], xc_b[:], start=False, stop=True).then_inc(filled.sem, 1)

            def conv(n, m, first, end):
                o = use(n, f"conv{m}") if first == 0 else fill[:, bank_of[f"conv{m}"], :]
                if first == 0:
                    pe.wait_ge(xin_set.sem, xin_set.after(n.shift(-1), f"{m}"))
                for tap in range(first, end):
                    dy, dx = tap // 3, tap % 3
                    last = nc.tensor.matmul(o[:, 0:TC], diag[:, m, tap, :], xin[:, m, dy:dy + ROWS, dx:dx + SIDE],
                                            start=(tap == 0), stop=(tap == 8))
                if end == 9:
                    last.then_inc(filled.sem, 1)

            def x_proj(n):
                o = use(n, "xp")
                pe.wait_ge(u_set.sem, u_set.after(n, "u"))
                for m in range(ND):
                    last = nc.tensor.matmul(o[0:2 * ST + RANK, 0:TC], xpw[:, m, :], u[:, m, :], start=(m == 0), stop=(m == ND - 1))
                last.then_inc(filled.sem, 1)

            def dt(n, m):
                o = use(n, f"dt{m}")
                if m == 0:
                    pe.wait_ge(dtl_set.sem, dtl_set.after(n, "x"))
                nc.tensor.matmul(o[:, 0:TC], dtw[:, bass.ts(m, P)], dtl[:], start=True, stop=True).then_inc(filled.sem, 1)

            def back(n, m):
                o = use(n, f"back{m}")
                if m == 0:
                    pe.wait_ge(normed.sem, normed.after(n, f"{ND - 1}"))
                for j in range(ND):
                    last = nc.tensor.transpose(o[:, bass.ts(j, P)], yt[:, j, bass.ts(m, P)], ident[:])
                last.then_inc(filled.sem, 1)

            def out(n, h):
                o = use(n, f"out{h}")
                if h == 0:
                    pe.wait_ge(gated.sem, gated.after(n, "x"))
                cols, lo = (P, 0) if h == 0 else (HALF, P)
                for m in range(ND):
                    last = nc.tensor.matmul(o[0:cols, 0:TC], wout[:, m, lo:lo + cols], og[:, m, :], start=(m == 0), stop=(m == ND - 1))
                last.then_inc(filled.sem, 1)

            def z_in(n, m):
                o = use(n, f"z{m}")[:, 0:TC]
                if m == 0:
                    pe.wait_ge(xz_in.sem, xz_in.after(n, "x"))
                nc.tensor.matmul(o, win_a[:, DI + m * P:DI + m * P + P], xz_a[:], start=True, stop=False)
                nc.tensor.matmul(o, win_b[:, DI + m * P:DI + m * P + P], xz_b[:], start=False, stop=True).then_inc(filled.sem, 1)

            def spread_b(n, s, par):
                pe.wait_ge(b_copied.sem, b_copied.after(n, "3") if s == 4 else b_copied.before(n, f"{s}"))
                if s == 0:
                    pe.wait_ge(bclo.sem, bclo.after(n, "x"))
                nc.tensor.matmul(bps[:, 0:TC], pick_r[:, s:s + 1].broadcast_to([4 * ST, P]), bc[:, par, :],
                                 start=True, stop=True).then_inc(b_spread.sem, 1)

            def spread_c(n, s, par):
                if s >= 2:
                    pe.wait_ge(scaled.sem, scaled.after(n, f"{s - 2}"))
                elif n.reg is not None or n.off > 0:
                    pe.wait_ge(scaled.sem, scaled.after(n.shift(-1), f"{s + ST - 2}"))
                nc.tensor.matmul(cps[:, s % 2, 0:TC], pick_r[:, ST + s:ST + s + 1].broadcast_to([4 * ST, P]), bc[:, par, :],
                                 start=True, stop=True).then_inc(c_spread.sem, 1)

            def emit(n, par):
                X, A, S, O = on("X", n), on("A", n), on("S", n), on("O", n)
                for s in range(ST):
                    if S:
                        spread_c(n, s, par)
                    if S and s + 5 < ST:
                        spread_b(n, s + 5, par)
                    if A and s + 5 >= ST:
                        spread_b(n, s + 5 - ST, 1 - par)
                    if A and s < 6:
                        m, late = s // 2, s % 2
                        conv(n, m, 4 * late, 4 + 5 * late)
                    if O and 1 <= s <= 3:
                        if s == 1:
                            pe.wait_ge(summed.sem, summed.after(n.shift(-1), "3"))
                        y_back(n, s - 1)
                    if A and s == 7:
                        x_proj(n)
                    if S and s == 8:
                        z_in(n, 0)
                    if A and s == 9:
                        dt(n, 0), dt(n, 1)
                    if A and s == 10:
                        dt(n, 2)
                    if O and s == 10:
                        back(n, 0)
                    if O and s == 11:
                        back(n, 1), back(n, 2)
                    if S and s == 12:
                        z_in(n, 1)
                    if X and s == 13:
                        pe.wait_ge(xc_in.sem, xc_in.after(n, "x"))
                        x_in(n, 0)
                    if S and s == 13:
                        z_in(n, 2)
                    if O and s >= 14:
                        out(n, s - 14)
                    if X and s >= 14:
                        x_in(n, s - 13)

            steps(pe, emit)

        @block.scalar
        def _(act):
            act.wait_ge(loaded, 16 * NLOADS)
            nc.scalar.activation(aneg[:], alog[:], ACT.Exp).then_inc(alogged, 1)
            act.wait_ge(prepared, 3)

            def filled_by(n, name):
                act.wait_ge(filled.sem, filled.after(n, name))
                return fill[:, bank_of[name], :]

            def more(n, first):
                return n.reg is not None or n.off > first

            def take_y(n, j):
                o = filled_by(n, f"yT{j}")
                if j == 0 and more(n, 1):
                    act.wait_ge(filled.sem, filled.after(n.shift(-1), "back2"))
                nc.scalar.activation(yt[:, j, :], o[:, 0:DI], ACT.Copy).then_inc(yt_set.sem, 1)

            def take_xin(n, m):
                o = filled_by(n, f"xin{m}")
                nc.scalar.activation(xin[:, m, :, 1:SIDE + 1], o[:, 0:TH].rearrange("p (r w) -> p r w", w=SIDE),
                                     ACT.Copy).then_inc(xin_set.sem, 1)

            def take_conv(n, m):
                o = filled_by(n, f"conv{m}")
                nc.scalar.activation(pre[:, m, :], o[:, 0:TC], ACT.Identity, bias=vecs[:, 0, m:m + 1]).then_inc(pre_set.sem, 1)

            def take_z(n, m):
                o = filled_by(n, f"z{m}")
                if m == 0 and on("O", n):
                    act.wait_ge(sz_set.sem, sz_set.after(n, "sz"))
                nc.scalar.activation(zpre[:, m, :], o[:, 0:TC], ACT.Copy).then_inc(zpre_set.sem, 1)

            def take_dt(n, m):
                o = filled_by(n, f"dt{m}")
                if m == 0 and more(n, -1):
                    act.wait_ge(relu_set.sem, relu_set.after(n.shift(-1), "x"))
                nc.scalar.activation(soft[:, m, :], o[:, 0:TC], ACT.Identity, bias=vecs[:, 1, m:m + 1]).then_inc(dt_set.sem, 1)

            def take_back(n, m):
                o = filled_by(n, f"back{m}")
                if m == 0 and more(n, 1):
                    act.wait_ge(filled.sem, filled.after(n.shift(-1), "out1"))
                nc.scalar.activation(og[:, m, :], o[:, 0:TC], ACT.Identity, bias=vecs[:, 4, m:m + 1],
                                     scale=vecs[:, 3, m:m + 1]).then_inc(affined.sem, 1)

            def take_out(n, h):
                rows = P if h == 0 else HALF
                o = filled_by(n, f"out{h}")
                if h == 0 and more(n, 1):
                    act.wait_ge(stored.sem, stored.after(n.shift(-1), "x"))
                nc.scalar.activation(fz[0:rows, h, :], o[0:rows, 0:TC], ACT.Identity, bias=fub[0:rows, h:h + 1]).then_inc(fz_set.sem, 1)

            def silus(n):
                if on("A", n):
                    act.wait_ge(pre_set.sem, pre_set.after(n, f"{ND - 1}"))
                    if more(n, -1):
                        act.wait_ge(ud_set.sem, ud_set.after(n.shift(-1), "x"))
                    nc.scalar.activation(u[:], pre[:], ACT.Silu).then_inc(u_set.sem, 1)
                if on("O", n):
                    act.wait_ge(zpre_set.sem, zpre_set.after(n.shift(-1), f"{ND - 1}"))
                    if more(n, 1):
                        act.wait_ge(gated.sem, gated.after(n.shift(-1), "x"))
                    nc.scalar.activation(sz[:], zpre[:], ACT.Silu).then_inc(sz_set.sem, 1)

            def softplus(n):
                act.wait_ge(dt_set.sem, dt_set.after(n, f"{ND - 1}"))
                if more(n, -1):
                    act.wait_ge(delta_set.sem, delta_set.after(n.shift(-1), "x"))
                nc.scalar.activation(soft2[:], soft[:], ACT.Abs).then_inc(abs_set.sem, 1)
                act.wait_ge(abs_set.sem, abs_set.after(n, "x"))
                nc.scalar.activation(soft2[:], soft2[:], ACT.Exp, scale=-1.0).then_inc(exp_set.sem, 1)
                act.wait_ge(exp_set.sem, exp_set.after(n, "x"))
                nc.scalar.activation(soft2[:], soft2[:], ACT.Ln, bias=1.0).then_inc(ln_set.sem, 1)

            def decays(n, s, par):
                for m in range(ND):
                    if s == 0 and m == 0:
                        act.wait_ge(delta_set.sem, delta_set.after(n.shift(-1), "x"))
                    if s > 0:
                        act.wait_ge(scanned.sem, scanned.after(n, f"{s - 1}.{m}"))
                    elif more(n, 0):
                        act.wait_ge(scanned.sem, scanned.after(n.shift(-1), f"{ST - 1}.{m}"))
                    nc.scalar.activation(decay[:, m, 0:TC], delta[:, par, m, :], ACT.Exp,
                                         scale=aneg[:, m, s:s + 1]).then_inc(decayed.sem, 1)

            def copy_b(n, t, early):
                spread = b_spread.after(n, f"{t}") if early or t > 4 else b_spread.after(n.shift(-1), f"{t}")
                act.wait_ge(b_spread.sem, spread)
                if t >= 4:
                    act.wait_ge(driven.sem, driven.after(n, f"{t - 4}") if t - 4 >= 3 else driven.after(n.shift(-1), f"{t - 4}"))
                elif on("S", n):
                    act.wait_ge(driven.sem, driven.after(n, f"{t + ST - 4}"))
                nc.scalar.activation(brow[:, t % RING, :], bps[:, 0:TC], ACT.Copy).then_inc(b_copied.sem, 1)

            def emit(n, par):
                X, A, S, O = on("X", n), on("A", n), on("S", n), on("O", n)
                for s in range(ST):
                    if S:
                        decays(n, s, par)
                    if S and s + 4 < ST:
                        copy_b(n, s + 4, False)
                    if A and s + 4 >= ST:
                        copy_b(n, s + 4 - ST, True)
                    if A and s in (2, 4, 6):
                        take_conv(n, s // 2 - 1)
                    if O and 2 <= s <= 4:
                        take_y(n, s - 2)
                    if s == 6:
                        silus(n)
                    if A and s == 8:
                        x_low(n, 1 - par)
                    if S and s == 9:
                        take_z(n, 0)
                    if A and s == 10:
                        take_dt(n, 0), take_dt(n, 1)
                    if A and s == 11:
                        take_dt(n, 2), softplus(n)
                    if O and s == 11:
                        take_back(n, 0)
                    if O and s == 12:
                        take_back(n, 1), take_back(n, 2)
                    if S and s == 13:
                        take_z(n, 1)
                    if X and s == 14:
                        take_xin(n, 0)
                    if S and s == 14:
                        take_z(n, 2)
                    if O and s == 15:
                        take_out(n, 0)
                    if X and s == 15:
                        take_xin(n, 1)
                if O:
                    take_out(n, 1)
                if X:
                    take_xin(n, 2)

            def x_low(n, nxt):
                o = filled_by(n, "xp")
                if n.reg is not None or n.off > 0:
                    act.wait_ge(c_spread.sem, c_spread.after(n.shift(-1), f"{ST - 1}"))
                nc.scalar.activation(bc[0:2 * ST, nxt, :], o[0:2 * ST, 0:TC], ACT.Copy).then_inc(bchi.sem, 1)
                nc.scalar.activation(dtl[:], o[2 * ST:2 * ST + RANK, 0:TC], ACT.Copy).then_inc(dtl_set.sem, 1)

            steps(act, emit)

        @block.gpsimd
        def _(pool):
            nc.gpsimd.memset(mhalf[:], -0.5).then_inc(prepared, 1)
            pool.wait_ge(loaded, 16 * NLOADS)

            def emit(n, par):
                A, S, O = on("A", n), on("S", n), on("O", n)
                nxt = 1 - par
                for s in range(ST):
                    sB = s + 3
                    if (S and sB < ST) or (A and sB >= ST):
                        t = sB % ST
                        mine = nxt if sB >= ST else par
                        pool.wait_ge(b_copied.sem, b_copied.after(n.shift(-1), "3") if t == 3 else b_copied.after(n, f"{t}"))
                        if sB >= ST:
                            pool.wait_ge(du_set.sem, du_set.after(n, "x"))
                        if t >= 4:
                            pool.wait_ge(scanned.sem, scanned.after(n, f"{t - 4}.{ND - 1}"))
                        elif sB >= ST and S:
                            pool.wait_ge(scanned.sem, scanned.after(n, f"{t + ST - 4}.{ND - 1}"))
                        elif t == 3 and (n.reg is not None or n.off > 0):
                            pool.wait_ge(scanned.sem, scanned.after(n.shift(-1), f"{ST - 1}.{ND - 1}"))
                        nc.gpsimd.tensor_tensor(drive[:, t % RING], du[:, mine], brow[:, t % RING, :].unsqueeze(1).broadcast_to([P, ND, TC]),
                                                ALU.mult).then_inc(driven.sem, 1)
                    if S and s:
                        take_carry(n, n, s - 1)
                    elif O and s == 0:
                        take_carry(n, n.shift(-1), ST - 1)
                    if O and s == 6:
                        mv_set_value = held(pool, mv_set.after(n, "x"))
                        pool.wait_ge(loaded, 16 * NLOADS)
                        pool.wait_ge(mv_set.sem, mv_set_value)
                        nc.gpsimd.tensor_scalar(rstd[:, 0, :], mv[:, :, 1], EPS, 1.0, ALU.add, ALU.mult).then_inc(veps_set.sem, 1)
                        pool.wait_ge(veps_set.sem, veps_set.after(n, "x"))
                        nc.gpsimd.tensor_tensor(rstd[:, 1, :], rstd[:, 0, :], mhalf[:], ALU.pow).then_inc(rstd_set.sem, 1)
                    if A and s == 12:
                        pool.wait_ge(ln_set.sem, ln_set.after(n, "x"))
                        pool.wait_ge(relu_set.sem, relu_set.after(n, "x"))
                        nc.gpsimd.tensor_tensor(delta[:, nxt], delta[:, nxt], soft2[:], ALU.add).then_inc(delta_set.sem, 1)
                        pool.wait_ge(delta_set.sem, delta_set.after(n, "x"))
                        nc.gpsimd.tensor_tensor(du[:, nxt], delta[:, nxt], u[:], ALU.mult).then_inc(du_set.sem, 1)
                    if O and s == 13:
                        pool.wait_ge(affined.sem, affined.after(n, f"{ND - 1}"))
                        pool.wait_ge(sz_set.sem, sz_set.after(n, "sz"))
                        nc.gpsimd.tensor_tensor(og[:], og[:], sz[:], ALU.mult).then_inc(gated.sem, 1)
                    if A and s == 15:
                        if S:
                            summed_value = held(pool, summed.after(n, "2"))
                            pool.wait_ge(loaded, 16 * NLOADS)
                            pool.wait_ge(summed.sem, summed_value)
                        for m in range(ND):
                            last = nc.gpsimd.tensor_scalar(part[:, 0, m, :], u[:, m, :], vecs[:, 2, m:m + 1], 1.0, ALU.mult, ALU.mult)
                        last.then_inc(ud_set.sem, 1)

            def take_carry(n, chunk, s):
                scanned_value = held(pool, scanned.after(chunk, f"{s}.{ND - 1}"))
                pool.wait_ge(loaded, 16 * NLOADS)
                pool.wait_ge(scanned.sem, scanned_value)
                nc.gpsimd.tensor_tensor(carry[:, s, :], hst[:, s % RING, :, TC - 1], keep[:, bass.ds(chunk.linear(ND, 0), ND)],
                                        ALU.mult).then_inc(carried.sem, 1)

            steps(pool, emit)

        @block.vector
        def _(dve):
            dve.wait_ge(loaded, 16 * NLOADS)
            nc.vector.tensor_copy(pick_r[:], pick[:])
            for m in range(ND):
                for tap in range(9):
                    last = nc.vector.tensor_scalar(diag[:, m, tap, :], ident[:], cw[:, m, tap:tap + 1], None, ALU.mult)
            nc.vector.memset(xin[:, :, :, 0:1], 0.0)
            last = nc.vector.memset(xin[:, :, :, SIDE + 1:SIDE + 2], 0.0).then_inc(prepared, 1)
            for m in range(ND):
                dve.wait_ge(merged, m + 1)
                nc.vector.tensor_copy(wout[:, m, :], fill[:, m % 2, 0:CH]).then_inc(mergedone, 1)
            dve.wait_ge(alogged, 1)
            nc.vector.tensor_scalar(aneg[:], aneg[:], -1.0, None, ALU.mult).then_inc(prepared, 1)

            def scale(n, s):
                g = s // 4
                dve.wait_ge(scanned.sem, scanned.after(n, f"{s}.{ND - 1}"))
                dve.wait_ge(c_spread.sem, c_spread.after(n, f"{s}"))
                if s % 4 == 0:
                    if g:
                        dve.wait_ge(summed.sem, summed.after(n, f"{g - 1}"))
                    elif n.reg is not None or n.off > 0:
                        dve.wait_ge(summed.sem, summed.after(n.shift(-1), "3"))
                nc.vector.tensor_tensor(part[:, 1 + s % 4], hst[:, s % RING], cps[:, s % 2, 0:TC].unsqueeze(1).broadcast_to([P, ND, TC]),
                                        ALU.mult).then_inc(scaled.sem, 1)

            def add_up(n, g):
                dve.wait_ge(scaled.sem, scaled.after(n, f"{4 * g + 3}"))
                if g == 0:
                    dve.wait_ge(ud_set.sem, ud_set.after(n.shift(-1), "x"))
                if g:
                    dve.wait_ge(summed.sem, summed.after(n, f"{g - 1}"))
                lo = g % 2
                dst = ysum[:] if g == 3 else part[:, 5 if g % 2 == 0 else 0]
                if g == 3 and (n.reg is not None or n.off > 0):
                    dve.wait_ge(filled.sem, filled.after(n, "yT2"))
                nc.vector.tensor_reduce(dst.rearrange("p m t -> p (m t)"),
                                        part[:, lo:lo + 5].rearrange("p k m t -> p (m t) k"), AX.X, ALU.add).then_inc(summed.sem, 1)

            def emit(n, par):
                A, S, O = on("A", n), on("S", n), on("O", n)
                nxt = 1 - par
                later = n.reg is not None or n.off > 0
                for s in range(ST):
                    if S:
                        for m in range(ND):
                            if m == 0:
                                dve.wait_ge(driven.sem, driven.after(n, f"{s}") if s >= 3 else driven.after(n.shift(-1), f"{s}"))
                                if s >= RING:
                                    dve.wait_ge(scaled.sem, scaled.after(n, f"{s - RING}"))
                                    dve.wait_ge(carried.sem, carried.after(n, f"{s - RING}"))
                                elif later:
                                    dve.wait_ge(scaled.sem, scaled.after(n.shift(-1), f"{s + ST - RING}"))
                                    if s < RING - 1:
                                        dve.wait_ge(carried.sem, carried.after(n.shift(-1), f"{s + ST - RING}"))
                                    else:
                                        dve.wait_ge(carried.sem, carried.after(n, f"{ST - 1}"))
                            dve.wait_ge(decayed.sem, decayed.after(n, f"{s}.{m}"))
                            nc.vector.tensor_tensor_scan(hst[:, s % RING, m, :], decay[:, m, 0:TC], drive[:, s % RING, m, :],
                                                         carry[:, s, m:m + 1] if later else 0.0, ALU.mult, ALU.add).then_inc(scanned.sem, 1)
                        if s >= 5 and s % 4 == 1:
                            add_up(n, (s - 5) // 4)
                        if s >= 1:
                            scale(n, s - 1)
                    if O and s == 5:
                        for j in range(ND):
                            dve.wait_ge(yt_set.sem, yt_set.after(n, f"{j}"))
                            nc.vector.bn_stats(st6[:, j, :], yt[:, j, :]).then_inc(stat_set.sem, 1)
                        stat_set_value = held(dve, stat_set.after(n, f"{ND - 1}"))
                        dve.wait_ge(loaded, 16 * NLOADS)
                        dve.wait_ge(stat_set.sem, stat_set_value)
                        for j in range(ND):
                            last = nc.vector.bn_aggr(mv[:, j, :], st6[:, j, :])
                        last.then_inc(mv_set.sem, 1)
                    if O and s == 8:
                        dve.wait_ge(rstd_set.sem, rstd_set.after(n, "x"))
                        for j in range(ND):
                            nc.vector.tensor_scalar(yt[:, j, :], yt[:, j, :], mv[:, j, 0:1], rstd[:, 1, j:j + 1],
                                                    ALU.subtract, ALU.mult).then_inc(normed.sem, 1)
                    if A and s == 9:
                        dve.wait_ge(bchi.sem, bchi.after(n, "x"))
                        dve.wait_ge(dtl_set.sem, dtl_set.after(n, "x"))
                        if n.reg is not None or n.off > 0:
                            dve.wait_ge(c_spread.sem, c_spread.after(n.shift(-1), f"{ST - 1}"))
                        nc.vector.tensor_tensor(bc[2 * ST:4 * ST, nxt, :], fill[0:2 * ST, bank_of["xp"], 0:TC], bc[0:2 * ST, nxt, :],
                                                ALU.subtract).then_inc(bclo.sem, 1)
                    if A and s == 12:
                        dve.wait_ge(dt_set.sem, dt_set.after(n, f"{ND - 1}"))
                        if later:
                            dve.wait_ge(decayed.sem, decayed.after(n.shift(-1), f"{ST - 1}.{ND - 1}"))
                        nc.vector.tensor_scalar(delta[:, nxt], soft[:], 0.0, None, ALU.max).then_inc(relu_set.sem, 1)
                if S:
                    scale(n, ST - 1)
                    add_up(n, 3)

            steps(dve, emit)


def sedenion_signs():
    def conj(x):
        return x if len(x) == 1 else np.concatenate([conj(x[:len(x) // 2]), -x[len(x) // 2:]])

    def mult(a, b):
        if len(a) == 1:
            return a * b
        h = len(a) // 2
        a1, a2, b1, b2 = a[:h], a[h:], b[:h], b[h:]
        return np.concatenate([mult(a1, b1) - mult(conj(b2), a2), mult(b2, a1) + mult(a2, conj(b1))])

    eye = np.eye(NK, dtype=np.int64)
    return [[int(mult(eye[i], eye[i ^ k])[k]) for k in range(NK)] for i in range(NK)]


def layer1(nc, d, nimg):
    when = {"E": (0, nimg - 1)}
    sign = sedenion_signs()
    pairs = range(NK // 2)
    tails = sorted({(sign[2 * p][2 * q] * sign[2 * p][2 * q + 1], sign[2 * p + 1][2 * q] * sign[2 * p + 1][2 * q + 1])
                    for p in pairs for q in pairs})
    ctx = ExitStack()
    with ctx:
        def sb(name, shape, dt=F32):
            return ctx.enter_context(nc.sbuf_tensor(name, shape, dt))

        def ps(name, shape):
            return ctx.enter_context(nc.psum_tensor(name, shape, F32))

        def sem(name):
            return ctx.enter_context(nc.semaphore(name))

        def count(name, events, w=1):
            return Count(sem(name), when, [(e, "E", w) for e in events])

        wmm, wkt = sb("wmm", [P, NK, P]), sb("wkt", [P, NK, P])
        wmt, wtt = sb("wmt", [P, 2, NK, P]), sb("wtt", [P, len(tails), NK // 2, P])
        pw_a, pw_b = sb("pw_a", [P, CH]), sb("pw_b", [P, 2, CH])
        f1_a, f1_b, f2 = sb("f1_a", [P, HID]), sb("f1_b", [HALF, HID]), sb("f2", [P, NM, CH])
        vec = sb("vec", [P, 6, 2])
        b1 = sb("b1", [P, NM])
        sgn = sb("sgn", [P, 4])
        idn = sb("idn", [P, P])
        half = sb("half", [P, NB])
        fn_a, fn_b = sb("fn_a", [P, TOK]), sb("fn_b", [HALF, TOK])
        fst, fmv, frs = sb("fst", [P, 2, NCH, 6]), sb("fmv", [P, 2, 2]), sb("frs", [P, 4, 2])
        xp_a, xp_b = sb("xp_a", [P, TOK]), sb("xp_b", [HALF, TOK])
        x1_a, x1_b = sb("x1_a", [P, TOK]), sb("x1_b", [HALF, TOK])
        xt = sb("xt", [BL, TURN, NB, CH])
        tst, tmv, trs = sb("tst", [BL, NB, 6]), sb("tmv", [BL, 2, NB, 2]), sb("trs", [BL, 2, 2, NB])
        xm = sb("xm", [P, NK, WT])
        tpp, tpm = sb("tpp", [P, NK // 2, WT]), sb("tpm", [P, NK // 2, WT])
        neg, ypre, ym = sb("neg", [P, 3, WT]), sb("ypre", [P, 3, WT]), sb("ym", [P, 3, WT])
        x2_a, x2_b = sb("x2_a", [P, 2, GT]), sb("x2_b", [HALF, 2, GT])
        r_a, r_b = sb("r_a", [P, 2, GT]), sb("r_b", [HALF, 2, GT])
        xa_a, xa_b = sb("xa_a", [P, GT]), sb("xa_b", [HALF, GT])
        h1 = sb("h1", [P, NM, GT])
        o_a, o_b = sb("o_a", [P, 2, GT]), sb("o_b", [HALF, 2, GT])
        wps = ps("wps", [P, 3, BANK])
        fill = ps("fill5", [P, 5, BANK])

        uses = []
        for q in range(NG + 2):
            if q < NG:
                uses += [f"turnH{q}a", f"turnH{q}b"]
            if q >= 2:
                uses += [f"backH{q - 2}a", f"backH{q - 2}b"]
        for g in range(NG):
            uses += [f"projM{g}a", f"projM{g}b", f"turnM{g}a", f"turnM{g}b", f"backM{g}a", f"backM{g}b"]
            uses += [f"fcoM{g}{m}" for m in range(NM)] + [f"fctM{g}a", f"fctM{g}b"]
        NBANK = 5
        bank_of = {u: i % NBANK for i, u in enumerate(uses)}
        groups = [f"H{g}" for g in range(NG)] + [f"M{g}" for g in range(NG)]
        order = {u: i for i, u in enumerate(groups)}
        ab = lambda names: [f"{n}{h}" for n in names for h in "ab"]
        gs = [f"{g}" for g in range(NG)]

        wloaded, wset, wready = sem("wloaded"), sem("wset"), sem("wready")
        filled = count("filled1", uses)
        fn_in, xp_in = count("fn_in", ["x"], 32), count("xp_in", ["x"], 32)
        fst_set = count("fst_set", [f"{h}{c}" for h in "ab" for c in range(NCH)])
        fmv_set, fve, frs_set = count("fmv_set", "ab"), count("fve", ["x"]), count("frs_set", ["x"])
        fnm, fnb = count("fnm", ["x"]), count("fnb", ["x"])
        spread = count("spread1", [f"{h}{r}" for r in range(WIN) for h in "ab"])
        x1_set = count("x1_set", ab(gs))
        turned = count("turned", ab(groups))
        tst_set = count("tst_set", [f"{q}.{j}" for q in groups for j in range(NB)])
        tmv_set, tve, trs_set = count("tmv_set", groups), count("tve", groups), count("trs_set", groups)
        normed = count("normed1", [f"{q}.{j}" for q in groups for j in range(NB)])
        xm_set, tpp_set, tpm_set = count("xm_set", gs), count("tpp_set", [f"{g}{h}" for g in gs for h in "01"]), count("tpm_set", ["x"])
        wtile = [f"{g}.{t}" for g in range(NG) for t in range(3)]
        wdone, neg_set, ypre_set = count("wdone", wtile), count("neg_set", wtile), count("ypre_set", wtile)
        ym_set = count("ym_set", gs)
        x2_set, r_set, xa_set = count("x2_set", ab(gs)), count("r_set", ab(gs)), count("xa_set", ab(gs))
        h1_set = count("h1_set", [f"{g}{m}" for g in gs for m in range(NM)])
        o_set = count("o_set", ab(gs))
        o_out = [count(f"o_out{par}", [g for g in gs if int(g) % 2 == par], 32) for par in range(2)]

        def reader(use):
            what, rest = use[:4], use[4:]
            g = rest[1:-1]
            if what == "turn":
                return turned, rest
            if what == "back":
                if rest[0] == "M":
                    return xa_set, rest[1:]
                return (xm_set, g) if rest[-1] == "a" else (tpp_set, g + "1")
            return {"proj": (x2_set, rest[1:]), "fcoM": (h1_set, use[4:]), "fctM": (o_set, use[4:])}[what if what == "proj" else use[:4]]

        def before_it(n, use):
            i = uses.index(use)
            if i >= NBANK:
                return n, uses[i - NBANK]
            return n.shift(-1), [u for u in uses if bank_of[u] == bank_of[use]][-1]

        def prior(c, n):
            return c.after(n.shift(-1), c.events[-1][0])

        block = ctx.enter_context(nc.Block())

        def images(eng, emit):
            emit(At(0))
            with eng.Fori(0, nimg - 1) as b:
                emit(At(1, b, 1))

        loads = [(wmm, d["wmm"]), (wkt, d["wkt"]), (wmt[:, 0], d["wmt"]), (wtt[:, 0], d["wtt"]),
                 (pw_a, d["pw"][0:P]), (pw_b[0:HALF, 0], d["pw"][P:CH]), (pw_b[HALF:P, 1], d["pw"][P:CH]),
                 (f1_a, d["f1"][0:P]), (f1_b, d["f1"][P:CH]), (f2, d["f2"]), (vec[:, :, 0:1], d["vec"][:, 0:P].rearrange("v (p o) -> p v o", o=1)),
                 (vec[0:HALF, :, 1:2], d["vec"][:, P:CH].rearrange("v (p o) -> p v o", o=1)), (b1, d["b1"]),
                 (sgn, d["sgn"]), (idn, d["ident"])]

        @block.sync
        def _(sp):
            for dst, src in loads:
                with nc.allow_non_contiguous_dma(reason="a few hundred numbers, once"):
                    sp.dma_start(dst if isinstance(dst, bass.AP) else dst[:], src).then_inc(wloaded, 16)

            def emit(n):
                if n.later():
                    fn_in_value = held(sp, prior(fn_in, n))
                    spread_value = held(sp, prior(spread, n))
                    sp.wait_ge(wloaded, 16 * len(loads))
                    sp.wait_ge(fn_in.sem, fn_in_value)
                    sp.wait_ge(spread.sem, spread_value)
                src = d["fz"][bass.ds(n.linear(NCH, 0), NCH)]
                sp.dma_start(fn_a[:].rearrange("p (c t) -> p c t", c=NCH), src[:, 0:P, :].rearrange("c p t -> p c t")).then_inc(fn_in.sem, 16)
                sp.dma_start(fn_b[:].rearrange("p (c t) -> p c t", c=NCH), src[:, P:CH, :].rearrange("c p t -> p c t")).then_inc(fn_in.sem, 16)
                if n.later():
                    xp_in_value = held(sp, prior(xp_in, n))
                    x1_set_value = held(sp, prior(x1_set, n))
                    sp.wait_ge(wloaded, 16 * len(loads))
                    sp.wait_ge(xp_in.sem, xp_in_value)
                    sp.wait_ge(x1_set.sem, x1_set_value)
                sp.dma_start(xp_a[:], d["xperm"][n.linear(1, 0), 0:P, :]).then_inc(xp_in.sem, 16)
                sp.dma_start(xp_b[:], d["xperm"][n.linear(1, 0), P:CH, :]).then_inc(xp_in.sem, 16)

            images(sp, emit)

        @block.gpsimd
        def _(pool):
            for i, (dst, value) in enumerate([(half[:], -0.5), (fmv[:], 1.0), (pw_b[HALF:P, 0], 0.0), (pw_b[0:HALF, 1], 0.0)]):
                nc.gpsimd.memset(dst, value).then_inc(wset, 1)
                pool.wait_ge(wset, i + 1)

            def rstd(n, q):
                r = order[q] % 2
                tmv_set_value = held(pool, tmv_set.after(n, q))
                pool.wait_ge(wloaded, 16 * len(loads))
                pool.wait_ge(tmv_set.sem, tmv_set_value)
                nc.gpsimd.tensor_scalar(trs[:, r, 0], tmv[:, r, :, 1], EPS, 1.0, ALU.add, ALU.mult).then_inc(tve.sem, 1)
                pool.wait_ge(tve.sem, tve.after(n, q))
                nc.gpsimd.tensor_tensor(trs[:, r, 1], trs[:, r, 0], half[0:BL], ALU.pow).then_inc(trs_set.sem, 1)

            def store(n, g):
                pool.wait_ge(o_set.sem, o_set.after(n, f"{g}b"))
                c = o_out[g % 2]
                for dst, lo, hi in ((o_a, 0, P), (o_b, P, CH)):
                    pool.dma_start(d["out"][n.linear(1, 0), lo:hi, bass.ts(g, GT)], dst[:, g % 2, :]).then_inc(c.sem, 16)

            def emit(n):
                if n.later():
                    pool.wait_ge(spread.sem, prior(spread, n))
                fmv_value = held(pool, fmv_set.after(n, "b"))
                pool.wait_ge(wloaded, 16 * len(loads))
                pool.wait_ge(fmv_set.sem, fmv_value)
                nc.gpsimd.tensor_scalar(frs[:, 0], fmv[:, :, 1], EPS, 1.0, ALU.add, ALU.mult).then_inc(fve.sem, 1)
                pool.wait_ge(fve.sem, fve.after(n, "x"))
                nc.gpsimd.tensor_tensor(frs[:, 1], frs[:, 0], half[:, 0:2], ALU.pow).then_inc(frs_set.sem, 1)
                pool.wait_ge(frs_set.sem, frs_set.after(n, "x"))
                nc.gpsimd.tensor_tensor(frs[:, 2], frs[:, 1], fmv[:, :, 0], ALU.mult).then_inc(fnm.sem, 1)
                fnm_value = held(pool, fnm.after(n, "x"))
                pool.wait_ge(wloaded, 16 * len(loads))
                pool.wait_ge(fnm.sem, fnm_value)
                nc.gpsimd.tensor_scalar(frs[:, 3], frs[:, 2], -1.0, 1.0, ALU.mult, ALU.mult).then_inc(fnb.sem, 1)
                for q in groups[:NG]:
                    rstd(n, q)
                for g in range(NG + 1):
                    if g < NG:
                        rstd(n, f"M{g}")
                    if g:
                        store(n, g - 1)

            images(pool, emit)
            for c in o_out:
                pool.wait_ge(c.sem, 32 * NG // 2 * nimg)

        @block.tensor
        def _(pe):
            pe.wait_ge(wloaded, 16 * len(loads))
            pe.wait_ge(wset, 4)
            pe.wait_ge(wready, 3)

            def use(n, name):
                step, user = before_it(n, name)
                c, event = reader(user)
                if step is not n and not n.later():
                    return fill[:, bank_of[name], :]
                value = c.after(step, event) if step is n else prior(c, n)
                if name[:4] in ("turn", "back") and name[-1] == "b":
                    value = held(pe, value)
                    pe.wait_ge(wloaded, 16 * len(loads))
                pe.wait_ge(c.sem, value)
                return fill[:, bank_of[name], :]

            def turn(n, q, src_a, src_b):
                o = use(n, f"turn{q}a")
                for j in range(NB):
                    last = nc.tensor.transpose(o[0:BL, bass.ts(j, P)], src_a[:, bass.ts(j, BL)], idn[:])
                last.then_inc(filled.sem, 1)
                o = use(n, f"turn{q}b")
                for j in range(NB):
                    last = nc.tensor.transpose(o[0:BL, bass.ts(j, HALF)], src_b[:, bass.ts(j, BL)], idn[0:HALF, 0:HALF])
                last.then_inc(filled.sem, 1)

            def back(n, q):
                pe.wait_ge(normed.sem, normed.after(n, f"{q}.{NB - 1}"))
                r = order[q] % TURN
                o = use(n, f"back{q}a")
                for j in range(NB):
                    last = nc.tensor.transpose(o[:, bass.ts(j, BL)], xt[:, r, j, 0:P], idn[0:BL, 0:BL])
                last.then_inc(filled.sem, 1)
                o = use(n, f"back{q}b")
                for j in range(NB):
                    last = nc.tensor.transpose(o[0:HALF, bass.ts(j, BL)], xt[:, r, j, P:CH], idn[0:BL, 0:BL])
                last.then_inc(filled.sem, 1)

            def window(n, g, t):
                if g:
                    pe.wait_ge(ypre_set.sem, ypre_set.after(n, f"{g - 1}.{t}"))
                elif n.later():
                    pe.wait_ge(ypre_set.sem, prior(ypre_set, n))
                plus, minus = [], []
                k0, k1 = 2 * g, 2 * g + 1
                for i in range(NK):
                    k = k1 if t == 1 else k0
                    w = wmm[:, i ^ k, :] if t < 2 else wmt[:, (1 - sign[i][k0] * sign[i][k1]) // 2, i ^ k0, :]
                    (plus if sign[i][k] > 0 else minus).append((w, xm[:, i, :]))
                for p in pairs:
                    k = k1 if t == 1 else k0
                    a, b = sign[2 * p][k], sign[2 * p + 1][k]
                    if t < 2:
                        w = wkt[:, (2 * p) ^ k, :]
                    else:
                        w = wtt[:, tails.index((a * sign[2 * p][k1], b * sign[2 * p + 1][k1])), ((2 * p) ^ k0) // 2, :]
                    (plus if a > 0 else minus).append((w, (tpp if a * b > 0 else tpm)[:, p, :]))
                for part, terms in enumerate([plus, minus]):
                    for e, (w, x) in enumerate(terms):
                        last = nc.tensor.matmul(wps[:, t, part * WT:(part + 1) * WT], w, x, start=(e == 0), stop=(e == len(terms) - 1))
                last.then_inc(wdone.sem, 1)

            def proj(n, g):
                pe.wait_ge(ym_set.sem, ym_set.after(n, f"{g}"))
                for h, lo, m in (("a", 0, P), ("b", P, HALF)):
                    o = use(n, f"projM{g}{h}")
                    nc.tensor.matmul(o[0:m, 0:GT], pw_a[:, lo:lo + m], ym[:, 0:2, :].rearrange("p a w -> p (a w)"), start=True, stop=False)
                    nc.tensor.matmul(o[0:m, 0:WT], pw_b[:, 0, lo:lo + m], ym[:, 2, :], start=False, stop=False)
                    nc.tensor.matmul(o[0:m, WT:GT], pw_b[:, 1, lo:lo + m], ym[:, 2, :], start=False, stop=True).then_inc(filled.sem, 1)

            def emit(n):
                for q in range(NG + 2):
                    if q < NG:
                        pe.wait_ge(x1_set.sem, x1_set.after(n, f"{q}b"))
                        turn(n, f"H{q}", x1_a[:, bass.ts(q, GT)], x1_b[:, bass.ts(q, GT)])
                    if q >= 2:
                        back(n, f"H{q - 2}")
                pe.wait_ge(xm_set.sem, xm_set.after(n, "7"))
                pe.wait_ge(tpp_set.sem, tpp_set.after(n, "71"))
                pe.wait_ge(tpm_set.sem, tpm_set.after(n, "x"))
                for g in range(NG + 1):
                    m = g - 1
                    if m >= 0:
                        proj(n, m)
                    if g < NG:
                        window(n, g, 0)
                    if m >= 0:
                        pe.wait_ge(x2_set.sem, x2_set.after(n, f"{m}b"))
                        turn(n, f"M{m}", x2_a[:, m % 2, :], x2_b[:, m % 2, :])
                    if g < NG:
                        window(n, g, 1)
                    if m >= 0:
                        back(n, f"M{m}")
                    if g < NG:
                        window(n, g, 2)
                    if m >= 0:
                        pe.wait_ge(xa_set.sem, xa_set.after(n, f"{m}b"))
                        for j in range(NM):
                            o = use(n, f"fcoM{m}{j}")[:, 0:GT]
                            nc.tensor.matmul(o, f1_a[:, bass.ts(j, P)], xa_a[:], start=True, stop=False)
                            nc.tensor.matmul(o, f1_b[:, bass.ts(j, P)], xa_b[:], start=False, stop=True).then_inc(filled.sem, 1)
                        for h, lo, w in (("a", 0, P), ("b", P, HALF)):
                            o = use(n, f"fctM{m}{h}")
                            for j in range(NM):
                                pe.wait_ge(h1_set.sem, h1_set.after(n, f"{m}{j}"))
                                last = nc.tensor.matmul(o[0:w, 0:GT], f2[:, j, lo:lo + w], h1[:, j, :], start=(j == 0), stop=(j == NM - 1))
                            last.then_inc(filled.sem, 1)

            images(pe, emit)

        @block.scalar
        def _(act):
            act.wait_ge(wloaded, 16 * len(loads))

            def filled_by(n, name):
                act.wait_ge(filled.sem, filled.after(n, name))
                return fill[:, bank_of[name], :]

            def take_turn(n, q):
                r = order[q] % TURN
                o = filled_by(n, f"turn{q}a")
                if order[q] >= TURN:
                    act.wait_ge(filled.sem, filled.after(n, f"back{groups[order[q] - TURN]}b"))
                elif n.later():
                    act.wait_ge(filled.sem, prior(filled, n))
                nc.scalar.activation(xt[:, r, :, 0:P], o[0:BL, 0:NB * P].rearrange("p (j c) -> p j c", j=NB), ACT.Copy).then_inc(turned.sem, 1)
                o = filled_by(n, f"turn{q}b")
                nc.scalar.activation(xt[:, r, :, P:CH], o[0:BL, 0:NB * HALF].rearrange("p (j c) -> p j c", j=NB), ACT.Copy).then_inc(turned.sem, 1)

            def negative(n, g, t):
                act.wait_ge(wdone.sem, wdone.after(n, f"{g}.{t}"))
                if t == 0:
                    if g:
                        act.wait_ge(ypre_set.sem, ypre_set.after(n, f"{g - 1}.2"))
                    elif n.later():
                        act.wait_ge(ypre_set.sem, prior(ypre_set, n))
                nc.scalar.activation(neg[:, t, :], wps[:, t, WT:2 * WT], ACT.Copy).then_inc(neg_set.sem, 1)

            def emit(n):
                act.wait_ge(frs_set.sem, frs_set.after(n, "x"))
                act.wait_ge(fnb.sem, fnb.after(n, "x"))
                if n.later():
                    act.wait_ge(x2_set.sem, prior(x2_set, n))
                for r in range(WIN):
                    for h, (src, dst, rows) in enumerate([(fn_a, x1_a, P), (fn_b, x1_b, HALF)]):
                        i = src[:].rearrange("p (wh r ww c) -> p r wh ww c", r=WIN, ww=NW, c=WIN)[:, r]
                        o = dst[:].rearrange("p (r c wh ww) -> p r wh ww c", r=WIN, c=WIN, ww=NW)[:, r]
                        nc.scalar.activation(o, i, ACT.Identity, bias=frs[0:rows, 3, h:h + 1], scale=frs[0:rows, 1, h:h + 1]).then_inc(spread.sem, 1)
                for q in range(NG + 2):
                    if q < NG:
                        take_turn(n, f"H{q}")
                    if q >= 2:
                        g = q - 2
                        o = filled_by(n, f"backH{g}a")
                        if g == 0:
                            if n.later():
                                act.wait_ge(wdone.sem, prior(wdone, n))
                        nc.scalar.activation(xm[:, 2 * g:2 * g + 2, :].rearrange("p a w -> p (a w)"), o[:, 0:GT], ACT.Identity,
                                             bias=vec[:, 1, 0:1], scale=vec[:, 0, 0:1]).then_inc(xm_set.sem, 1)
                        o = filled_by(n, f"backH{g}b")
                        for h in range(2):
                            nc.scalar.activation(tpp[h * HALF:(h + 1) * HALF, g, :], o[0:HALF, h * WT:(h + 1) * WT], ACT.Identity,
                                                 bias=vec[0:HALF, 1, 1:2], scale=vec[0:HALF, 0, 1:2]).then_inc(tpp_set.sem, 1)
                for g in range(NG + 1):
                    m = g - 1
                    if m >= 0:
                        act.wait_ge(x2_set.sem, x2_set.after(n, f"{m}b"))
                        if m >= 2:
                            act.wait_ge(o_set.sem, o_set.after(n, f"{m - 2}b"))
                        elif n.later():
                            act.wait_ge(o_set.sem, prior(o_set, n))
                        nc.scalar.activation(r_a[:, m % 2, :], x2_a[:, m % 2, :], ACT.Identity, bias=vec[:, 5, 0:1]).then_inc(r_set.sem, 1)
                        nc.scalar.activation(r_b[:, m % 2, :], x2_b[:, m % 2, :], ACT.Identity, bias=vec[0:HALF, 5, 1:2]).then_inc(r_set.sem, 1)
                    if g < NG:
                        negative(n, g, 0)
                    if m >= 0:
                        take_turn(n, f"M{m}")
                    if g < NG:
                        negative(n, g, 1)
                    if m >= 0:
                        for h, dst, rows in (("a", xa_a, P), ("b", xa_b, HALF)):
                            o = filled_by(n, f"backM{m}{h}")
                            c = "ab".index(h)
                            nc.scalar.activation(dst[:], o[0:rows, 0:GT], ACT.Identity, bias=vec[0:rows, 4, c:c + 1],
                                                 scale=vec[0:rows, 3, c:c + 1]).then_inc(xa_set.sem, 1)
                    if g < NG:
                        negative(n, g, 2)
                    if m >= 0:
                        for j in range(NM):
                            o = filled_by(n, f"fcoM{m}{j}")
                            if j == 0:
                                if m:
                                    act.wait_ge(filled.sem, filled.after(n, f"fctM{m - 1}b"))
                                elif n.later():
                                    act.wait_ge(filled.sem, prior(filled, n))
                            nc.scalar.activation(h1[:, j, :], o[:, 0:GT], ACT.Gelu, bias=b1[:, j:j + 1]).then_inc(h1_set.sem, 1)
                    if g < NG:
                        act.wait_ge(ypre_set.sem, ypre_set.after(n, f"{g}.2"))
                        nc.scalar.activation(ym[:], ypre[:], ACT.Gelu).then_inc(ym_set.sem, 1)

            images(act, emit)

        @block.vector
        def _(dve):
            dve.wait_ge(wloaded, 16 * len(loads))
            dve.wait_ge(wset, 4)
            nc.vector.tensor_copy(wmt[:, 1, :, 0:HALF], wmt[:, 0, :, 0:HALF])
            nc.vector.tensor_scalar(wmt[:, 1, :, HALF:P], wmt[:, 0, :, HALF:P], -1.0, None, ALU.mult).then_inc(wready, 1)
            for v in range(1, len(tails)):
                nc.vector.tensor_copy(wtt[:, v, :, 0:HALF], wtt[:, 0, :, 0:HALF])
            for v in reversed(range(len(tails))):
                col = [(1, 1), (1, -1), (-1, 1), (-1, -1)].index(tails[v])
                if v == 0:
                    last.then_inc(wready, 1)
                    dve.wait_ge(wready, 2)
                last = nc.vector.tensor_scalar(wtt[:, v, :, HALF:P], wtt[:, 0, :, HALF:P], sgn[:, col:col + 1], None, ALU.mult)
            last.then_inc(wready, 1)

            def statistics(n, q):
                r, r2 = order[q] % TURN, order[q] % 2
                dve.wait_ge(turned.sem, turned.after(n, f"{q}b"))
                if order[q] >= 2:
                    dve.wait_ge(normed.sem, normed.after(n, f"{groups[order[q] - 2]}.{NB - 1}"))
                elif n.later():
                    dve.wait_ge(normed.sem, prior(normed, n))
                for j in range(NB):
                    nc.vector.bn_stats(tst[:, j, :], xt[:, r, j, :]).then_inc(tst_set.sem, 1)
                tst_set_value = held(dve, tst_set.after(n, f"{q}.{NB - 1}"))
                dve.wait_ge(wloaded, 16 * len(loads))
                dve.wait_ge(tst_set.sem, tst_set_value)
                for j in range(NB):
                    last = nc.vector.bn_aggr(tmv[:, r2, j, :], tst[:, j, :])
                last.then_inc(tmv_set.sem, 1)

            def normalise(n, q):
                r, r2 = order[q] % TURN, order[q] % 2
                dve.wait_ge(trs_set.sem, trs_set.after(n, q))
                for j in range(NB):
                    nc.vector.tensor_scalar(xt[:, r, j, :], xt[:, r, j, :], tmv[:, r2, j, 0:1], trs[:, r2, 1, j:j + 1],
                                            ALU.subtract, ALU.mult).then_inc(normed.sem, 1)

            def subtract(n, g, t):
                dve.wait_ge(neg_set.sem, neg_set.after(n, f"{g}.{t}"))
                if t == 0:
                    if g:
                        dve.wait_ge(ym_set.sem, ym_set.after(n, f"{g - 1}"))
                    elif n.later():
                        dve.wait_ge(ym_set.sem, prior(ym_set, n))
                nc.vector.tensor_tensor(ypre[:, t, :], wps[:, t, 0:WT], neg[:, t, :], ALU.subtract).then_inc(ypre_set.sem, 1)

            def emit(n):
                dve.wait_ge(fn_in.sem, fn_in.after(n, "x"))
                if n.later():
                    dve.wait_ge(fnm.sem, prior(fnm, n))
                for h, (src, rows) in enumerate([(fn_a, P), (fn_b, HALF)]):
                    for c in range(NCH):
                        nc.vector.bn_stats(fst[0:rows, h, c, :], src[:, bass.ts(c, TC)]).then_inc(fst_set.sem, 1)
                    fst_set_value = held(dve, fst_set.after(n, f"{'ab'[h]}{NCH - 1}"))
                    dve.wait_ge(wloaded, 16 * len(loads))
                    dve.wait_ge(fst_set.sem, fst_set_value)
                    nc.vector.bn_aggr(fmv[0:rows, h, :], fst[0:rows, h, :, :].rearrange("p c s -> p (c s)")).then_inc(fmv_set.sem, 1)
                dve.wait_ge(xp_in.sem, xp_in.after(n, "x"))
                for q in range(NG + 2):
                    if q < NG:
                        r = q // 2
                        for h, dst, src in (("a", x1_a, xp_a), ("b", x1_b, xp_b)):
                            dve.wait_ge(spread.sem, spread.after(n, f"{h}{r}"))
                            nc.vector.tensor_tensor(dst[:, bass.ts(q, GT)], dst[:, bass.ts(q, GT)], src[:, bass.ts(q, GT)], ALU.add).then_inc(x1_set.sem, 1)
                    if 1 <= q <= NG:
                        statistics(n, f"H{q - 1}")
                        normalise(n, f"H{q - 1}")
                dve.wait_ge(tpp_set.sem, tpp_set.after(n, "71"))
                nc.vector.tensor_scalar(tpm[:].rearrange("p a w -> p (a w)"), tpp[:].rearrange("p a w -> p (a w)"), sgn[:, 1:2], None, ALU.mult).then_inc(tpm_set.sem, 1)
                for g in range(NG + 1):
                    m = g - 1
                    if m >= 0:
                        for c, (h, dst, x1, rows) in enumerate([("a", x2_a, x1_a, P), ("b", x2_b, x1_b, HALF)]):
                            use = f"projM{m}{h}"
                            dve.wait_ge(filled.sem, filled.after(n, use))
                            if m >= 2:
                                dve.wait_ge(r_set.sem, r_set.after(n, f"{m - 2}b"))
                                dve.wait_ge(turned.sem, turned.after(n, f"M{m - 2}b"))
                            elif n.later():
                                dve.wait_ge(r_set.sem, prior(r_set, n))
                            nc.vector.scalar_tensor_tensor(dst[:, m % 2, :], fill[0:rows, bank_of[use], 0:GT], vec[0:rows, 2, c:c + 1],
                                                           x1[:, bass.ts(m, GT)], ALU.add, ALU.add).then_inc(x2_set.sem, 1)
                    if g < NG:
                        subtract(n, g, 0)
                    if m >= 0:
                        statistics(n, f"M{m}")
                        normalise(n, f"M{m}")
                    if g < NG:
                        subtract(n, g, 1)
                        subtract(n, g, 2)
                    if m >= 0:
                        for h, dst, res, rows in (("a", o_a, r_a, P), ("b", o_b, r_b, HALF)):
                            use = f"fctM{m}{h}"
                            dve.wait_ge(filled.sem, filled.after(n, use))
                            dve.wait_ge(r_set.sem, r_set.after(n, f"{m}{h}"))
                            c = o_out[m % 2]
                            if m >= 2:
                                dve.wait_ge(c.sem, c.after(n, f"{m - 2}"))
                            elif n.later():
                                dve.wait_ge(c.sem, prior(c, n))
                            nc.vector.tensor_tensor(dst[:, m % 2, :], fill[0:rows, bank_of[use], 0:GT], res[:, m % 2, :], ALU.add).then_inc(o_set.sem, 1)

            images(dve, emit)


def layers(nc, d):
    d = dict(d)
    d["fz"] = nc.dram_tensor("fused_dram", (IMG * NCH, CH, TC), F32, kind="Internal").ap()
    layer0(nc, d, IMG)
    layer1(nc, d, IMG)


def layouts(a):
    def tiles(v):
        return v.reshape((ND, P) + v.shape[1:]).swapaxes(0, 1)

    x = a["x"]
    padded = np.zeros((IMG, CH, SIDE + 2, SIDE), x.dtype)
    padded[:, :, 1:SIDE + 1] = x
    keep = np.ones((P, IMG * NCH, ND), np.float32)
    keep[:, NCH - 1::NCH] = 0
    xw = a["L0_conv_x_proj_w"]
    w = a["L1_conv_w_sed"]
    other = np.arange(NK) ^ 1
    mm, mt, tm, tt = w[:, :P, :P], w[:, :P, P:], w[:, P:, :P], w[:, P:, P:]
    even = np.arange(0, NK, 2)
    sgn = np.ones((P, 4), np.float32)
    sgn[HALF:, 1] = sgn[:HALF, 2] = sgn[:, 3] = -1
    return dict(
        xch=np.stack([padded[:, :, ROWS * c:ROWS * (c + 1) + 2].reshape(IMG, CH, TH) for c in range(NCH)], 1).reshape(-1, CH, TH),
        win=a["L0_conv_in_proj_w"].T,
        cw=tiles(a["L0_conv_conv_w"].reshape(DI, 9)),
        xpw=tiles(np.concatenate([xw[RANK:], xw[:RANK]]).T),
        dtw=a["L0_conv_dt_proj_w"].T,
        opw=a["L0_conv_out_proj_w"],
        fuw=a["L0_conv_fuse_w"][:, :, 0, 0].T,
        vecs=np.stack([tiles(a["L0_conv_" + k]) for k in ("conv_b", "dt_proj_b", "D_param", "ln_g", "ln_b")], 1),
        alog=tiles(a["L0_conv_A_log"]),
        ident=np.eye(P, dtype=np.float32),
        pick=np.tile(np.eye(2 * ST, dtype=np.float32), (2, 1)),
        keep=keep.reshape(P, -1),
        fub=a["L0_conv_fuse_b"].reshape(CH, 1),
        xperm=x.reshape(IMG, CH, NW, WIN, NW, WIN).transpose(0, 1, 3, 5, 2, 4).reshape(IMG, CH, TOK),
        wmm=mm.transpose(1, 0, 2),
        wkt=np.concatenate([tm, tm[other]], 1).transpose(1, 0, 2),
        wmt=np.concatenate([mt, mt[other]], 2).transpose(1, 0, 2),
        wtt=np.concatenate([np.concatenate([tt[even], tt[even + 1]], 2), np.concatenate([tt[even + 1], tt[even]], 2)], 1).transpose(1, 0, 2),
        pw=a["L1_conv_proj_w"], f1=a["L1_conv_fc1_w"],
        f2=a["L1_conv_fc2_w"].reshape(NM, P, CH).transpose(1, 0, 2),
        vec=np.stack([a["L1_conv_" + k] for k in ("norm1_g", "norm1_b", "proj_b", "norm2_g", "norm2_b", "fc2_b")]),
        b1=a["L1_conv_fc1_b"].reshape(NM, P).T,
        sgn=sgn)


def kernel(**inputs):
    import concourse.bacc as bacc
    from concourse.bass_utils import run_bass_kernel_spmd

    nc = bacc.Bacc("TRN2", target_bir_lowering=False, num_devices=1)
    arrays, d = {}, {}
    for name, a in layouts({k: np.asarray(v) for k, v in inputs.items()}).items():
        arrays[f"{name}_dram"] = np.ascontiguousarray(a)
        d[name] = nc.dram_tensor(f"{name}_dram", a.shape, F32, kind="ExternalInput").ap()
    d["out"] = nc.dram_tensor("out_dram", (IMG, CH, TOK), F32, kind="ExternalOutput").ap()
    layers(nc, d)
    got = run_bass_kernel_spmd(nc, [arrays], core_ids=[0]).results[0]["out_dram"]
    return got.reshape(IMG, CH, WIN, WIN, NW, NW).transpose(0, 1, 4, 2, 5, 3).reshape(IMG, CH, SIDE, SIDE)
```

```python
from contextlib import ExitStack

import numpy as np

import concourse.bass as bass
from concourse import mybir
from concourse.alu_op_type import AluOpType as ALU

F32 = mybir.dt.float32
F32R = mybir.dt.float32r
ACT = mybir.ActivationFunctionType
AX = mybir.AxisListType

P = 128
CH, HALF = 192, 64
IMG, SIDE = 8, 48
DI, ST, RANK = 384, 16, 12
ND = DI // P
ROWS = 8
TC = ROWS * SIDE
TH = (ROWS + 2) * SIDE
NCH = SIDE // ROWS
BANK = 512
RING = 4
AHEAD = 2
BY_PE = (2, 3, 4, 5, 6, 7, 8, 9, 11)
BY_DVE = tuple(s for s in range(ST) if s not in BY_PE)
EPS = 1e-5
TOK = SIDE * SIDE
WIN = 4
NW = SIDE // WIN
WT = NW * NW
NK = WIN * WIN
GT = 2 * WT
NG = NK // 2
BL, NB = 96, 3
HID = 4 * CH
NM = HID // P
TURN = 4



class At:

    def __init__(self, off, reg=None, mult=0):
        self.off, self.reg, self.mult = off, reg, mult

    def linear(self, k, c):
        c = k * self.off + c
        return c if self.reg is None else self.reg * (self.mult * k) + c

    def later(self):
        return self.reg is not None or self.off > 0

    def shift(self, d):
        return At(self.off + d, self.reg, self.mult)


class Count:

    def __init__(self, sem, when, events):
        self.sem, self.when, self.events = sem, when, events

    def _at(self, step, name, after):
        total, const = 0, 0
        inside, found = 0, False
        for ev, kind, w in self.events:
            first, last = self.when[kind]
            if step.reg is None:
                const += w * min(max(step.off - first, 0), last - first + 1)
                on = first <= step.off <= last
            else:
                total += w
                const -= w * first
                on = True
            if found:
                continue
            if ev == name:
                found = True
                inside += w if after and on else 0
            else:
                inside += w if on else 0
        assert found, name
        return const + inside if step.reg is None else step.linear(total, const + inside)

    def after(self, step, name):
        return self._at(step, name, True)

    def before(self, step, name):
        return self._at(step, name, False)


def held(eng, value):
    return value if isinstance(value, int) else eng.to_reg(value)


def layer0(nc, d, nimg):
    NS = nimg * NCH
    when = {"X": (-2, NS - 3), "A": (-1, NS - 2), "S": (0, NS - 1), "O": (1, NS)}
    ctx = ExitStack()
    with ctx:
        def sb(name, shape, dt=F32):
            return ctx.enter_context(nc.sbuf_tensor(name, shape, dt))

        def ps(name, shape):
            return ctx.enter_context(nc.psum_tensor(name, shape, F32))

        def sem(name):
            return ctx.enter_context(nc.semaphore(name))

        def count(name, events):
            return Count(sem(name), when, events)

        win_a, win_b = sb("win_a", [P, 2 * DI]), sb("win_b", [HALF, 2 * DI])
        cw, diag = sb("cw", [P, ND, 9]), sb("diag", [P, ND, 9, P])
        xpw = sb("xpw", [P, ND, RANK + 2 * ST])
        dtw = sb("dtw", [RANK, DI])
        opw_a, opw_b = sb("opw_a", [P, DI]), sb("opw_b", [HALF, DI])
        fuw_a, fuw_b = sb("fuw_a", [P, CH]), sb("fuw_b", [HALF, CH])
        wout = sb("wout", [P, ND, CH])
        vecs = sb("vecs", [P, 5, ND])
        fub = sb("fub", [P, 2])
        alog = sb("alog", [P, ND, ST])
        aneg = sb("aneg", [P, ND, ST])
        ident = sb("ident", [P, P])
        pick, pick_r = sb("pick", [4 * ST, 2 * ST]), sb("pick_r", [4 * ST, 2 * ST], F32R)
        keep = sb("keep", [P, NS * ND])
        mhalf = sb("mhalf", [P, ND])
        xc_a, xc_b = sb("xc_a", [P, TH]), sb("xc_b", [HALF, TH])
        xz_a, xz_b = sb("xz_a", [P, TC]), sb("xz_b", [HALF, TC])
        xin = sb("xin", [P, ND, ROWS + 2, SIDE + 2])
        pre, u = sb("pre", [P, ND, TC]), sb("u", [P, ND, TC])
        dtl = sb("dtl", [RANK, TC])
        soft = sb("soft", [P, ND, TC])
        delta = sb("delta", [P, 2, ND, TC])
        du = sb("du", [P, 2, ND, TC])
        bc = sb("bc", [4 * ST, 2, TC], F32R)
        brow = sb("brow", [P, RING, TC])
        drive = sb("drive", [P, RING, ND, TC])
        hst = sb("hst", [P, RING, ND, TC])
        carry = sb("carry", [P, ST, ND])
        decay = sb("decay", [P, RING, ND, TC])
        prod = sb("prod", [P, RING, ND, TC])
        ud, total = sb("ud", [P, ND, TC]), sb("total", [P, ND, TC])
        ysum = sb("ysum", [P, ND, TC])
        zpre, sz = sb("zpre", [P, ND, TC]), sb("sz", [P, ND, TC])
        yt = sb("yt", [P, ND, DI])
        st6, mv = sb("st6", [P, ND, 6]), sb("mv", [P, ND, 2])
        rstd = sb("rstd", [P, 2, ND])
        og = sb("og", [P, ND, TC])
        fz = sb("fz", [P, 2, TC])
        gather = ps("gather", [P, ND, BANK])
        bps = ps("bps", [P, BANK])
        cps = ps("cps", [P, 2, BANK])
        fill = ps("fill", [P, 2, BANK])

        loaded, prepared, merged, mergedone = sem("loaded"), sem("prepared"), sem("merged"), sem("mergedone")
        alogged = sem("alogged")
        uses = [("conv1", "A", 0), ("yT0", "O", 1), ("yT1", "O", 1), ("conv2", "A", 0), ("yT2", "O", 1),
                ("xp", "A", 1), ("z0", "S", 0), ("dt0", "A", 0), ("dt1", "A", 1), ("dt2", "A", 0), ("xin0", "X", 1),
                ("back0", "O", 0), ("xin1", "X", 1), ("back1", "O", 0), ("back2", "O", 1), ("xin2", "X", 0),
                ("z1", "S", 1), ("z2", "S", 0), ("out0", "O", 1), ("out1", "O", 0), ("conv0", "X", 1)]
        bank_of = {name: bank for name, _, bank in uses}
        filled = count("filled", [(name, kind, 1) for name, kind, _ in uses])
        xc_in = count("xc_in", [("x", "X", 32)])
        xz_in = count("xz_in", [("x", "S", 32)])
        ahead = lambda k: [(f"{s}", "S", 1) for s in range(k, ST)] + [(f"{s}", "A", 1) for s in range(k)]
        b_spread, b_copied, driven = count("b_spread", ahead(5)), count("b_copied", ahead(4)), count("driven", ahead(3))
        c_spread = count("c_spread", [(f"{s}", "S", 1) for s in range(ST)])
        decayed = count("decayed", [(f"{s % ST}.{m}", "S" if s < ST else "A", 1) for s in range(AHEAD, ST + AHEAD) for m in range(ND)])
        scanned = count("scanned", [(f"{s}.{m}", "S", 1) for s in range(ST) for m in range(ND)])
        scaled = count("scaled", [(f"{s}", "S", 1) for s in range(ST)])
        gathered = count("gathered", [(f"{s}", "S", 1) for s in BY_PE])
        added = count("added", [(f"{s}", "S", 1) for s in BY_DVE])
        summed = count("summed", [(f"{m}", "S", 1) for m in range(ND)])
        carried = count("carried", [(f"{ST - 1}", "O", 1)] + [(f"{s}", "S", 1) for s in range(ST - 1)])
        xin_set = count("xin_set", [(f"{m}", "X", 1) for m in range(ND)])
        pre_set = count("pre_set", [(f"{m}", "A", 1) for m in range(ND)])
        u_set = count("u_set", [("u", "A", 1)])
        sz_set = count("sz_set", [("sz", "O", 1)])
        zpre_set = count("zpre_set", [(f"{m}", "S", 1) for m in range(ND)])
        bchi, bclo, dtl_set = count("bchi", [("x", "A", 1)]), count("bclo", [("x", "A", 1)]), count("dtl_set", [("x", "A", 1)])
        dt_set = count("dt_set", [(f"{m}", "A", 1) for m in range(ND)])
        abs_set = count("abs_set", [(f"{m}", "A", 1) for m in range(ND)])
        exp_set, ln_set = count("exp_set", [("x", "A", 1)]), count("ln_set", [("x", "A", 1)])
        delta_set, du_set, ud_set = count("delta_set", [("x", "A", 1)]), count("du_set", [("x", "A", 1)]), count("ud_set", [("x", "A", 1)])
        yt_set = count("yt_set", [(f"{j}", "O", 1) for j in range(ND)])
        stat_set = count("stat_set", [(f"{j}", "O", 1) for j in range(ND)])
        mv_set = count("mv_set", [("x", "O", 1)])
        veps_set, rstd_set = count("veps_set", [("x", "O", 1)]), count("rstd_set", [("x", "O", 1)])
        normed = count("normed", [(f"{j}", "O", 1) for j in range(ND)])
        affined = count("affined", [(f"{m}", "O", 1) for m in range(ND)])
        gated = count("gated", [("x", "O", 1)])
        fz_set = count("fz_set", [("0", "O", 1), ("1", "O", 1)])
        stored = count("stored", [("x", "O", 32)])
        NLOADS = 16

        def readers(name):
            what, i = name.rstrip("012"), name[-1]
            return {"yT": [(yt_set, i)], "xin": [(xin_set, i)], "conv": [(pre_set, i)], "xp": [(dtl_set, "x"), (bclo, "x")],
                    "back": [(affined, i)], "dt": [(dt_set, i)], "out": [(fz_set, i)],
                    "z": [(zpre_set, i)]}[what]

        def before_it(n, name):
            names = [name for name, _, _ in uses]
            kinds = {name: kind for name, kind, _ in uses}
            for back in range(3):
                step = n.shift(-back)
                upto = names.index(name) if back == 0 else len(names)
                for other in reversed(names[:upto]):
                    if bank_of[other] == bank_of[name] and on(kinds[other], step):
                        return step, other
            return None

        def on(kind, n):
            return n.reg is not None or when[kind][0] <= n.off <= when[kind][1]

        def steps(eng, emit):
            for n in range(-2, 2):
                emit(At(n), n % 2)
            with eng.Fori(0, (NS - 4) // 2) as m:
                emit(At(2, m, 2), 0)
                emit(At(3, m, 2), 1)
            emit(At(NS - 2), NS % 2)
            emit(At(NS - 1), (NS - 1) % 2)
            emit(At(NS), NS % 2)

        block = ctx.enter_context(nc.Block())

        @block.sync
        def _(sp):
            for dst, src in [(win_a, d["win"][0:P]), (win_b, d["win"][P:CH]), (cw, d["cw"]), (xpw, d["xpw"]),
                             (dtw, d["dtw"]), (opw_a, d["opw"][0:P]), (opw_b, d["opw"][P:CH]),
                             (fuw_a, d["fuw"][0:P]), (fuw_b, d["fuw"][P:CH]), (vecs, d["vecs"]),
                             (alog, d["alog"]), (ident, d["ident"]), (pick, d["pick"]),
                             (keep, d["keep"])]:
                sp.dma_start(dst[:], src).then_inc(loaded, 16)
            sp.dma_start(fub[:, 0:1], d["fub"][0:P]).then_inc(loaded, 16)
            sp.dma_start(fub[0:HALF, 1:2], d["fub"][P:CH]).then_inc(loaded, 16)

            def emit(n, par):
                if on("X", n):
                    if n.reg is not None or n.off > -2:
                        xc_in_value = held(sp, xc_in.after(n.shift(-1), "x"))
                        filled_value = held(sp, filled.after(n.shift(-1), "xin2"))
                        sp.wait_ge(loaded, 16 * NLOADS)
                        sp.wait_ge(xc_in.sem, xc_in_value)
                        sp.wait_ge(filled.sem, filled_value)
                    j = n.linear(1, 2)
                    sp.dma_start(xc_a[:], d["xch"][j, 0:P, :]).then_inc(xc_in.sem, 16)
                    sp.dma_start(xc_b[:], d["xch"][j, P:CH, :]).then_inc(xc_in.sem, 16)
                if on("S", n):
                    if n.reg is not None or n.off > 0:
                        xz_in_value = held(sp, xz_in.after(n.shift(-1), "x"))
                        filled_value = held(sp, filled.after(n.shift(-1), "z2"))
                        sp.wait_ge(loaded, 16 * NLOADS)
                        sp.wait_ge(xz_in.sem, xz_in_value)
                        sp.wait_ge(filled.sem, filled_value)
                    j = n.linear(1, 0)
                    sp.dma_start(xz_a[:], d["xch"][j, 0:P, SIDE:SIDE + TC]).then_inc(xz_in.sem, 16)
                    sp.dma_start(xz_b[:], d["xch"][j, P:CH, SIDE:SIDE + TC]).then_inc(xz_in.sem, 16)
                if on("O", n):
                    sp.wait_ge(fz_set.sem, fz_set.after(n, "1"))
                    j = n.linear(1, -1)
                    sp.dma_start(d["fz"][j, 0:P, :], fz[:, 0, :]).then_inc(stored.sem, 16)
                    sp.dma_start(d["fz"][j, P:CH, :], fz[0:HALF, 1, :]).then_inc(stored.sem, 16)

            steps(sp, emit)
            sp.wait_ge(stored.sem, stored.after(At(NS), "x"))

        @block.tensor
        def _(pe):
            pe.wait_ge(loaded, 16 * NLOADS)
            for m in range(ND):
                if m >= 2:
                    pe.wait_ge(mergedone, m - 1)
                o = fill[:, m % 2, 0:CH]
                nc.tensor.matmul(o, opw_a[:, bass.ts(m, P)], fuw_a[:], start=True, stop=False)
                nc.tensor.matmul(o, opw_b[:, bass.ts(m, P)], fuw_b[:], start=False, stop=True).then_inc(merged, 1)
            pe.wait_ge(mergedone, ND)
            pe.wait_ge(prepared, 3)

            def use(n, name):
                earlier = before_it(n, name)
                for c, event in readers(earlier[1]) if earlier else []:
                    pe.wait_ge(c.sem, c.after(earlier[0].shift(1) if earlier[1] == "conv0" else earlier[0], event))
                return fill[:, bank_of[name], :]

            def y_back(n, j):
                o = use(n, f"yT{j}")
                for m in range(ND):
                    last = nc.tensor.transpose(o[:, bass.ts(m, P)], ysum[:, m, bass.ts(j, P)], ident[:])
                last.then_inc(filled.sem, 1)

            def x_in(n, m):
                o = use(n, f"xin{m}")[:, 0:TH]
                nc.tensor.matmul(o, win_a[:, bass.ts(m, P)], xc_a[:], start=True, stop=False)
                nc.tensor.matmul(o, win_b[:, bass.ts(m, P)], xc_b[:], start=False, stop=True).then_inc(filled.sem, 1)

            def conv(n, m, first, end):
                o = use(n, f"conv{m}") if first == 0 else fill[:, bank_of[f"conv{m}"], :]
                if first == 0:
                    pe.wait_ge(xin_set.sem, xin_set.after(n if m == 0 else n.shift(-1), f"{m}"))
                for tap in range(first, end):
                    dy, dx = tap // 3, tap % 3
                    last = nc.tensor.matmul(o[:, 0:TC], diag[:, m, tap, :], xin[:, m, dy:dy + ROWS, dx:dx + SIDE],
                                            start=(tap == 0), stop=(tap == 8))
                if end == 9:
                    last.then_inc(filled.sem, 1)

            def x_proj(n):
                o = use(n, "xp")
                pe.wait_ge(u_set.sem, u_set.after(n, "u"))
                for m in range(ND):
                    last = nc.tensor.matmul(o[0:2 * ST + RANK, 0:TC], xpw[:, m, :], u[:, m, :], start=(m == 0), stop=(m == ND - 1))
                last.then_inc(filled.sem, 1)

            def dt(n, m):
                o = use(n, f"dt{m}")
                if m == 0:
                    pe.wait_ge(dtl_set.sem, dtl_set.after(n, "x"))
                nc.tensor.matmul(o[:, 0:TC], dtw[:, bass.ts(m, P)], dtl[:], start=True, stop=True).then_inc(filled.sem, 1)

            def back(n, m):
                o = use(n, f"back{m}")
                if m == 0:
                    pe.wait_ge(normed.sem, normed.after(n, f"{ND - 1}"))
                for j in range(ND):
                    last = nc.tensor.transpose(o[:, bass.ts(j, P)], yt[:, j, bass.ts(m, P)], ident[:])
                last.then_inc(filled.sem, 1)

            def out(n, h):
                o = use(n, f"out{h}")
                if h == 0:
                    pe.wait_ge(gated.sem, gated.after(n, "x"))
                cols, lo = (P, 0) if h == 0 else (HALF, P)
                for m in range(ND):
                    last = nc.tensor.matmul(o[0:cols, 0:TC], wout[:, m, lo:lo + cols], og[:, m, :], start=(m == 0), stop=(m == ND - 1))
                last.then_inc(filled.sem, 1)

            def z_in(n, m):
                o = use(n, f"z{m}")[:, 0:TC]
                if m == 0:
                    pe.wait_ge(xz_in.sem, xz_in.after(n, "x"))
                nc.tensor.matmul(o, win_a[:, DI + m * P:DI + m * P + P], xz_a[:], start=True, stop=False)
                nc.tensor.matmul(o, win_b[:, DI + m * P:DI + m * P + P], xz_b[:], start=False, stop=True).then_inc(filled.sem, 1)

            def spread_b(n, s, par):
                pe.wait_ge(b_copied.sem, b_copied.after(n, "3") if s == 4 else b_copied.before(n, f"{s}"))
                if s == 0:
                    pe.wait_ge(bclo.sem, bclo.after(n, "x"))
                nc.tensor.matmul(bps[:, 0:TC], pick_r[:, s:s + 1].broadcast_to([4 * ST, P]), bc[:, par, :],
                                 start=True, stop=True).then_inc(b_spread.sem, 1)

            def spread_c(n, s, par):
                if s >= 2:
                    pe.wait_ge(scaled.sem, scaled.after(n, f"{s - 2}"))
                elif n.reg is not None or n.off > 0:
                    pe.wait_ge(scaled.sem, scaled.after(n.shift(-1), f"{s + ST - 2}"))
                nc.tensor.matmul(cps[:, s % 2, 0:TC], pick_r[:, ST + s:ST + s + 1].broadcast_to([4 * ST, P]), bc[:, par, :],
                                 start=True, stop=True).then_inc(c_spread.sem, 1)

            def gather_up(n, s):
                pe.wait_ge(scaled.sem, scaled.after(n, f"{s}"))
                if s == BY_PE[0] and n.later():
                    pe.wait_ge(summed.sem, summed.after(n.shift(-1), f"{ND - 1}"))
                for m in range(ND):
                    last = nc.tensor.matmul(gather[:, m, 0:TC], ident[:], prod[:, s % RING, m, :], start=(s == BY_PE[0]), stop=(s == BY_PE[-1]))
                last.then_inc(gathered.sem, 1)

            def emit(n, par):
                X, A, S, O = on("X", n), on("A", n), on("S", n), on("O", n)
                for s in range(ST):
                    if S:
                        spread_c(n, s, par)
                    if S and s - 2 in BY_PE:
                        gather_up(n, s - 2)
                    if S and s + 5 < ST:
                        spread_b(n, s + 5, par)
                    if A and s + 5 >= ST:
                        spread_b(n, s + 5 - ST, 1 - par)
                    if A and s < 4:
                        conv(n, 1 + s // 2, 4 * (s % 2), 4 + 5 * (s % 2))
                    if O and 1 <= s <= 3:
                        if s == 1:
                            pe.wait_ge(summed.sem, summed.after(n.shift(-1), f"{ND - 1}"))
                        y_back(n, s - 1)
                    if A and s == 5:
                        x_proj(n)
                    if S and s == 6:
                        z_in(n, 0)
                    if A and s == 7:
                        dt(n, 0), dt(n, 1)
                    if A and s == 8:
                        dt(n, 2)
                    if X and s == 8:
                        pe.wait_ge(xc_in.sem, xc_in.after(n, "x"))
                        x_in(n, 0)
                    if O and s == 9:
                        back(n, 0)
                    if X and s == 9:
                        x_in(n, 1)
                    if O and s == 10:
                        back(n, 1), back(n, 2)
                    if X and s == 11:
                        x_in(n, 2)
                    if S and s in (11, 12):
                        z_in(n, s - 10)
                    if O and s in (13, 14):
                        out(n, s - 13)
                    if X and s >= 14:
                        conv(n, 0, 4 * (s - 14), 4 + 5 * (s - 14))

            steps(pe, emit)

        @block.scalar
        def _(act):
            act.wait_ge(loaded, 16 * NLOADS)
            nc.scalar.activation(aneg[:], alog[:], ACT.Exp).then_inc(alogged, 1)
            act.wait_ge(prepared, 3)

            def filled_by(n, name):
                act.wait_ge(filled.sem, filled.after(n, name))
                return fill[:, bank_of[name], :]

            def more(n, first):
                return n.reg is not None or n.off > first

            def take_y(n, j):
                o = filled_by(n, f"yT{j}")
                if j == 0 and more(n, 1):
                    act.wait_ge(filled.sem, filled.after(n.shift(-1), "back2"))
                nc.scalar.activation(yt[:, j, :], o[:, 0:DI], ACT.Copy).then_inc(yt_set.sem, 1)

            def take_xin(n, m):
                o = filled_by(n, f"xin{m}")
                nc.scalar.activation(xin[:, m, :, 1:SIDE + 1], o[:, 0:TH].rearrange("p (r w) -> p r w", w=SIDE),
                                     ACT.Copy).then_inc(xin_set.sem, 1)

            def take_conv(n, m):
                o = filled_by(n if m else n.shift(-1), f"conv{m}")
                nc.scalar.activation(pre[:, m, :], o[:, 0:TC], ACT.Identity, bias=vecs[:, 0, m:m + 1]).then_inc(pre_set.sem, 1)

            def take_z(n, m):
                o = filled_by(n, f"z{m}")
                if m == 0 and on("O", n):
                    act.wait_ge(sz_set.sem, sz_set.after(n, "sz"))
                nc.scalar.activation(zpre[:, m, :], o[:, 0:TC], ACT.Copy).then_inc(zpre_set.sem, 1)

            def take_dt(n, m, nxt):
                o = filled_by(n, f"dt{m}")
                if m == 0 and more(n, -1):
                    act.wait_ge(delta_set.sem, delta_set.after(n.shift(-1), "x"))
                nc.scalar.activation(soft[:, m, :], o[:, 0:TC], ACT.Abs, bias=vecs[:, 1, m:m + 1]).then_inc(abs_set.sem, 1)
                if m == 0 and n.later():
                    act.wait_ge(decayed.sem, decayed.after(n.shift(-1), f"{ST - 1}.{ND - 1}"))
                nc.scalar.activation(delta[:, nxt, m, :], o[:, 0:TC], ACT.Relu, bias=vecs[:, 1, m:m + 1]).then_inc(dt_set.sem, 1)

            def take_back(n, m):
                o = filled_by(n, f"back{m}")
                if m == 0 and more(n, 1):
                    act.wait_ge(filled.sem, filled.after(n.shift(-1), "out1"))
                nc.scalar.activation(og[:, m, :], o[:, 0:TC], ACT.Identity, bias=vecs[:, 4, m:m + 1],
                                     scale=vecs[:, 3, m:m + 1]).then_inc(affined.sem, 1)

            def take_out(n, h):
                rows = P if h == 0 else HALF
                o = filled_by(n, f"out{h}")
                if h == 0 and more(n, 1):
                    act.wait_ge(stored.sem, stored.after(n.shift(-1), "x"))
                nc.scalar.activation(fz[0:rows, h, :], o[0:rows, 0:TC], ACT.Identity, bias=fub[0:rows, h:h + 1]).then_inc(fz_set.sem, 1)

            def silus(n):
                if on("A", n):
                    act.wait_ge(pre_set.sem, pre_set.after(n, f"{ND - 1}"))
                    if more(n, -1):
                        act.wait_ge(du_set.sem, du_set.after(n.shift(-1), "x"))
                    nc.scalar.activation(u[:], pre[:], ACT.Silu).then_inc(u_set.sem, 1)
                if on("O", n):
                    act.wait_ge(zpre_set.sem, zpre_set.after(n.shift(-1), f"{ND - 1}"))
                    if more(n, 1):
                        act.wait_ge(gated.sem, gated.after(n.shift(-1), "x"))
                    nc.scalar.activation(sz[:], zpre[:], ACT.Silu).then_inc(sz_set.sem, 1)

            def softplus_exp(n):
                act.wait_ge(abs_set.sem, abs_set.after(n, f"{ND - 1}"))
                nc.scalar.activation(soft[:], soft[:], ACT.Exp, scale=-1.0).then_inc(exp_set.sem, 1)

            def softplus_log(n):
                act.wait_ge(exp_set.sem, exp_set.after(n, "x"))
                nc.scalar.activation(soft[:], soft[:], ACT.Ln, bias=1.0).then_inc(ln_set.sem, 1)

            def decays(n, s, par):
                for m in range(ND):
                    if s == 0 and m == 0:
                        act.wait_ge(delta_set.sem, delta_set.after(n, "x"))
                    if s >= RING:
                        act.wait_ge(scanned.sem, scanned.after(n, f"{s - RING}.{m}"))
                    elif s >= AHEAD and n.later():
                        act.wait_ge(scanned.sem, scanned.after(n.shift(-1), f"{s + ST - RING}.{m}"))
                    elif s < AHEAD and on("S", n):
                        act.wait_ge(scanned.sem, scanned.after(n, f"{s + ST - RING}.{m}"))
                    nc.scalar.activation(decay[:, s % RING, m, :], delta[:, par, m, :], ACT.Exp,
                                         scale=aneg[:, m, s:s + 1]).then_inc(decayed.sem, 1)

            def copy_b(n, t, early):
                spread = b_spread.after(n, f"{t}") if early or t > 4 else b_spread.after(n.shift(-1), f"{t}")
                act.wait_ge(b_spread.sem, spread)
                if t >= 4:
                    act.wait_ge(driven.sem, driven.after(n, f"{t - 4}") if t - 4 >= 3 else driven.after(n.shift(-1), f"{t - 4}"))
                elif on("S", n):
                    act.wait_ge(driven.sem, driven.after(n, f"{t + ST - 4}"))
                nc.scalar.activation(brow[:, t % RING, :], bps[:, 0:TC], ACT.Copy).then_inc(b_copied.sem, 1)

            def emit(n, par):
                X, A, S, O = on("X", n), on("A", n), on("S", n), on("O", n)
                for s in range(ST):
                    if S and s + 4 < ST:
                        copy_b(n, s + 4, False)
                    if A and s + 4 >= ST:
                        copy_b(n, s + 4 - ST, True)
                    if S and s + AHEAD < ST:
                        decays(n, s + AHEAD, par)
                    if A and s + AHEAD >= ST:
                        decays(n, s + AHEAD - ST, 1 - par)
                    if A and s in (0, 2, 4):
                        take_conv(n, s // 2)
                    if O and 2 <= s <= 4:
                        take_y(n, s - 2)
                    if s == 4:
                        silus(n)
                    if A and s == 6:
                        x_low(n, 1 - par)
                    if S and s == 7:
                        take_z(n, 0)
                    if A and s == 8:
                        take_dt(n, 0, 1 - par), take_dt(n, 1, 1 - par)
                    if A and s == 9:
                        take_dt(n, 2, 1 - par)
                    if X and s == 9:
                        take_xin(n, 0)
                    if A and s == 9:
                        softplus_exp(n)
                    if A and s == 10:
                        softplus_log(n)
                    if O and s == 10:
                        take_back(n, 0)
                    if X and s == 10:
                        take_xin(n, 1)
                    if O and s == 11:
                        take_back(n, 1), take_back(n, 2)
                    if X and s == 12:
                        take_xin(n, 2)
                    if S and s in (12, 13):
                        take_z(n, s - 11)
                    if O and s >= 14:
                        take_out(n, s - 14)

            def x_low(n, nxt):
                o = filled_by(n, "xp")
                if n.reg is not None or n.off > 0:
                    act.wait_ge(c_spread.sem, c_spread.after(n.shift(-1), f"{ST - 1}"))
                nc.scalar.activation(bc[0:2 * ST, nxt, :], o[0:2 * ST, 0:TC], ACT.Copy).then_inc(bchi.sem, 1)
                nc.scalar.activation(dtl[:], o[2 * ST:2 * ST + RANK, 0:TC], ACT.Copy).then_inc(dtl_set.sem, 1)

            steps(act, emit)

        @block.gpsimd
        def _(pool):
            nc.gpsimd.memset(mhalf[:], -0.5).then_inc(prepared, 1)
            pool.wait_ge(loaded, 16 * NLOADS)

            def emit(n, par):
                A, S, O = on("A", n), on("S", n), on("O", n)
                nxt = 1 - par
                for s in range(ST):
                    sB = s + 3
                    if (S and sB < ST) or (A and sB >= ST):
                        t = sB % ST
                        mine = nxt if sB >= ST else par
                        pool.wait_ge(b_copied.sem, b_copied.after(n.shift(-1), "3") if t == 3 else b_copied.after(n, f"{t}"))
                        if sB >= ST:
                            pool.wait_ge(du_set.sem, du_set.after(n, "x"))
                        if t >= 4:
                            pool.wait_ge(scanned.sem, scanned.after(n, f"{t - 4}.{ND - 1}"))
                        elif sB >= ST and S:
                            pool.wait_ge(scanned.sem, scanned.after(n, f"{t + ST - 4}.{ND - 1}"))
                        elif t == 3 and (n.reg is not None or n.off > 0):
                            pool.wait_ge(scanned.sem, scanned.after(n.shift(-1), f"{ST - 1}.{ND - 1}"))
                        nc.gpsimd.tensor_tensor(drive[:, t % RING], du[:, mine], brow[:, t % RING, :].unsqueeze(1).broadcast_to([P, ND, TC]),
                                                ALU.mult).then_inc(driven.sem, 1)
                    if S and s:
                        take_carry(n, n, s - 1)
                    elif O and s == 0:
                        take_carry(n, n.shift(-1), ST - 1)
                    if O and s == 7:
                        mv_set_value = held(pool, mv_set.after(n, "x"))
                        pool.wait_ge(loaded, 16 * NLOADS)
                        pool.wait_ge(mv_set.sem, mv_set_value)
                        nc.gpsimd.tensor_scalar(rstd[:, 0, :], mv[:, :, 1], EPS, 1.0, ALU.add, ALU.mult).then_inc(veps_set.sem, 1)
                        pool.wait_ge(veps_set.sem, veps_set.after(n, "x"))
                        nc.gpsimd.tensor_tensor(rstd[:, 1, :], rstd[:, 0, :], mhalf[:], ALU.pow).then_inc(rstd_set.sem, 1)
                    if A and s == 11:
                        pool.wait_ge(ln_set.sem, ln_set.after(n, "x"))
                        pool.wait_ge(dt_set.sem, dt_set.after(n, f"{ND - 1}"))
                        nc.gpsimd.tensor_tensor(delta[:, nxt], delta[:, nxt], soft[:], ALU.add).then_inc(delta_set.sem, 1)
                        pool.wait_ge(delta_set.sem, delta_set.after(n, "x"))
                        nc.gpsimd.tensor_tensor(du[:, nxt], delta[:, nxt], u[:], ALU.mult).then_inc(du_set.sem, 1)
                    if O and s == 12:
                        pool.wait_ge(affined.sem, affined.after(n, f"{ND - 1}"))
                        pool.wait_ge(sz_set.sem, sz_set.after(n, "sz"))
                        nc.gpsimd.tensor_tensor(og[:], og[:], sz[:], ALU.mult).then_inc(gated.sem, 1)
                    if A and s == 8:
                        u_value = held(pool, u_set.after(n, "u"))
                        if S:
                            added_value = held(pool, added.after(n, f"{BY_DVE[0]}"))
                        pool.wait_ge(loaded, 16 * NLOADS)
                        pool.wait_ge(u_set.sem, u_value)
                        if S:
                            pool.wait_ge(added.sem, added_value)
                        for m in range(ND):
                            last = nc.gpsimd.tensor_scalar(ud[:, m, :], u[:, m, :], vecs[:, 2, m:m + 1], 1.0, ALU.mult, ALU.mult)
                        last.then_inc(ud_set.sem, 1)

            def take_carry(n, chunk, s):
                scanned_value = held(pool, scanned.after(chunk, f"{s}.{ND - 1}"))
                pool.wait_ge(loaded, 16 * NLOADS)
                pool.wait_ge(scanned.sem, scanned_value)
                nc.gpsimd.tensor_tensor(carry[:, s, :], hst[:, s % RING, :, TC - 1], keep[:, bass.ds(chunk.linear(ND, 0), ND)],
                                        ALU.mult).then_inc(carried.sem, 1)

            steps(pool, emit)

        @block.vector
        def _(dve):
            dve.wait_ge(loaded, 16 * NLOADS)
            nc.vector.tensor_copy(pick_r[:], pick[:])
            for m in range(ND):
                for tap in range(9):
                    last = nc.vector.tensor_scalar(diag[:, m, tap, :], ident[:], cw[:, m, tap:tap + 1], None, ALU.mult)
            nc.vector.memset(xin[:, :, :, 0:1], 0.0)
            last = nc.vector.memset(xin[:, :, :, SIDE + 1:SIDE + 2], 0.0).then_inc(prepared, 1)
            for m in range(ND):
                dve.wait_ge(merged, m + 1)
                nc.vector.tensor_copy(wout[:, m, :], fill[:, m % 2, 0:CH]).then_inc(mergedone, 1)
            dve.wait_ge(alogged, 1)
            nc.vector.tensor_scalar(aneg[:], aneg[:], -1.0, None, ALU.mult).then_inc(prepared, 1)

            def scale(n, s):
                dve.wait_ge(scanned.sem, scanned.after(n, f"{s}.{ND - 1}"))
                dve.wait_ge(c_spread.sem, c_spread.after(n, f"{s}"))
                if s >= RING or n.later():
                    step, t = (n, s - RING) if s >= RING else (n.shift(-1), s + ST - RING)
                    c = gathered if t in BY_PE else added
                    dve.wait_ge(c.sem, c.after(step, f"{t}"))
                nc.vector.tensor_tensor(prod[:, s % RING], hst[:, s % RING], cps[:, s % 2, 0:TC].unsqueeze(1).broadcast_to([P, ND, TC]),
                                        ALU.mult).then_inc(scaled.sem, 1)

            def add(n, s):
                dve.wait_ge(scaled.sem, scaled.after(n, f"{s}"))
                if s == BY_DVE[0]:
                    dve.wait_ge(ud_set.sem, ud_set.after(n.shift(-1), "x"))
                    if n.later():
                        dve.wait_ge(summed.sem, summed.after(n.shift(-1), f"{ND - 1}"))
                else:
                    dve.wait_ge(added.sem, added.before(n, f"{s}"))
                nc.vector.tensor_tensor(total[:], (ud if s == BY_DVE[0] else total)[:], prod[:, s % RING], ALU.add).then_inc(added.sem, 1)

            def add_up(n):
                dve.wait_ge(added.sem, added.after(n, f"{BY_DVE[-1]}"))
                dve.wait_ge(gathered.sem, gathered.after(n, f"{BY_PE[-1]}"))
                if n.later():
                    dve.wait_ge(filled.sem, filled.after(n, "yT2"))
                for m in range(ND):
                    nc.vector.tensor_tensor(ysum[:, m, :], gather[:, m, 0:TC], total[:, m, :], ALU.add).then_inc(summed.sem, 1)

            def emit(n, par):
                A, S, O = on("A", n), on("S", n), on("O", n)
                nxt = 1 - par
                later = n.reg is not None or n.off > 0
                for s in range(ST):
                    if S:
                        for m in range(ND):
                            if m == 0:
                                dve.wait_ge(driven.sem, driven.after(n, f"{s}") if s >= 3 else driven.after(n.shift(-1), f"{s}"))
                                if s >= RING:
                                    dve.wait_ge(scaled.sem, scaled.after(n, f"{s - RING}"))
                                    dve.wait_ge(carried.sem, carried.after(n, f"{s - RING}"))
                                elif later:
                                    dve.wait_ge(scaled.sem, scaled.after(n.shift(-1), f"{s + ST - RING}"))
                                    if s < RING - 1:
                                        dve.wait_ge(carried.sem, carried.after(n.shift(-1), f"{s + ST - RING}"))
                                    else:
                                        dve.wait_ge(carried.sem, carried.after(n, f"{ST - 1}"))
                            dve.wait_ge(decayed.sem, decayed.after(n if s >= AHEAD else n.shift(-1), f"{s}.{m}"))
                            nc.vector.tensor_tensor_scan(hst[:, s % RING, m, :], decay[:, s % RING, m, :], drive[:, s % RING, m, :],
                                                         carry[:, s, m:m + 1] if later else 0.0, ALU.mult, ALU.add).then_inc(scanned.sem, 1)
                        if s >= 1:
                            scale(n, s - 1)
                        if s - 2 in BY_DVE:
                            add(n, s - 2)
                    if O and s == 6:
                        for j in range(ND):
                            dve.wait_ge(yt_set.sem, yt_set.after(n, f"{j}"))
                            nc.vector.bn_stats(st6[:, j, :], yt[:, j, :]).then_inc(stat_set.sem, 1)
                        stat_set_value = held(dve, stat_set.after(n, f"{ND - 1}"))
                        dve.wait_ge(loaded, 16 * NLOADS)
                        dve.wait_ge(stat_set.sem, stat_set_value)
                        for j in range(ND):
                            last = nc.vector.bn_aggr(mv[:, j, :], st6[:, j, :])
                        last.then_inc(mv_set.sem, 1)
                    if O and s == 8:
                        dve.wait_ge(rstd_set.sem, rstd_set.after(n, "x"))
                        for j in range(ND):
                            nc.vector.tensor_scalar(yt[:, j, :], yt[:, j, :], mv[:, j, 0:1], rstd[:, 1, j:j + 1],
                                                    ALU.subtract, ALU.mult).then_inc(normed.sem, 1)
                    if A and s == 7:
                        dve.wait_ge(bchi.sem, bchi.after(n, "x"))
                        dve.wait_ge(dtl_set.sem, dtl_set.after(n, "x"))
                        if n.reg is not None or n.off > 0:
                            dve.wait_ge(c_spread.sem, c_spread.after(n.shift(-1), f"{ST - 1}"))
                        nc.vector.tensor_tensor(bc[2 * ST:4 * ST, nxt, :], fill[0:2 * ST, bank_of["xp"], 0:TC], bc[0:2 * ST, nxt, :],
                                                ALU.subtract).then_inc(bclo.sem, 1)
                if S:
                    scale(n, ST - 1)
                    if ST - 2 in BY_DVE:
                        add(n, ST - 2)
                    add(n, ST - 1)
                    add_up(n)

            steps(dve, emit)


def sedenion_signs():
    def conj(x):
        return x if len(x) == 1 else np.concatenate([conj(x[:len(x) // 2]), -x[len(x) // 2:]])

    def mult(a, b):
        if len(a) == 1:
            return a * b
        h = len(a) // 2
        a1, a2, b1, b2 = a[:h], a[h:], b[:h], b[h:]
        return np.concatenate([mult(a1, b1) - mult(conj(b2), a2), mult(b2, a1) + mult(a2, conj(b1))])

    eye = np.eye(NK, dtype=np.int64)
    return [[int(mult(eye[i], eye[i ^ k])[k]) for k in range(NK)] for i in range(NK)]


def layer1(nc, d, nimg):
    when = {"H": (-1, nimg - 2), "E": (0, nimg - 1)}
    sign = sedenion_signs()
    pairs = range(NK // 2)
    tails = sorted({(sign[2 * p][2 * q] * sign[2 * p][2 * q + 1], sign[2 * p + 1][2 * q] * sign[2 * p + 1][2 * q + 1])
                    for p in pairs for q in pairs})
    ctx = ExitStack()
    with ctx:
        def sb(name, shape, dt=F32):
            return ctx.enter_context(nc.sbuf_tensor(name, shape, dt))

        def ps(name, shape):
            return ctx.enter_context(nc.psum_tensor(name, shape, F32))

        def sem(name):
            return ctx.enter_context(nc.semaphore(name))

        def count(name, kind, events, w=1):
            return Count(sem(name), when, [(e, kind or ("H" if "H" in e else "E"), w) for e in events])

        wmm, wkt = sb("wmm", [P, NK, P]), sb("wkt", [P, NK, P])
        wmt, wtt = sb("wmt", [P, 2, NK, P]), sb("wtt", [P, len(tails), NK // 2, P])
        pw_a, pw_b = sb("pw_a", [P, CH]), sb("pw_b", [P, 2, CH])
        f1w, f1t, f1l = sb("f1w", [P, 2, HID], F32R), sb("f1t", [P, HID], F32R), sb("f1l", [HALF, HID], F32R)
        f2w = sb("f2w", [P, 2, NM * CH + HALF], F32R)
        vec = sb("vec", [P, 6, 2])
        b1 = sb("b1", [P, NM])
        sgn = sb("sgn", [P, 4])
        idn = sb("idn", [P, P])
        half = sb("half", [P, NB])
        fn_a, fn_b = sb("fn_a", [P, TOK]), sb("fn_b", [HALF, TOK])
        fst, fmv, frs = sb("fst", [P, 2, NCH, 6]), sb("fmv", [P, 2, 2]), sb("frs", [P, 4, 2])
        x1_a, x1_b = sb("x1_a", [P, 2, TOK]), sb("x1_b", [HALF, 2, TOK])
        xt = sb("xt", [BL, TURN, NB, CH])
        tst, tmv, trs = sb("tst", [BL, NB, 6]), sb("tmv", [BL, 2, NB, 2]), sb("trs", [BL, 2, 2, NB])
        xm = sb("xm", [P, 2, NK, WT])
        tpp, tpm = sb("tpp", [P, 2, NK // 2, WT]), sb("tpm", [P, 2, NK // 2, WT])
        neg, ypre, ym = sb("neg", [P, 3, WT]), sb("ypre", [P, 3, WT]), sb("ym", [P, 3, WT])
        x2_a, x2_b = sb("x2_a", [P, 2, GT]), sb("x2_b", [HALF, 2, GT])
        xa_a, xa_b = sb("xa_a", [P, GT]), sb("xa_b", [HALF, GT])
        xs, xt2 = sb("xs", [P, 2, GT], F32R), sb("xt2", [P, GT], F32R)
        h1, hs = sb("h1", [P, 2, GT]), sb("hs", [P, 2, NM, GT], F32R)
        o_a, o_b = sb("o_a", [P, 2, GT]), sb("o_b", [HALF, 2, GT])
        wps = ps("wps", [P, 3, BANK])
        fill = ps("fill5", [P, 5, BANK])

        TURNS = {1: (0,), 2: (1,), 3: (2,), 4: (3,), 5: (4,), 6: (5,), 7: (6, 7)}
        turns = lambda g: TURNS.get(g, ())
        uses, groups = [], []
        for g in range(NG + 1):
            m = g - 1
            if m >= 0:
                uses += [f"projM{m}a", f"projM{m}b"]
                groups.append(f"M{m}")
            uses += [f"backH{q}{h}" for q in turns(g - 1) for h in "ab"]
            if m >= 0:
                uses += [f"turnM{m}a", f"turnM{m}b", f"backM{m}a", f"backM{m}b"]
            uses += [f"turnH{q}{h}" for q in turns(g) for h in "ab"]
            groups += [f"H{q}" for q in turns(g)]
            if m >= 0:
                uses += [f"fcoM{m}{j}" for j in range(NM)] + [f"fctM{m}a", f"fctM{m}b"]
        NBANK = 5
        while len(uses) % NBANK:
            NBANK -= 1
        bank_of = {u: i % NBANK for i, u in enumerate(uses)}
        order = {u: i for i, u in enumerate(groups)}
        ab = lambda names: [f"{n}{h}" for n in names for h in "ab"]
        gs = [f"{g}" for g in range(NG)]

        wloaded, wset, wready, wcut = sem("wloaded"), sem("wset"), sem("wready"), sem("wcut")
        filled = count("filled1", None, uses)
        fn_in, xp_in = count("fn_in", "H", ["x"], 32), count("xp_in", "H", ["x"], 32)
        fst_set = count("fst_set", "H", [f"{h}{c}" for h in "ab" for c in range(NCH)])
        fmv_set, fve, frs_set = count("fmv_set", "H", "ab"), count("fve", "H", ["x"]), count("frs_set", "H", ["x"])
        fnm, fnb = count("fnm", "H", ["x"]), count("fnb", "H", ["x"])
        spread = count("spread1", "H", [f"{h}{r}" for r in range(WIN) for h in "ab"])
        x1_set = count("x1_set", "H", ab(gs))
        turned = count("turned", None, ab(groups))
        tst_set = count("tst_set", None, [f"{q}.{j}" for q in groups for j in range(NB)])
        tmv_set, tve, trs_set = count("tmv_set", None, groups), count("tve", None, groups), count("trs_set", None, groups)
        normed = count("normed1", None, [f"{q}.{j}" for q in groups for j in range(NB)])
        xm_set, tpp_set = count("xm_set", "H", gs), count("tpp_set", "H", [f"{g}{h}" for g in gs for h in "01"])
        tpm_set = count("tpm_set", "H", ["x"])
        wtile = [f"{g}.{t}" for g in range(NG) for t in range(3)]
        wdone, neg_set, ypre_set = count("wdone", "E", wtile), count("neg_set", "E", wtile), count("ypre_set", "E", wtile)
        ym_set = count("ym_set", "E", gs)
        x2_set, xa_set, xs_set = count("x2_set", "E", ab(gs)), count("xa_set", "E", ab(gs)), count("xs_set", "E", ab(gs))
        hs_set = count("hs_set", "E", [f"{g}{m}" for g in gs for m in range(NM)])
        h1_set = count("h1_set", "E", [f"{g}{m}" for g in gs for m in range(NM)])
        o_set = count("o_set", "E", ab(gs))
        o_out = [count(f"o_out{par}", "E", [g for g in gs if int(g) % 2 == par], 32) for par in range(2)]

        def reader(use):
            what, rest = use[:4], use[4:]
            g = rest[1:-1]
            if what == "turn":
                return turned, rest
            if what == "back":
                if rest[0] == "M":
                    return xa_set, rest[1:]
                return (xm_set, g) if rest[-1] == "a" else (tpp_set, g + "1")
            return {"proj": (x2_set, rest[1:]), "fcoM": (h1_set, use[4:]), "fctM": (o_set, use[4:])}[what if what == "proj" else use[:4]]

        def on(kind, n):
            return n.reg is not None or when[kind][0] <= n.off <= when[kind][1]

        def more(kind, n):
            return n.reg is not None or n.off > when[kind][0]

        def before_it(n, name, names, ring):
            i = names.index(name)
            for back in range(3):
                step = n.shift(-back)
                for k in reversed(range(i if back == 0 else len(names))):
                    if k % ring == i % ring and on("H" if "H" in names[k] else "E", step):
                        return step, names[k]
            return None

        def prior(c, n):
            return c.after(n.shift(-1), c.events[-1][0])

        block = ctx.enter_context(nc.Block())

        def images(eng, emit):
            emit(At(-1), 1)
            emit(At(0), 0)
            with eng.Fori(0, (nimg - 2) // 2) as b:
                emit(At(1, b, 2), 1)
                emit(At(2, b, 2), 0)
            emit(At(nimg - 1), (nimg - 1) % 2)

        raw1, raw2, raw1t = fn_a[:, 0:HID], fn_a[:, HID:HID + NM * CH], x1_a[:, 0, 0:HID]
        loads = [(wmm, d["wmm"]), (wkt, d["wkt"]), (wmt[:, 0], d["wmt"]), (wtt[:, 0], d["wtt"]),
                 (pw_a, d["pw"][0:P]), (pw_b[0:HALF, 0], d["pw"][P:CH]), (pw_b[HALF:P, 1], d["pw"][P:CH]),
                 (raw1, d["f1"][0:P]), (raw1t[0:HALF], d["f1"][P:CH]), (raw1t[HALF:P], d["f1"][P:CH]),
                 (raw2.rearrange("p (j c) -> p j c", j=NM), d["f2"]), (vec[:, :, 0:1], d["vec"][:, 0:P].rearrange("v (p o) -> p v o", o=1)),
                 (vec[0:HALF, :, 1:2], d["vec"][:, P:CH].rearrange("v (p o) -> p v o", o=1)), (b1, d["b1"]),
                 (sgn, d["sgn"]), (idn, d["ident"])]

        @block.sync
        def _(sp):
            for dst, src in loads:
                with nc.allow_non_contiguous_dma(reason="a few hundred numbers, once"):
                    sp.dma_start(dst if isinstance(dst, bass.AP) else dst[:], src).then_inc(wloaded, 16)

            def emit(n, par):
                if not on("H", n):
                    return
                if not more("H", n):
                    sp.wait_ge(wready, 4)
                else:
                    fn_value, x1_value = held(sp, prior(fn_in, n)), held(sp, prior(x1_set, n))
                    sp.wait_ge(wloaded, 16 * len(loads))
                    sp.wait_ge(fn_in.sem, fn_value)
                    sp.wait_ge(x1_set.sem, x1_value)
                src = d["fz"][bass.ds(n.linear(NCH, NCH), NCH)]
                sp.dma_start(fn_a[:].rearrange("p (c t) -> p c t", c=NCH), src[:, 0:P, :].rearrange("c p t -> p c t")).then_inc(fn_in.sem, 16)
                sp.dma_start(fn_b[:].rearrange("p (c t) -> p c t", c=NCH), src[:, P:CH, :].rearrange("c p t -> p c t")).then_inc(fn_in.sem, 16)
                if on("E", n) and more("E", n):
                    xp_value, x2_value = held(sp, prior(xp_in, n)), held(sp, prior(x2_set, n))
                    sp.wait_ge(wloaded, 16 * len(loads))
                    sp.wait_ge(xp_in.sem, xp_value)
                    sp.wait_ge(x2_set.sem, x2_value)
                sp.dma_start(x1_a[:, 1 - par, :], d["xperm"][n.linear(1, 1), 0:P, :]).then_inc(xp_in.sem, 16)
                sp.dma_start(x1_b[:, 1 - par, :], d["xperm"][n.linear(1, 1), P:CH, :]).then_inc(xp_in.sem, 16)

            images(sp, emit)

        @block.gpsimd
        def _(pool):
            for i, (dst, value) in enumerate([(half[:], -0.5), (fmv[:], 1.0), (pw_b[HALF:P, 0], 0.0), (pw_b[0:HALF, 1], 0.0)]):
                nc.gpsimd.memset(dst, value).then_inc(wset, 1)
                pool.wait_ge(wset, i + 1)

            def rstd(n, q):
                r = order[q] % 2
                tmv_set_value = held(pool, tmv_set.after(n, q))
                pool.wait_ge(wloaded, 16 * len(loads))
                pool.wait_ge(tmv_set.sem, tmv_set_value)
                nc.gpsimd.tensor_scalar(trs[:, r, 0], tmv[:, r, :, 1], EPS, 1.0, ALU.add, ALU.mult).then_inc(tve.sem, 1)
                pool.wait_ge(tve.sem, tve.after(n, q))
                nc.gpsimd.tensor_tensor(trs[:, r, 1], trs[:, r, 0], half[0:BL], ALU.pow).then_inc(trs_set.sem, 1)

            def store(n, g):
                pool.wait_ge(o_set.sem, o_set.after(n, f"{g}b"))
                c = o_out[g % 2]
                for dst, lo, hi in ((o_a, 0, P), (o_b, P, CH)):
                    pool.dma_start(d["out"][n.linear(1, 0), lo:hi, bass.ts(g, GT)], dst[:, g % 2, :]).then_inc(c.sem, 16)

            def emit(n, par):
                if on("H", n):
                    if more("H", n):
                        pool.wait_ge(spread.sem, prior(spread, n))
                    fmv_value = held(pool, fmv_set.after(n, "b"))
                    pool.wait_ge(wloaded, 16 * len(loads))
                    pool.wait_ge(fmv_set.sem, fmv_value)
                    nc.gpsimd.tensor_scalar(frs[:, 0], fmv[:, :, 1], EPS, 1.0, ALU.add, ALU.mult).then_inc(fve.sem, 1)
                    pool.wait_ge(fve.sem, fve.after(n, "x"))
                    nc.gpsimd.tensor_tensor(frs[:, 1], frs[:, 0], half[:, 0:2], ALU.pow).then_inc(frs_set.sem, 1)
                    pool.wait_ge(frs_set.sem, frs_set.after(n, "x"))
                    nc.gpsimd.tensor_tensor(frs[:, 2], frs[:, 1], fmv[:, :, 0], ALU.mult).then_inc(fnm.sem, 1)
                    fnm_value = held(pool, fnm.after(n, "x"))
                    pool.wait_ge(wloaded, 16 * len(loads))
                    pool.wait_ge(fnm.sem, fnm_value)
                    nc.gpsimd.tensor_scalar(frs[:, 3], frs[:, 2], -1.0, 1.0, ALU.mult, ALU.mult).then_inc(fnb.sem, 1)
                for g in range(NG + 1):
                    if on("E", n) and g >= 1:
                        rstd(n, f"M{g - 1}")
                    if on("H", n):
                        for q in turns(g):
                            rstd(n, f"H{q}")
                    if on("E", n) and g >= 1:
                        store(n, g - 1)

            images(pool, emit)
            for c in o_out:
                pool.wait_ge(c.sem, 32 * NG // 2 * nimg)

        @block.tensor
        def _(pe):
            pe.wait_ge(wloaded, 16 * len(loads))
            pe.wait_ge(wset, 4)
            pe.wait_ge(wready, 4)

            def use(n, name):
                earlier = before_it(n, name, uses, NBANK)
                if earlier is not None:
                    step, user = earlier
                    c, event = reader(user)
                    value = c.after(step, event)
                    if name[:4] in ("turn", "back") and name[-1] == "b":
                        value = held(pe, value)
                        pe.wait_ge(wloaded, 16 * len(loads))
                    pe.wait_ge(c.sem, value)
                return fill[:, bank_of[name], :]

            def turn(n, q, src_a, src_b):
                o = use(n, f"turn{q}a")
                for j in range(NB):
                    last = nc.tensor.transpose(o[0:BL, bass.ts(j, P)], src_a[:, bass.ts(j, BL)], idn[:])
                last.then_inc(filled.sem, 1)
                o = use(n, f"turn{q}b")
                for j in range(NB):
                    last = nc.tensor.transpose(o[0:BL, bass.ts(j, HALF)], src_b[:, bass.ts(j, BL)], idn[0:HALF, 0:HALF])
                last.then_inc(filled.sem, 1)

            def back(n, q):
                pe.wait_ge(normed.sem, normed.after(n, f"{q}.{NB - 1}"))
                r = order[q] % TURN
                o = use(n, f"back{q}a")
                for j in range(NB):
                    last = nc.tensor.transpose(o[:, bass.ts(j, BL)], xt[:, r, j, 0:P], idn[0:BL, 0:BL])
                last.then_inc(filled.sem, 1)
                o = use(n, f"back{q}b")
                for j in range(NB):
                    last = nc.tensor.transpose(o[0:HALF, bass.ts(j, BL)], xt[:, r, j, P:CH], idn[0:BL, 0:BL])
                last.then_inc(filled.sem, 1)

            def window(n, g, t, par):
                if g:
                    pe.wait_ge(ypre_set.sem, ypre_set.after(n, f"{g - 1}.{t}"))
                elif more("E", n):
                    pe.wait_ge(ypre_set.sem, prior(ypre_set, n))
                plus, minus = [], []
                k0, k1 = 2 * g, 2 * g + 1
                for i in range(NK):
                    k = k1 if t == 1 else k0
                    w = wmm[:, i ^ k, :] if t < 2 else wmt[:, (1 - sign[i][k0] * sign[i][k1]) // 2, i ^ k0, :]
                    (plus if sign[i][k] > 0 else minus).append((w, xm[:, par, i, :]))
                for p in pairs:
                    k = k1 if t == 1 else k0
                    a, b = sign[2 * p][k], sign[2 * p + 1][k]
                    if t < 2:
                        w = wkt[:, (2 * p) ^ k, :]
                    else:
                        w = wtt[:, tails.index((a * sign[2 * p][k1], b * sign[2 * p + 1][k1])), ((2 * p) ^ k0) // 2, :]
                    (plus if a > 0 else minus).append((w, (tpp if a * b > 0 else tpm)[:, par, p, :]))
                for part, terms in enumerate([plus, minus]):
                    for e, (w, x) in enumerate(terms):
                        last = nc.tensor.matmul(wps[:, t, part * WT:(part + 1) * WT], w, x, start=(e == 0), stop=(e == len(terms) - 1))
                last.then_inc(wdone.sem, 1)

            def proj(n, g):
                pe.wait_ge(ym_set.sem, ym_set.after(n, f"{g}"))
                for h, lo, m in (("a", 0, P), ("b", P, HALF)):
                    o = use(n, f"projM{g}{h}")
                    nc.tensor.matmul(o[0:m, 0:GT], pw_a[:, lo:lo + m], ym[:, 0:2, :].rearrange("p a w -> p (a w)"), start=True, stop=False)
                    nc.tensor.matmul(o[0:m, 0:WT], pw_b[:, 0, lo:lo + m], ym[:, 2, :], start=False, stop=False)
                    nc.tensor.matmul(o[0:m, WT:GT], pw_b[:, 1, lo:lo + m], ym[:, 2, :], start=False, stop=True).then_inc(filled.sem, 1)

            def emit(n, par):
                H, E = on("H", n), on("E", n)
                if E:
                    pe.wait_ge(xm_set.sem, prior(xm_set, n))
                    pe.wait_ge(tpm_set.sem, prior(tpm_set, n))
                for g in range(NG + 1):
                    m = g - 1
                    if E and m >= 0:
                        proj(n, m)
                    if H:
                        for q in turns(g - 1):
                            back(n, f"H{q}")
                    if E and g < NG:
                        window(n, g, 0, par)
                    if E and m >= 0:
                        pe.wait_ge(x2_set.sem, x2_set.after(n, f"{m}b"))
                        turn(n, f"M{m}", x2_a[:, m % 2, :], x2_b[:, m % 2, :])
                    if E and g < NG:
                        window(n, g, 1, par)
                    if E and m >= 0:
                        back(n, f"M{m}")
                    if E and g < NG:
                        window(n, g, 2, par)
                    if H:
                        for q in turns(g):
                            pe.wait_ge(x1_set.sem, x1_set.after(n, f"{q}b"))
                            turn(n, f"H{q}", x1_a[:, 1 - par, bass.ts(q, GT)], x1_b[:, 1 - par, bass.ts(q, GT)])
                    if E and m >= 0:
                        pe.wait_ge(xs_set.sem, xs_set.after(n, f"{m}b"))
                        for j in range(NM):
                            o = use(n, f"fcoM{m}{j}")[:, 0:GT]
                            w = bass.ts(j, P)
                            nc.tensor.matmul(o, f1w[:, 0, w], xs[:, 0, :], start=True, stop=False)
                            nc.tensor.matmul(o, f1w[:, 1, w], xs[:, 0, :], start=False, stop=False)
                            nc.tensor.matmul(o, f1w[:, 0, w], xs[:, 1, :], start=False, stop=False)
                            nc.tensor.matmul(o, f1t[:, w], xt2[:], start=False, stop=False)
                            nc.tensor.matmul(o, f1l[:, w], xt2[0:HALF], start=False, stop=True).then_inc(filled.sem, 1)
                        for h, lo in (("a", 0), ("b", P)):
                            o = use(n, f"fctM{m}{h}")[:, 0:GT]
                            for j in range(NM):
                                pe.wait_ge(hs_set.sem, hs_set.after(n, f"{m}{j}"))
                                w = bass.ds(j * CH + lo, P)
                                nc.tensor.matmul(o, f2w[:, 0, w], hs[:, 0, j, :], start=(j == 0), stop=False)
                                nc.tensor.matmul(o, f2w[:, 1, w], hs[:, 0, j, :], start=False, stop=False)
                                last = nc.tensor.matmul(o, f2w[:, 0, w], hs[:, 1, j, :], start=False, stop=(j == NM - 1))
                            last.then_inc(filled.sem, 1)

            images(pe, emit)

        @block.scalar
        def _(act):
            act.wait_ge(wloaded, 16 * len(loads))

            def filled_by(n, name):
                act.wait_ge(filled.sem, filled.after(n, name))
                return fill[:, bank_of[name], :]

            def take_turn(n, q):
                r = order[q] % TURN
                o = filled_by(n, f"turn{q}a")
                earlier = before_it(n, q, groups, TURN)
                if earlier is not None:
                    act.wait_ge(filled.sem, filled.after(earlier[0], f"back{earlier[1]}b"))
                nc.scalar.activation(xt[:, r, :, 0:P], o[0:BL, 0:NB * P].rearrange("p (j c) -> p j c", j=NB), ACT.Copy).then_inc(turned.sem, 1)
                o = filled_by(n, f"turn{q}b")
                nc.scalar.activation(xt[:, r, :, P:CH], o[0:BL, 0:NB * HALF].rearrange("p (j c) -> p j c", j=NB), ACT.Copy).then_inc(turned.sem, 1)

            def negative(n, g, t):
                act.wait_ge(wdone.sem, wdone.after(n, f"{g}.{t}"))
                if t == 0:
                    if g:
                        act.wait_ge(ypre_set.sem, ypre_set.after(n, f"{g - 1}.2"))
                    elif more("E", n):
                        act.wait_ge(ypre_set.sem, prior(ypre_set, n))
                nc.scalar.activation(neg[:, t, :], wps[:, t, WT:2 * WT], ACT.Copy).then_inc(neg_set.sem, 1)

            def finish_layer0(n):
                act.wait_ge(frs_set.sem, frs_set.after(n, "x"))
                act.wait_ge(fnb.sem, fnb.after(n, "x"))
                for r in range(WIN):
                    for h, (buf, rows) in enumerate([(fn_a, P), (fn_b, HALF)]):
                        rowsof = buf[:].rearrange("p (wh r x) -> p r wh x", r=WIN, wh=NW)[:, r]
                        nc.scalar.activation(rowsof, rowsof, ACT.Identity, bias=frs[0:rows, 3, h:h + 1],
                                             scale=frs[0:rows, 1, h:h + 1]).then_inc(spread.sem, 1)

            def take_windows(n, g, nxt):
                o = filled_by(n, f"backH{g}a")
                if g == 0 and on("E", n) and more("E", n):
                    act.wait_ge(wdone.sem, prior(wdone, n))
                nc.scalar.activation(xm[:, nxt, 2 * g:2 * g + 2, :].rearrange("p a w -> p (a w)"), o[:, 0:GT], ACT.Identity,
                                     bias=vec[:, 1, 0:1], scale=vec[:, 0, 0:1]).then_inc(xm_set.sem, 1)
                o = filled_by(n, f"backH{g}b")
                for h in range(2):
                    nc.scalar.activation(tpp[h * HALF:(h + 1) * HALF, nxt, g, :], o[0:HALF, h * WT:(h + 1) * WT], ACT.Identity,
                                         bias=vec[0:HALF, 1, 1:2], scale=vec[0:HALF, 0, 1:2]).then_inc(tpp_set.sem, 1)

            def emit(n, par):
                H, E = on("H", n), on("E", n)
                for g in range(NG + 1):
                    m = g - 1
                    if H:
                        for q in turns(g - 1):
                            take_windows(n, q, 1 - par)
                    if E and g < NG:
                        negative(n, g, 0)
                    if E and m >= 0:
                        take_turn(n, f"M{m}")
                    if E and g < NG:
                        negative(n, g, 1)
                    if E and m >= 0:
                        for c, (h, high, dst, rows) in enumerate([("a", xs[:, 0, :], xa_a, P), ("b", xt2[0:HALF], xa_b, HALF)]):
                            o = filled_by(n, f"backM{m}{h}")[0:rows, 0:GT]
                            g2, b2 = vec[0:rows, 3, c:c + 1], vec[0:rows, 4, c:c + 1]
                            nc.scalar.activation(high, o, ACT.Identity, bias=b2, scale=g2)
                            nc.scalar.activation(dst[:], o, ACT.Identity, bias=b2, scale=g2).then_inc(xa_set.sem, 1)
                    if E and g < NG:
                        negative(n, g, 2)
                    if H:
                        for q in turns(g):
                            take_turn(n, f"H{q}")
                    if E and m >= 0:
                        for j in range(NM):
                            o = filled_by(n, f"fcoM{m}{j}")
                            if j == 0:
                                if m:
                                    act.wait_ge(filled.sem, filled.after(n, f"fctM{m - 1}b"))
                                elif more("E", n):
                                    act.wait_ge(filled.sem, prior(filled, n))
                            nc.scalar.activation(hs[:, 0, j, :], o[:, 0:GT], ACT.Gelu, bias=b1[:, j:j + 1])
                            if m or j >= 2:
                                act.wait_ge(hs_set.sem, hs_set.before(n, f"{m}{j}") - 1)
                            elif more("E", n):
                                act.wait_ge(hs_set.sem, hs_set.after(n.shift(-1), f"{NG - 1}{NM - 2 + j}"))
                            nc.scalar.activation(h1[:, j % 2, :], o[:, 0:GT], ACT.Gelu, bias=b1[:, j:j + 1]).then_inc(h1_set.sem, 1)
                    if E and g < NG:
                        act.wait_ge(ypre_set.sem, ypre_set.after(n, f"{g}.2"))
                        nc.scalar.activation(ym[:], ypre[:], ACT.Gelu).then_inc(ym_set.sem, 1)
                    if H and g == 0:
                        finish_layer0(n)

            images(act, emit)

        @block.vector
        def _(dve):
            dve.wait_ge(wloaded, 16 * len(loads))
            dve.wait_ge(wset, 4)
            nc.vector.tensor_copy(wmt[:, 1, :, 0:HALF], wmt[:, 0, :, 0:HALF])
            nc.vector.tensor_scalar(wmt[:, 1, :, HALF:P], wmt[:, 0, :, HALF:P], -1.0, None, ALU.mult).then_inc(wready, 1)
            for v in range(1, len(tails)):
                nc.vector.tensor_copy(wtt[:, v, :, 0:HALF], wtt[:, 0, :, 0:HALF])
            for v in reversed(range(len(tails))):
                col = [(1, 1), (1, -1), (-1, 1), (-1, -1)].index(tails[v])
                if v == 0:
                    last.then_inc(wready, 1)
                    dve.wait_ge(wready, 2)
                last = nc.vector.tensor_scalar(wtt[:, v, :, HALF:P], wtt[:, 0, :, HALF:P], sgn[:, col:col + 1], None, ALU.mult)
            last.then_inc(wready, 1)
            nc.vector.tensor_copy(f1w[:, 0, :], raw1)
            nc.vector.tensor_copy(f1t[:], raw1t)
            nc.vector.tensor_copy(f2w[:, 0, 0:NM * CH], raw2)
            nc.vector.tensor_copy(f2w[:, 0, NM * CH:], raw2[:, 0:HALF])
            nc.vector.tensor_copy(f2w[:, 1, NM * CH:], raw2[:, 0:HALF]).then_inc(wcut, 1)
            dve.wait_ge(wcut, 1)
            nc.vector.tensor_tensor(f1w[:, 1, :], raw1, f1w[:, 0, :], ALU.subtract)
            nc.vector.tensor_tensor(f1l[:], raw1t[0:HALF], f1t[0:HALF], ALU.subtract)
            nc.vector.tensor_tensor(f2w[:, 1, 0:NM * CH], raw2, f2w[:, 0, 0:NM * CH], ALU.subtract).then_inc(wready, 1)

            def statistics(n, q):
                r, r2 = order[q] % TURN, order[q] % 2
                dve.wait_ge(turned.sem, turned.after(n, f"{q}b"))
                if q != "H0" or more("H", n):
                    dve.wait_ge(normed.sem, normed.before(n, f"{q}.0"))
                for j in range(NB):
                    nc.vector.bn_stats(tst[:, j, :], xt[:, r, j, :]).then_inc(tst_set.sem, 1)
                tst_set_value = held(dve, tst_set.after(n, f"{q}.{NB - 1}"))
                dve.wait_ge(wloaded, 16 * len(loads))
                dve.wait_ge(tst_set.sem, tst_set_value)
                for j in range(NB):
                    last = nc.vector.bn_aggr(tmv[:, r2, j, :], tst[:, j, :])
                last.then_inc(tmv_set.sem, 1)

            def normalise(n, q):
                r, r2 = order[q] % TURN, order[q] % 2
                dve.wait_ge(trs_set.sem, trs_set.after(n, q))
                for j in range(NB):
                    nc.vector.tensor_scalar(xt[:, r, j, :], xt[:, r, j, :], tmv[:, r2, j, 0:1], trs[:, r2, 1, j:j + 1],
                                            ALU.subtract, ALU.mult).then_inc(normed.sem, 1)

            def subtract(n, g, t):
                dve.wait_ge(neg_set.sem, neg_set.after(n, f"{g}.{t}"))
                if t == 0:
                    if g:
                        dve.wait_ge(ym_set.sem, ym_set.after(n, f"{g - 1}"))
                    elif more("E", n):
                        dve.wait_ge(ym_set.sem, prior(ym_set, n))
                nc.vector.tensor_tensor(ypre[:, t, :], wps[:, t, 0:WT], neg[:, t, :], ALU.subtract).then_inc(ypre_set.sem, 1)

            def layer0_statistics(n):
                dve.wait_ge(fn_in.sem, fn_in.after(n, "x"))
                if more("H", n):
                    dve.wait_ge(fnm.sem, prior(fnm, n))
                for h, (src, rows) in enumerate([(fn_a, P), (fn_b, HALF)]):
                    for c in range(NCH):
                        nc.vector.bn_stats(fst[0:rows, h, c, :], src[:, bass.ts(c, TC)]).then_inc(fst_set.sem, 1)
                    fst_set_value = held(dve, fst_set.after(n, f"{'ab'[h]}{NCH - 1}"))
                    dve.wait_ge(wloaded, 16 * len(loads))
                    dve.wait_ge(fst_set.sem, fst_set_value)
                    nc.vector.bn_aggr(fmv[0:rows, h, :], fst[0:rows, h, :, :].rearrange("p c s -> p (c s)")).then_inc(fmv_set.sem, 1)

            def add_input(n, q, nxt):
                r, c0 = 2 * q // WIN, 2 * q % WIN
                if q == 0:
                    dve.wait_ge(xp_in.sem, xp_in.after(n, "x"))
                for h, dst, src in (("a", x1_a, fn_a), ("b", x1_b, fn_b)):
                    dve.wait_ge(spread.sem, spread.after(n, f"{h}{r}"))
                    o = dst[:, nxt, bass.ts(q, GT)].rearrange("p (c wh ww) -> p c wh ww", c=2, wh=NW)
                    i = src[:].rearrange("p (wh r ww c) -> p r c wh ww", r=WIN, ww=NW, c=WIN)[:, r, c0:c0 + 2]
                    nc.vector.tensor_tensor(o, o, i, ALU.add).then_inc(x1_set.sem, 1)

            def emit(n, par):
                H, E = on("H", n), on("E", n)
                if H:
                    layer0_statistics(n)
                for g in range(NG + 1):
                    m = g - 1
                    if E and m >= 0:
                        for c, (h, dst, x1, rows) in enumerate([("a", x2_a, x1_a, P), ("b", x2_b, x1_b, HALF)]):
                            use = f"projM{m}{h}"
                            dve.wait_ge(filled.sem, filled.after(n, use))
                            if m >= 2:
                                dve.wait_ge(turned.sem, turned.after(n, f"M{m - 2}b"))
                                dve.wait_ge(o_set.sem, o_set.after(n, f"{m - 2}b"))
                            elif more("E", n):
                                dve.wait_ge(o_set.sem, prior(o_set, n))
                            nc.vector.scalar_tensor_tensor(dst[:, m % 2, :], fill[0:rows, bank_of[use], 0:GT], vec[0:rows, 2, c:c + 1],
                                                           x1[:, par, bass.ts(m, GT)], ALU.add, ALU.add).then_inc(x2_set.sem, 1)
                    if E and g < NG:
                        subtract(n, g, 0)
                    if E and m >= 0:
                        statistics(n, f"M{m}")
                        normalise(n, f"M{m}")
                    if E and g < NG:
                        subtract(n, g, 1)
                    if E and m >= 0:
                        dve.wait_ge(xa_set.sem, xa_set.after(n, f"{m}a"))
                        nc.vector.tensor_tensor(xs[:, 1, :], xa_a[:], xs[:, 0, :], ALU.subtract).then_inc(xs_set.sem, 1)
                        dve.wait_ge(xa_set.sem, xa_set.after(n, f"{m}b"))
                        nc.vector.tensor_tensor(xt2[HALF:P], xa_b[:], xt2[0:HALF], ALU.subtract).then_inc(xs_set.sem, 1)
                    if H:
                        for q in turns(g):
                            add_input(n, q, 1 - par)
                    if E and g < NG:
                        subtract(n, g, 2)
                    if H:
                        for q in turns(g):
                            statistics(n, f"H{q}")
                            if q + 1 in turns(g):
                                normalise(n, f"H{q}")
                    if H and g == NG:
                        dve.wait_ge(tpp_set.sem, tpp_set.after(n, f"{NG - 1}1"))
                        nc.vector.tensor_scalar(tpm[:, 1 - par].rearrange("p a w -> p (a w)"), tpp[:, 1 - par].rearrange("p a w -> p (a w)"),
                                                sgn[:, 1:2], None, ALU.mult).then_inc(tpm_set.sem, 1)
                    if E and m >= 0:
                        for j in range(NM):
                            dve.wait_ge(h1_set.sem, h1_set.after(n, f"{m}{j}"))
                            nc.vector.tensor_tensor(hs[:, 1, j, :], h1[:, j % 2, :], hs[:, 0, j, :], ALU.subtract).then_inc(hs_set.sem, 1)
                    if H and turns(g):
                        normalise(n, f"H{turns(g)[-1]}")
                    if E and m >= 0:
                        for h, dst, x2, rows in (("a", o_a, x2_a, P), ("b", o_b, x2_b, HALF)):
                            use = f"fctM{m}{h}"
                            dve.wait_ge(filled.sem, filled.after(n, use))
                            c = o_out[m % 2]
                            if m >= 2:
                                dve.wait_ge(c.sem, c.after(n, f"{m - 2}"))
                            elif more("E", n):
                                dve.wait_ge(c.sem, prior(c, n))
                            col = "ab".index(h)
                            nc.vector.scalar_tensor_tensor(dst[:, m % 2, :], fill[0:rows, bank_of[use], 0:GT], vec[0:rows, 5, col:col + 1],
                                                           x2[:, m % 2, :], ALU.add, ALU.add).then_inc(o_set.sem, 1)

            images(dve, emit)


def layers(nc, d):
    d = dict(d)
    d["fz"] = nc.dram_tensor("fused_dram", (IMG * NCH, CH, TC), F32, kind="Internal").ap()
    layer0(nc, d, IMG)
    layer1(nc, d, IMG)


def layouts(a):
    def tiles(v):
        return v.reshape((ND, P) + v.shape[1:]).swapaxes(0, 1)

    x = a["x"]
    padded = np.zeros((IMG, CH, SIDE + 2, SIDE), x.dtype)
    padded[:, :, 1:SIDE + 1] = x
    keep = np.ones((P, IMG * NCH, ND), np.float32)
    keep[:, NCH - 1::NCH] = 0
    xw = a["L0_conv_x_proj_w"]
    w = a["L1_conv_w_sed"]
    other = np.arange(NK) ^ 1
    mm, mt, tm, tt = w[:, :P, :P], w[:, :P, P:], w[:, P:, :P], w[:, P:, P:]
    even = np.arange(0, NK, 2)
    sgn = np.ones((P, 4), np.float32)
    sgn[HALF:, 1] = sgn[:HALF, 2] = sgn[:, 3] = -1
    return dict(
        xch=np.stack([padded[:, :, ROWS * c:ROWS * (c + 1) + 2].reshape(IMG, CH, TH) for c in range(NCH)], 1).reshape(-1, CH, TH),
        win=a["L0_conv_in_proj_w"].T,
        cw=tiles(a["L0_conv_conv_w"].reshape(DI, 9)),
        xpw=tiles(np.concatenate([xw[RANK:], xw[:RANK]]).T),
        dtw=a["L0_conv_dt_proj_w"].T,
        opw=a["L0_conv_out_proj_w"],
        fuw=a["L0_conv_fuse_w"][:, :, 0, 0].T,
        vecs=np.stack([tiles(a["L0_conv_" + k]) for k in ("conv_b", "dt_proj_b", "D_param", "ln_g", "ln_b")], 1),
        alog=tiles(a["L0_conv_A_log"]),
        ident=np.eye(P, dtype=np.float32),
        pick=np.tile(np.eye(2 * ST, dtype=np.float32), (2, 1)),
        keep=keep.reshape(P, -1),
        fub=a["L0_conv_fuse_b"].reshape(CH, 1),
        xperm=x.reshape(IMG, CH, NW, WIN, NW, WIN).transpose(0, 1, 3, 5, 2, 4).reshape(IMG, CH, TOK),
        wmm=mm.transpose(1, 0, 2),
        wkt=np.concatenate([tm, tm[other]], 1).transpose(1, 0, 2),
        wmt=np.concatenate([mt, mt[other]], 2).transpose(1, 0, 2),
        wtt=np.concatenate([np.concatenate([tt[even], tt[even + 1]], 2), np.concatenate([tt[even + 1], tt[even]], 2)], 1).transpose(1, 0, 2),
        pw=a["L1_conv_proj_w"], f1=a["L1_conv_fc1_w"],
        f2=a["L1_conv_fc2_w"].reshape(NM, P, CH).transpose(1, 0, 2),
        vec=np.stack([a["L1_conv_" + k] for k in ("norm1_g", "norm1_b", "proj_b", "norm2_g", "norm2_b", "fc2_b")]),
        b1=a["L1_conv_fc1_b"].reshape(NM, P).T,
        sgn=sgn)


def kernel(**inputs):
    import concourse.bacc as bacc
    from concourse.bass_utils import run_bass_kernel_spmd

    nc = bacc.Bacc("TRN2", target_bir_lowering=False, num_devices=1)
    arrays, d = {}, {}
    for name, a in layouts({k: np.asarray(v) for k, v in inputs.items()}).items():
        arrays[f"{name}_dram"] = np.ascontiguousarray(a)
        d[name] = nc.dram_tensor(f"{name}_dram", a.shape, F32, kind="ExternalInput").ap()
    d["out"] = nc.dram_tensor("out_dram", (IMG, CH, TOK), F32, kind="ExternalOutput").ap()
    layers(nc, d)
    got = run_bass_kernel_spmd(nc, [arrays], core_ids=[0]).results[0]["out_dram"]
    return got.reshape(IMG, CH, WIN, WIN, NW, NW).transpose(0, 1, 4, 2, 5, 3).reshape(IMG, CH, SIDE, SIDE)
```

```python
from contextlib import ExitStack

import numpy as np

import concourse.bass as bass
from concourse import mybir
from concourse.alu_op_type import AluOpType as ALU

F32 = mybir.dt.float32
F32R = mybir.dt.float32r
ACT = mybir.ActivationFunctionType
AX = mybir.AxisListType

P = 128
CH, HALF = 192, 64
IMG, SIDE = 8, 48
DI, ST, RANK = 384, 16, 12
ND = DI // P
ROWS = 8
TC = ROWS * SIDE
TH = (ROWS + 2) * SIDE
NCH = SIDE // ROWS
BANK = 512
LOW = 64
RING = 4
AHEAD = 2
BY_PE = (2, 3, 4, 5, 6, 7, 8, 9, 10)
BY_DVE = tuple(s for s in range(ST) if s not in BY_PE)
EPS = 1e-5
TOK = SIDE * SIDE
WIN = 4
NW = SIDE // WIN
WT = NW * NW
NK = WIN * WIN
GT = 2 * WT
NG = NK // 2
BL, NB = 96, 3
HID = 4 * CH
NM = HID // P
TURN = 4



class At:

    def __init__(self, off, reg=None, mult=0):
        self.off, self.reg, self.mult = off, reg, mult

    def linear(self, k, c):
        c = k * self.off + c
        return c if self.reg is None else self.reg * (self.mult * k) + c

    def later(self):
        return self.reg is not None or self.off > 0

    def shift(self, d):
        return At(self.off + d, self.reg, self.mult)


class Count:

    def __init__(self, sem, when, events):
        self.sem, self.when, self.events = sem, when, events

    def _at(self, step, name, after):
        total, const = 0, 0
        inside, found = 0, False
        for ev, kind, w in self.events:
            first, last = self.when[kind]
            if step.reg is None:
                const += w * min(max(step.off - first, 0), last - first + 1)
                on = first <= step.off <= last
            else:
                total += w
                const -= w * first
                on = True
            if found:
                continue
            if ev == name:
                found = True
                inside += w if after and on else 0
            else:
                inside += w if on else 0
        assert found, name
        return const + inside if step.reg is None else step.linear(total, const + inside)

    def after(self, step, name):
        return self._at(step, name, True)

    def before(self, step, name):
        return self._at(step, name, False)


def held(eng, value):
    return value if isinstance(value, int) else eng.to_reg(value)


def layer0(nc, d, nimg):
    NS = nimg * NCH
    when = {"X": (-2, NS - 3), "A": (-1, NS - 2), "S": (0, NS - 1), "O": (1, NS)}
    ctx = ExitStack()
    with ctx:
        def sb(name, shape, dt=F32):
            return ctx.enter_context(nc.sbuf_tensor(name, shape, dt))

        def ps(name, shape):
            return ctx.enter_context(nc.psum_tensor(name, shape, F32))

        def sem(name):
            return ctx.enter_context(nc.semaphore(name))

        def count(name, events):
            return Count(sem(name), when, events)

        win_a, win_b = sb("win_a", [P, 2 * DI]), sb("win_b", [HALF, 2 * DI])
        cw, diag = sb("cw", [P, ND, 9]), sb("diag", [P, ND, 9, P])
        xpw = sb("xpw", [P, ND, LOW])
        dtw, dtw_r = sb("dtw", [P, DI]), sb("dtw_r", [P, DI], F32R)
        parts = sb("parts", [P, 2])
        opw_a, opw_b = sb("opw_a", [P, DI]), sb("opw_b", [HALF, DI])
        fuw_a, fuw_b = sb("fuw_a", [P, CH]), sb("fuw_b", [HALF, CH])
        wout = sb("wout", [P, ND, CH])
        vecs = sb("vecs", [P, 5, ND])
        fub = sb("fub", [P, 2])
        alog = sb("alog", [P, ND, ST])
        aneg = sb("aneg", [P, ND, ST])
        ident = sb("ident", [P, P])
        pick, pick_r = sb("pick", [P, 2 * ST]), sb("pick_r", [P, 2 * ST], F32R)
        keep = sb("keep", [P, NS * ND])
        mhalf = sb("mhalf", [P, ND])
        xc_a, xc_b = sb("xc_a", [P, TH]), sb("xc_b", [HALF, TH])
        xz_a, xz_b = sb("xz_a", [P, TC]), sb("xz_b", [HALF, TC])
        xin = sb("xin", [P, ND, ROWS + 2, SIDE + 2])
        pre, u = sb("pre", [P, ND, TC]), sb("u", [P, ND, TC])
        soft = sb("soft", [P, ND, TC])
        delta = sb("delta", [P, 2, ND, TC])
        du = sb("du", [P, 2, ND, TC])
        low = sb("low", [P, 2, TC], F32R)
        brow = sb("brow", [P, RING, TC])
        drive = sb("drive", [P, RING, ND, TC])
        hst = sb("hst", [P, RING, ND, TC])
        carry = sb("carry", [P, ST, ND])
        decay = sb("decay", [P, RING, ND, TC])
        prod = sb("prod", [P, RING, ND, TC])
        ud, total = sb("ud", [P, ND, TC]), sb("total", [P, ND, TC])
        ysum = sb("ysum", [P, ND, TC])
        zpre, sz = sb("zpre", [P, ND, TC]), sb("sz", [P, ND, TC])
        yt = sb("yt", [P, ND, DI])
        st6, mv = sb("st6", [P, ND, 6]), sb("mv", [P, ND, 2])
        rstd = sb("rstd", [P, 2, ND])
        og = sb("og", [P, ND, TC])
        fz = sb("fz", [P, 2, TC])
        gather = ps("gather", [P, ND, BANK])
        bps = ps("bps", [P, BANK])
        cps = ps("cps", [P, 2, BANK])
        fill = ps("fill", [P, 2, BANK])

        loaded, prepared, merged, mergedone = sem("loaded"), sem("prepared"), sem("merged"), sem("mergedone")
        alogged, cut = sem("alogged"), sem("cut")
        uses = [("conv1", "A", 0), ("yT0", "O", 1), ("yT1", "O", 1), ("conv2", "A", 0), ("yT2", "O", 1),
                ("xp", "A", 1), ("z0", "S", 0), ("dt0", "A", 0), ("dt1", "A", 1), ("dt2", "A", 0), ("xin0", "X", 1),
                ("back0", "O", 0), ("xin1", "X", 1), ("back1", "O", 0), ("back2", "O", 1), ("xin2", "X", 0),
                ("z1", "S", 1), ("z2", "S", 0), ("out0", "O", 1), ("out1", "O", 0), ("conv0", "X", 1)]
        bank_of = {name: bank for name, _, bank in uses}
        filled = count("filled", [(name, kind, 1) for name, kind, _ in uses])
        xc_in = count("xc_in", [("x", "X", 32)])
        xz_in = count("xz_in", [("x", "S", 32)])
        ahead = lambda k: [(f"{s}", "S", 1) for s in range(k, ST)] + [(f"{s}", "A", 1) for s in range(k)]
        b_spread, b_copied, driven = count("b_spread", ahead(5)), count("b_copied", ahead(4)), count("driven", ahead(3))
        c_spread = count("c_spread", [(f"{s}", "S", 1) for s in range(ST)])
        decayed = count("decayed", [(f"{s % ST}.{m}", "S" if s < ST else "A", 1) for s in range(AHEAD, ST + AHEAD) for m in range(ND)])
        scanned = count("scanned", [(f"{s}.{m}", "S", 1) for s in range(ST) for m in range(ND)])
        scaled = count("scaled", [(f"{s}", "S", 1) for s in range(ST)])
        gathered = count("gathered", [(f"{s}", "S", 1) for s in BY_PE])
        added = count("added", [(f"{s}", "S", 1) for s in BY_DVE])
        summed = count("summed", [(f"{m}", "S", 1) for m in range(ND)])
        carried = count("carried", [(f"{ST - 1}", "O", 1)] + [(f"{s}", "S", 1) for s in range(ST - 1)])
        xin_set = count("xin_set", [(f"{m}", "X", 1) for m in range(ND)])
        pre_set = count("pre_set", [(f"{m}", "A", 1) for m in range(ND)])
        u_set = count("u_set", [("u", "A", 1)])
        sz_set = count("sz_set", [("sz", "O", 1)])
        zpre_set = count("zpre_set", [(f"{m}", "S", 1) for m in range(ND)])
        low_high, low_low = count("lowhi", [("x", "A", 1)]), count("lowlo", [("x", "A", 1)])
        dt_set = count("dt_set", [(f"{m}", "A", 1) for m in range(ND)])
        abs_set = count("abs_set", [(f"{m}", "A", 1) for m in range(ND)])
        exp_set, ln_set = count("exp_set", [("x", "A", 1)]), count("ln_set", [("x", "A", 1)])
        delta_set, du_set, ud_set = count("delta_set", [("x", "A", 1)]), count("du_set", [("x", "A", 1)]), count("ud_set", [("x", "A", 1)])
        yt_set = count("yt_set", [(f"{j}", "O", 1) for j in range(ND)])
        stat_set = count("stat_set", [(f"{j}", "O", 1) for j in range(ND)])
        mv_set = count("mv_set", [("x", "O", 1)])
        veps_set, rstd_set = count("veps_set", [("x", "O", 1)]), count("rstd_set", [("x", "O", 1)])
        normed = count("normed", [(f"{j}", "O", 1) for j in range(ND)])
        affined = count("affined", [(f"{m}", "O", 1) for m in range(ND)])
        gated = count("gated", [("x", "O", 1)])
        fz_set = count("fz_set", [("0", "O", 1), ("1", "O", 1)])
        stored = count("stored", [("x", "O", 32)])
        NLOADS = 17

        def readers(name):
            what, i = name.rstrip("012"), name[-1]
            return {"yT": [(yt_set, i)], "xin": [(xin_set, i)], "conv": [(pre_set, i)], "xp": [(low_low, "x")],
                    "back": [(affined, i)], "dt": [(dt_set, i)], "out": [(fz_set, i)],
                    "z": [(zpre_set, i)]}[what]

        def before_it(n, name):
            names = [name for name, _, _ in uses]
            kinds = {name: kind for name, kind, _ in uses}
            for back in range(3):
                step = n.shift(-back)
                upto = names.index(name) if back == 0 else len(names)
                for other in reversed(names[:upto]):
                    if bank_of[other] == bank_of[name] and on(kinds[other], step):
                        return step, other
            return None

        def on(kind, n):
            return n.reg is not None or when[kind][0] <= n.off <= when[kind][1]

        def steps(eng, emit):
            for n in range(-2, 2):
                emit(At(n), n % 2)
            with eng.Fori(0, (NS - 4) // 2) as m:
                emit(At(2, m, 2), 0)
                emit(At(3, m, 2), 1)
            emit(At(NS - 2), NS % 2)
            emit(At(NS - 1), (NS - 1) % 2)
            emit(At(NS), NS % 2)

        block = ctx.enter_context(nc.Block())

        @block.sync
        def _(sp):
            for dst, src in [(win_a, d["win"][0:P]), (win_b, d["win"][P:CH]), (cw, d["cw"]), (xpw, d["xpw"]),
                             (dtw, d["dtw"]), (opw_a, d["opw"][0:P]), (opw_b, d["opw"][P:CH]),
                             (fuw_a, d["fuw"][0:P]), (fuw_b, d["fuw"][P:CH]), (vecs, d["vecs"]),
                             (alog, d["alog"]), (ident, d["ident"]), (pick, d["pick"]),
                             (keep, d["keep"]), (parts, d["parts"])]:
                sp.dma_start(dst[:], src).then_inc(loaded, 16)
            sp.dma_start(fub[:, 0:1], d["fub"][0:P]).then_inc(loaded, 16)
            sp.dma_start(fub[0:HALF, 1:2], d["fub"][P:CH]).then_inc(loaded, 16)

            def emit(n, par):
                if on("X", n):
                    if n.reg is not None or n.off > -2:
                        xc_in_value = held(sp, xc_in.after(n.shift(-1), "x"))
                        filled_value = held(sp, filled.after(n.shift(-1), "xin2"))
                        sp.wait_ge(loaded, 16 * NLOADS)
                        sp.wait_ge(xc_in.sem, xc_in_value)
                        sp.wait_ge(filled.sem, filled_value)
                    j = n.linear(1, 2)
                    sp.dma_start(xc_a[:], d["xch"][j, 0:P, :]).then_inc(xc_in.sem, 16)
                    sp.dma_start(xc_b[:], d["xch"][j, P:CH, :]).then_inc(xc_in.sem, 16)
                if on("S", n):
                    if n.reg is not None or n.off > 0:
                        xz_in_value = held(sp, xz_in.after(n.shift(-1), "x"))
                        filled_value = held(sp, filled.after(n.shift(-1), "z2"))
                        sp.wait_ge(loaded, 16 * NLOADS)
                        sp.wait_ge(xz_in.sem, xz_in_value)
                        sp.wait_ge(filled.sem, filled_value)
                    j = n.linear(1, 0)
                    sp.dma_start(xz_a[:], d["xch"][j, 0:P, SIDE:SIDE + TC]).then_inc(xz_in.sem, 16)
                    sp.dma_start(xz_b[:], d["xch"][j, P:CH, SIDE:SIDE + TC]).then_inc(xz_in.sem, 16)
                if on("O", n):
                    sp.wait_ge(fz_set.sem, fz_set.after(n, "1"))
                    j = n.linear(1, -1)
                    sp.dma_start(d["fz"][j, 0:P, :], fz[:, 0, :]).then_inc(stored.sem, 16)
                    sp.dma_start(d["fz"][j, P:CH, :], fz[0:HALF, 1, :]).then_inc(stored.sem, 16)

            steps(sp, emit)
            sp.wait_ge(stored.sem, stored.after(At(NS), "x"))

        @block.tensor
        def _(pe):
            pe.wait_ge(loaded, 16 * NLOADS)
            for m in range(ND):
                if m >= 2:
                    pe.wait_ge(mergedone, m - 1)
                o = fill[:, m % 2, 0:CH]
                nc.tensor.matmul(o, opw_a[:, bass.ts(m, P)], fuw_a[:], start=True, stop=False)
                nc.tensor.matmul(o, opw_b[:, bass.ts(m, P)], fuw_b[:], start=False, stop=True).then_inc(merged, 1)
            pe.wait_ge(mergedone, ND)
            pe.wait_ge(prepared, 3)

            def use(n, name):
                earlier = before_it(n, name)
                for c, event in readers(earlier[1]) if earlier else []:
                    pe.wait_ge(c.sem, c.after(earlier[0].shift(1) if earlier[1] == "conv0" else earlier[0], event))
                return fill[:, bank_of[name], :]

            def y_back(n, j):
                o = use(n, f"yT{j}")
                for m in range(ND):
                    last = nc.tensor.transpose(o[:, bass.ts(m, P)], ysum[:, m, bass.ts(j, P)], ident[:])
                last.then_inc(filled.sem, 1)

            def x_in(n, m):
                o = use(n, f"xin{m}")[:, 0:TH]
                nc.tensor.matmul(o, win_a[:, bass.ts(m, P)], xc_a[:], start=True, stop=False)
                nc.tensor.matmul(o, win_b[:, bass.ts(m, P)], xc_b[:], start=False, stop=True).then_inc(filled.sem, 1)

            def conv(n, m, first, end):
                o = use(n, f"conv{m}") if first == 0 else fill[:, bank_of[f"conv{m}"], :]
                if first == 0:
                    pe.wait_ge(xin_set.sem, xin_set.after(n if m == 0 else n.shift(-1), f"{m}"))
                for tap in range(first, end):
                    dy, dx = tap // 3, tap % 3
                    last = nc.tensor.matmul(o[:, 0:TC], diag[:, m, tap, :], xin[:, m, dy:dy + ROWS, dx:dx + SIDE],
                                            start=(tap == 0), stop=(tap == 8))
                if end == 9:
                    last.then_inc(filled.sem, 1)

            def x_proj(n):
                o = use(n, "xp")
                pe.wait_ge(u_set.sem, u_set.after(n, "u"))
                for m in range(ND):
                    last = nc.tensor.matmul(o[0:LOW, 0:TC], xpw[:, m, :], u[:, m, :], start=(m == 0), stop=(m == ND - 1))
                last.then_inc(filled.sem, 1)

            def dt(n, m, nxt):
                o = use(n, f"dt{m}")
                if m == 0:
                    pe.wait_ge(low_low.sem, low_low.after(n, "x"))
                nc.tensor.matmul(o[:, 0:TC], dtw_r[:, bass.ts(m, P)], low[:, nxt, :], start=True, stop=True).then_inc(filled.sem, 1)

            def back(n, m):
                o = use(n, f"back{m}")
                if m == 0:
                    pe.wait_ge(normed.sem, normed.after(n, f"{ND - 1}"))
                for j in range(ND):
                    last = nc.tensor.transpose(o[:, bass.ts(j, P)], yt[:, j, bass.ts(m, P)], ident[:])
                last.then_inc(filled.sem, 1)

            def out(n, h):
                o = use(n, f"out{h}")
                if h == 0:
                    pe.wait_ge(gated.sem, gated.after(n, "x"))
                cols, lo = (P, 0) if h == 0 else (HALF, P)
                for m in range(ND):
                    last = nc.tensor.matmul(o[0:cols, 0:TC], wout[:, m, lo:lo + cols], og[:, m, :], start=(m == 0), stop=(m == ND - 1))
                last.then_inc(filled.sem, 1)

            def z_in(n, m):
                o = use(n, f"z{m}")[:, 0:TC]
                if m == 0:
                    pe.wait_ge(xz_in.sem, xz_in.after(n, "x"))
                nc.tensor.matmul(o, win_a[:, DI + m * P:DI + m * P + P], xz_a[:], start=True, stop=False)
                nc.tensor.matmul(o, win_b[:, DI + m * P:DI + m * P + P], xz_b[:], start=False, stop=True).then_inc(filled.sem, 1)

            def spread_b(n, s, par):
                pe.wait_ge(b_copied.sem, b_copied.after(n, "3") if s == 4 else b_copied.before(n, f"{s}"))
                if s == 0:
                    pe.wait_ge(low_low.sem, low_low.after(n, "x"))
                nc.tensor.matmul(bps[:, 0:TC], pick_r[:, s:s + 1].broadcast_to([P, P]), low[:, par, :],
                                 start=True, stop=True).then_inc(b_spread.sem, 1)

            def spread_c(n, s, par):
                if s >= 2:
                    pe.wait_ge(scaled.sem, scaled.after(n, f"{s - 2}"))
                elif n.reg is not None or n.off > 0:
                    pe.wait_ge(scaled.sem, scaled.after(n.shift(-1), f"{s + ST - 2}"))
                nc.tensor.matmul(cps[:, s % 2, 0:TC], pick_r[:, ST + s:ST + s + 1].broadcast_to([P, P]), low[:, par, :],
                                 start=True, stop=True).then_inc(c_spread.sem, 1)

            def gather_up(n, s):
                pe.wait_ge(scaled.sem, scaled.after(n, f"{s}"))
                if s == BY_PE[0] and n.later():
                    pe.wait_ge(summed.sem, summed.after(n.shift(-1), f"{ND - 1}"))
                for m in range(ND):
                    last = nc.tensor.matmul(gather[:, m, 0:TC], ident[:], prod[:, s % RING, m, :], start=(s == BY_PE[0]), stop=(s == BY_PE[-1]))
                last.then_inc(gathered.sem, 1)

            def emit(n, par):
                X, A, S, O = on("X", n), on("A", n), on("S", n), on("O", n)
                for s in range(ST):
                    if S:
                        spread_c(n, s, par)
                    if S and s - 2 in BY_PE:
                        gather_up(n, s - 2)
                    if S and s + 5 < ST:
                        spread_b(n, s + 5, par)
                    if A and s + 5 >= ST:
                        spread_b(n, s + 5 - ST, 1 - par)
                    if A and s < 4:
                        conv(n, 1 + s // 2, 4 * (s % 2), 4 + 5 * (s % 2))
                    if O and 1 <= s <= 3:
                        if s == 1:
                            pe.wait_ge(summed.sem, summed.after(n.shift(-1), f"{ND - 1}"))
                        y_back(n, s - 1)
                    if A and s == 5:
                        x_proj(n)
                    if S and s == 6:
                        z_in(n, 0)
                    if A and s == 7:
                        dt(n, 0, 1 - par), dt(n, 1, 1 - par)
                    if A and s == 8:
                        dt(n, 2, 1 - par)
                    if X and s == 8:
                        pe.wait_ge(xc_in.sem, xc_in.after(n, "x"))
                        x_in(n, 0)
                    if O and s == 9:
                        back(n, 0)
                    if X and s == 9:
                        x_in(n, 1)
                    if O and s == 10:
                        back(n, 1), back(n, 2)
                    if X and s == 11:
                        x_in(n, 2)
                    if S and s in (11, 12):
                        z_in(n, s - 10)
                    if O and s in (13, 14):
                        out(n, s - 13)
                    if X and s >= 14:
                        conv(n, 0, 3 * (s - 14), 3 + 6 * (s - 14))

            steps(pe, emit)

        @block.scalar
        def _(act):
            act.wait_ge(loaded, 16 * NLOADS)
            nc.scalar.activation(aneg[:], alog[:], ACT.Exp).then_inc(alogged, 1)
            act.wait_ge(prepared, 3)

            def filled_by(n, name):
                act.wait_ge(filled.sem, filled.after(n, name))
                return fill[:, bank_of[name], :]

            def more(n, first):
                return n.reg is not None or n.off > first

            def take_y(n, j):
                o = filled_by(n, f"yT{j}")
                if j == 0 and more(n, 1):
                    act.wait_ge(filled.sem, filled.after(n.shift(-1), "back2"))
                nc.scalar.activation(yt[:, j, :], o[:, 0:DI], ACT.Copy).then_inc(yt_set.sem, 1)

            def take_xin(n, m):
                o = filled_by(n, f"xin{m}")
                nc.scalar.activation(xin[:, m, :, 1:SIDE + 1], o[:, 0:TH].rearrange("p (r w) -> p r w", w=SIDE),
                                     ACT.Copy).then_inc(xin_set.sem, 1)

            def take_conv(n, m):
                o = filled_by(n if m else n.shift(-1), f"conv{m}")
                nc.scalar.activation(pre[:, m, :], o[:, 0:TC], ACT.Identity, bias=vecs[:, 0, m:m + 1]).then_inc(pre_set.sem, 1)

            def take_z(n, m):
                o = filled_by(n, f"z{m}")
                if m == 0 and on("O", n):
                    act.wait_ge(sz_set.sem, sz_set.after(n, "sz"))
                nc.scalar.activation(zpre[:, m, :], o[:, 0:TC], ACT.Copy).then_inc(zpre_set.sem, 1)

            def take_dt(n, m, nxt):
                o = filled_by(n, f"dt{m}")
                if m == 0 and more(n, -1):
                    act.wait_ge(delta_set.sem, delta_set.after(n.shift(-1), "x"))
                nc.scalar.activation(soft[:, m, :], o[:, 0:TC], ACT.Abs, bias=vecs[:, 1, m:m + 1]).then_inc(abs_set.sem, 1)
                if m == 0 and n.later():
                    act.wait_ge(decayed.sem, decayed.after(n.shift(-1), f"{ST - 1}.{ND - 1}"))
                nc.scalar.activation(delta[:, nxt, m, :], o[:, 0:TC], ACT.Relu, bias=vecs[:, 1, m:m + 1]).then_inc(dt_set.sem, 1)

            def take_back(n, m):
                o = filled_by(n, f"back{m}")
                if m == 0 and more(n, 1):
                    act.wait_ge(filled.sem, filled.after(n.shift(-1), "out1"))
                nc.scalar.activation(og[:, m, :], o[:, 0:TC], ACT.Identity, bias=vecs[:, 4, m:m + 1],
                                     scale=vecs[:, 3, m:m + 1]).then_inc(affined.sem, 1)

            def take_out(n, h):
                rows = P if h == 0 else HALF
                o = filled_by(n, f"out{h}")
                if h == 0 and more(n, 1):
                    act.wait_ge(stored.sem, stored.after(n.shift(-1), "x"))
                nc.scalar.activation(fz[0:rows, h, :], o[0:rows, 0:TC], ACT.Identity, bias=fub[0:rows, h:h + 1]).then_inc(fz_set.sem, 1)

            def silus(n):
                if on("A", n):
                    act.wait_ge(pre_set.sem, pre_set.after(n, f"{ND - 1}"))
                    if more(n, -1):
                        act.wait_ge(du_set.sem, du_set.after(n.shift(-1), "x"))
                    nc.scalar.activation(u[:], pre[:], ACT.Silu).then_inc(u_set.sem, 1)
                if on("O", n):
                    act.wait_ge(zpre_set.sem, zpre_set.after(n.shift(-1), f"{ND - 1}"))
                    if more(n, 1):
                        act.wait_ge(gated.sem, gated.after(n.shift(-1), "x"))
                    nc.scalar.activation(sz[:], zpre[:], ACT.Silu).then_inc(sz_set.sem, 1)

            def softplus_exp(n):
                act.wait_ge(abs_set.sem, abs_set.after(n, f"{ND - 1}"))
                nc.scalar.activation(soft[:], soft[:], ACT.Exp, scale=-1.0).then_inc(exp_set.sem, 1)

            def softplus_log(n):
                act.wait_ge(exp_set.sem, exp_set.after(n, "x"))
                nc.scalar.activation(soft[:], soft[:], ACT.Ln, bias=1.0).then_inc(ln_set.sem, 1)

            def decays(n, s, par):
                for m in range(ND):
                    if s == 0 and m == 0:
                        act.wait_ge(delta_set.sem, delta_set.after(n, "x"))
                    if s >= RING:
                        act.wait_ge(scanned.sem, scanned.after(n, f"{s - RING}.{m}"))
                    elif s >= AHEAD and n.later():
                        act.wait_ge(scanned.sem, scanned.after(n.shift(-1), f"{s + ST - RING}.{m}"))
                    elif s < AHEAD and on("S", n):
                        act.wait_ge(scanned.sem, scanned.after(n, f"{s + ST - RING}.{m}"))
                    nc.scalar.activation(decay[:, s % RING, m, :], delta[:, par, m, :], ACT.Exp,
                                         scale=aneg[:, m, s:s + 1]).then_inc(decayed.sem, 1)

            def copy_b(n, t, early):
                spread = b_spread.after(n, f"{t}") if early or t > 4 else b_spread.after(n.shift(-1), f"{t}")
                act.wait_ge(b_spread.sem, spread)
                if t >= 4:
                    act.wait_ge(driven.sem, driven.after(n, f"{t - 4}") if t - 4 >= 3 else driven.after(n.shift(-1), f"{t - 4}"))
                elif on("S", n):
                    act.wait_ge(driven.sem, driven.after(n, f"{t + ST - 4}"))
                nc.scalar.activation(brow[:, t % RING, :], bps[:, 0:TC], ACT.Copy).then_inc(b_copied.sem, 1)

            def emit(n, par):
                X, A, S, O = on("X", n), on("A", n), on("S", n), on("O", n)
                for s in range(ST):
                    if S and s + 4 < ST:
                        copy_b(n, s + 4, False)
                    if A and s + 4 >= ST:
                        copy_b(n, s + 4 - ST, True)
                    if O and s == 11:
                        take_back(n, 1), take_back(n, 2)
                    if S and s + AHEAD < ST:
                        decays(n, s + AHEAD, par)
                    if A and s + AHEAD >= ST:
                        decays(n, s + AHEAD - ST, 1 - par)
                    if A and s in (0, 2, 4):
                        take_conv(n, s // 2)
                    if O and 2 <= s <= 4:
                        take_y(n, s - 2)
                    if s == 4:
                        silus(n)
                    if A and s == 6:
                        x_low(n, 1 - par)
                    if S and s == 7:
                        take_z(n, 0)
                    if A and s == 8:
                        take_dt(n, 0, 1 - par), take_dt(n, 1, 1 - par)
                    if A and s == 9:
                        take_dt(n, 2, 1 - par)
                    if X and s == 9:
                        take_xin(n, 0)
                    if A and s == 9:
                        softplus_exp(n)
                    if A and s == 10:
                        softplus_log(n)
                    if O and s == 10:
                        take_back(n, 0)
                    if X and s == 10:
                        take_xin(n, 1)
                    if X and s == 12:
                        take_xin(n, 2)
                    if S and s in (12, 13):
                        take_z(n, s - 11)
                    if O and s >= 14:
                        take_out(n, s - 14)

            def x_low(n, nxt):
                o = filled_by(n, "xp")
                if n.reg is not None or n.off > 0:
                    act.wait_ge(c_spread.sem, c_spread.after(n.shift(-1), f"{ST - 1}"))
                nc.scalar.activation(low[0:LOW, nxt, :], o[0:LOW, 0:TC], ACT.Copy).then_inc(low_high.sem, 1)

            steps(act, emit)

        @block.gpsimd
        def _(pool):
            nc.gpsimd.memset(mhalf[:], -0.5).then_inc(prepared, 1)
            pool.wait_ge(loaded, 16 * NLOADS)

            def emit(n, par):
                A, S, O = on("A", n), on("S", n), on("O", n)
                nxt = 1 - par
                for s in range(ST):
                    sB = s + 3
                    if (S and sB < ST) or (A and sB >= ST):
                        t = sB % ST
                        mine = nxt if sB >= ST else par
                        pool.wait_ge(b_copied.sem, b_copied.after(n.shift(-1), "3") if t == 3 else b_copied.after(n, f"{t}"))
                        if sB >= ST:
                            pool.wait_ge(du_set.sem, du_set.after(n, "x"))
                        if t >= 4:
                            pool.wait_ge(scanned.sem, scanned.after(n, f"{t - 4}.{ND - 1}"))
                        elif sB >= ST and S:
                            pool.wait_ge(scanned.sem, scanned.after(n, f"{t + ST - 4}.{ND - 1}"))
                        elif t == 3 and (n.reg is not None or n.off > 0):
                            pool.wait_ge(scanned.sem, scanned.after(n.shift(-1), f"{ST - 1}.{ND - 1}"))
                        nc.gpsimd.tensor_tensor(drive[:, t % RING], du[:, mine], brow[:, t % RING, :].unsqueeze(1).broadcast_to([P, ND, TC]),
                                                ALU.mult).then_inc(driven.sem, 1)
                    if S and s:
                        take_carry(n, n, s - 1)
                    elif O and s == 0:
                        take_carry(n, n.shift(-1), ST - 1)
                    if O and s == 7:
                        mv_set_value = held(pool, mv_set.after(n, "x"))
                        pool.wait_ge(loaded, 16 * NLOADS)
                        pool.wait_ge(mv_set.sem, mv_set_value)
                        nc.gpsimd.tensor_scalar(rstd[:, 0, :], mv[:, :, 1], EPS, 1.0, ALU.add, ALU.mult).then_inc(veps_set.sem, 1)
                        pool.wait_ge(veps_set.sem, veps_set.after(n, "x"))
                        nc.gpsimd.tensor_tensor(rstd[:, 1, :], rstd[:, 0, :], mhalf[:], ALU.pow).then_inc(rstd_set.sem, 1)
                    if A and s == 11:
                        pool.wait_ge(ln_set.sem, ln_set.after(n, "x"))
                        pool.wait_ge(dt_set.sem, dt_set.after(n, f"{ND - 1}"))
                        nc.gpsimd.tensor_tensor(delta[:, nxt], delta[:, nxt], soft[:], ALU.add).then_inc(delta_set.sem, 1)
                        pool.wait_ge(delta_set.sem, delta_set.after(n, "x"))
                        nc.gpsimd.tensor_tensor(du[:, nxt], delta[:, nxt], u[:], ALU.mult).then_inc(du_set.sem, 1)
                    if O and s == 12:
                        pool.wait_ge(affined.sem, affined.after(n, f"{ND - 1}"))
                        pool.wait_ge(sz_set.sem, sz_set.after(n, "sz"))
                        nc.gpsimd.tensor_tensor(og[:], og[:], sz[:], ALU.mult).then_inc(gated.sem, 1)
                    if A and s == 8:
                        u_value = held(pool, u_set.after(n, "u"))
                        if S:
                            added_value = held(pool, added.after(n, f"{BY_DVE[0]}"))
                        pool.wait_ge(loaded, 16 * NLOADS)
                        pool.wait_ge(u_set.sem, u_value)
                        if S:
                            pool.wait_ge(added.sem, added_value)
                        for m in range(ND):
                            last = nc.gpsimd.tensor_scalar(ud[:, m, :], u[:, m, :], vecs[:, 2, m:m + 1], 1.0, ALU.mult, ALU.mult)
                        last.then_inc(ud_set.sem, 1)

            def take_carry(n, chunk, s):
                scanned_value = held(pool, scanned.after(chunk, f"{s}.{ND - 1}"))
                pool.wait_ge(loaded, 16 * NLOADS)
                pool.wait_ge(scanned.sem, scanned_value)
                nc.gpsimd.tensor_tensor(carry[:, s, :], hst[:, s % RING, :, TC - 1], keep[:, bass.ds(chunk.linear(ND, 0), ND)],
                                        ALU.mult).then_inc(carried.sem, 1)

            steps(pool, emit)

        @block.vector
        def _(dve):
            dve.wait_ge(loaded, 16 * NLOADS)
            nc.vector.tensor_copy(pick_r[:], pick[:])
            nc.vector.tensor_copy(dtw_r[:], dtw[:]).then_inc(cut, 1)
            dve.wait_ge(cut, 1)
            nc.vector.tensor_tensor(dtw[:], dtw[:], dtw_r[:], ALU.subtract).then_inc(cut, 1)
            dve.wait_ge(cut, 2)
            nc.vector.tensor_scalar(dtw[:], dtw[:], parts[:, 1:2], None, ALU.mult).then_inc(cut, 1)
            dve.wait_ge(cut, 3)
            nc.vector.scalar_tensor_tensor(dtw_r[:], dtw_r[:], parts[:, 0:1], dtw[:], ALU.mult, ALU.add)
            for m in range(ND):
                for tap in range(9):
                    last = nc.vector.tensor_scalar(diag[:, m, tap, :], ident[:], cw[:, m, tap:tap + 1], None, ALU.mult)
            nc.vector.memset(xin[:, :, :, 0:1], 0.0)
            last = nc.vector.memset(xin[:, :, :, SIDE + 1:SIDE + 2], 0.0).then_inc(prepared, 1)
            for m in range(ND):
                dve.wait_ge(merged, m + 1)
                nc.vector.tensor_copy(wout[:, m, :], fill[:, m % 2, 0:CH]).then_inc(mergedone, 1)
            dve.wait_ge(alogged, 1)
            nc.vector.tensor_scalar(aneg[:], aneg[:], -1.0, None, ALU.mult).then_inc(prepared, 1)

            def scale(n, s):
                dve.wait_ge(scanned.sem, scanned.after(n, f"{s}.{ND - 1}"))
                dve.wait_ge(c_spread.sem, c_spread.after(n, f"{s}"))
                if s >= RING or n.later():
                    step, t = (n, s - RING) if s >= RING else (n.shift(-1), s + ST - RING)
                    c = gathered if t in BY_PE else added
                    dve.wait_ge(c.sem, c.after(step, f"{t}"))
                nc.vector.tensor_tensor(prod[:, s % RING], hst[:, s % RING], cps[:, s % 2, 0:TC].unsqueeze(1).broadcast_to([P, ND, TC]),
                                        ALU.mult).then_inc(scaled.sem, 1)

            def add(n, s):
                dve.wait_ge(scaled.sem, scaled.after(n, f"{s}"))
                if s == BY_DVE[0]:
                    dve.wait_ge(ud_set.sem, ud_set.after(n.shift(-1), "x"))
                    if n.later():
                        dve.wait_ge(summed.sem, summed.after(n.shift(-1), f"{ND - 1}"))
                else:
                    dve.wait_ge(added.sem, added.before(n, f"{s}"))
                nc.vector.tensor_tensor(total[:], (ud if s == BY_DVE[0] else total)[:], prod[:, s % RING], ALU.add).then_inc(added.sem, 1)

            def add_up(n):
                dve.wait_ge(added.sem, added.after(n, f"{BY_DVE[-1]}"))
                dve.wait_ge(gathered.sem, gathered.after(n, f"{BY_PE[-1]}"))
                if n.later():
                    dve.wait_ge(filled.sem, filled.after(n, "yT2"))
                for m in range(ND):
                    nc.vector.tensor_tensor(ysum[:, m, :], gather[:, m, 0:TC], total[:, m, :], ALU.add).then_inc(summed.sem, 1)

            def emit(n, par):
                A, S, O = on("A", n), on("S", n), on("O", n)
                nxt = 1 - par
                later = n.reg is not None or n.off > 0
                for s in range(ST):
                    if S:
                        for m in range(ND):
                            if m == 0:
                                dve.wait_ge(driven.sem, driven.after(n, f"{s}") if s >= 3 else driven.after(n.shift(-1), f"{s}"))
                                if s >= RING:
                                    dve.wait_ge(scaled.sem, scaled.after(n, f"{s - RING}"))
                                    dve.wait_ge(carried.sem, carried.after(n, f"{s - RING}"))
                                elif later:
                                    dve.wait_ge(scaled.sem, scaled.after(n.shift(-1), f"{s + ST - RING}"))
                                    if s < RING - 1:
                                        dve.wait_ge(carried.sem, carried.after(n.shift(-1), f"{s + ST - RING}"))
                                    else:
                                        dve.wait_ge(carried.sem, carried.after(n, f"{ST - 1}"))
                            dve.wait_ge(decayed.sem, decayed.after(n if s >= AHEAD else n.shift(-1), f"{s}.{m}"))
                            nc.vector.tensor_tensor_scan(hst[:, s % RING, m, :], decay[:, s % RING, m, :], drive[:, s % RING, m, :],
                                                         carry[:, s, m:m + 1] if later else 0.0, ALU.mult, ALU.add).then_inc(scanned.sem, 1)
                        if s >= 1:
                            scale(n, s - 1)
                        if s - 2 in BY_DVE:
                            add(n, s - 2)
                    if O and s == 6:
                        for j in range(ND):
                            dve.wait_ge(yt_set.sem, yt_set.after(n, f"{j}"))
                            nc.vector.bn_stats(st6[:, j, :], yt[:, j, :]).then_inc(stat_set.sem, 1)
                        stat_set_value = held(dve, stat_set.after(n, f"{ND - 1}"))
                        dve.wait_ge(loaded, 16 * NLOADS)
                        dve.wait_ge(stat_set.sem, stat_set_value)
                        for j in range(ND):
                            last = nc.vector.bn_aggr(mv[:, j, :], st6[:, j, :])
                        last.then_inc(mv_set.sem, 1)
                    if O and s == 8:
                        dve.wait_ge(rstd_set.sem, rstd_set.after(n, "x"))
                        for j in range(ND):
                            nc.vector.tensor_scalar(yt[:, j, :], yt[:, j, :], mv[:, j, 0:1], rstd[:, 1, j:j + 1],
                                                    ALU.subtract, ALU.mult).then_inc(normed.sem, 1)
                    if A and s == 7:
                        dve.wait_ge(low_high.sem, low_high.after(n, "x"))
                        if n.reg is not None or n.off > 0:
                            dve.wait_ge(c_spread.sem, c_spread.after(n.shift(-1), f"{ST - 1}"))
                        nc.vector.tensor_tensor(low[LOW:P, nxt, :], fill[0:LOW, bank_of["xp"], 0:TC], low[0:LOW, nxt, :],
                                                ALU.subtract).then_inc(low_low.sem, 1)
                if S:
                    scale(n, ST - 1)
                    if ST - 2 in BY_DVE:
                        add(n, ST - 2)
                    add(n, ST - 1)
                    add_up(n)

            steps(dve, emit)


def sedenion_signs():
    def conj(x):
        return x if len(x) == 1 else np.concatenate([conj(x[:len(x) // 2]), -x[len(x) // 2:]])

    def mult(a, b):
        if len(a) == 1:
            return a * b
        h = len(a) // 2
        a1, a2, b1, b2 = a[:h], a[h:], b[:h], b[h:]
        return np.concatenate([mult(a1, b1) - mult(conj(b2), a2), mult(b2, a1) + mult(a2, conj(b1))])

    eye = np.eye(NK, dtype=np.int64)
    return [[int(mult(eye[i], eye[i ^ k])[k]) for k in range(NK)] for i in range(NK)]


def layer1(nc, d, nimg):
    when = {"H": (-1, nimg - 2), "E": (0, nimg - 1)}
    sign = sedenion_signs()
    pairs = range(NK // 2)
    tails = sorted({(sign[2 * p][2 * q] * sign[2 * p][2 * q + 1], sign[2 * p + 1][2 * q] * sign[2 * p + 1][2 * q + 1])
                    for p in pairs for q in pairs})
    ctx = ExitStack()
    with ctx:
        def sb(name, shape, dt=F32):
            return ctx.enter_context(nc.sbuf_tensor(name, shape, dt))

        def ps(name, shape):
            return ctx.enter_context(nc.psum_tensor(name, shape, F32))

        def sem(name):
            return ctx.enter_context(nc.semaphore(name))

        def count(name, kind, events, w=1):
            return Count(sem(name), when, [(e, kind or ("H" if "H" in e else "E"), w) for e in events])

        wmm, wkt = sb("wmm", [P, NK, P]), sb("wkt", [P, NK, P])
        wmt, wtt = sb("wmt", [P, 2, NK, P]), sb("wtt", [P, len(tails), NK // 2, P])
        pw_a, pw_b = sb("pw_a", [P, CH]), sb("pw_b", [P, 2, CH])
        f1w, f1t, f1l = sb("f1w", [P, 2, HID], F32R), sb("f1t", [P, HID], F32R), sb("f1l", [HALF, HID], F32R)
        f2w, f2t = sb("f2w", [P, 2, NM, P], F32R), sb("f2t", [P, NM, P], F32R)
        vec = sb("vec", [P, 6, 2])
        b1 = sb("b1", [P, NM])
        sgn = sb("sgn", [P, 4])
        idn = sb("idn", [P, P])
        half = sb("half", [P, NB])
        fn_a, fn_b = sb("fn_a", [P, TOK]), sb("fn_b", [HALF, TOK])
        fst, fmv, frs = sb("fst", [P, 2, NCH, 6]), sb("fmv", [P, 2, 2]), sb("frs", [P, 4, 2])
        x1_a, x1_b = sb("x1_a", [P, 2, TOK]), sb("x1_b", [HALF, 2, TOK])
        xt = sb("xt", [BL, TURN, NB, CH])
        tst, tmv, trs = sb("tst", [BL, NB, 6]), sb("tmv", [BL, 2, NB, 2]), sb("trs", [BL, 2, 2, NB])
        xm = sb("xm", [P, 2, NK, WT])
        tpp, tpm = sb("tpp", [P, 2, NK // 2, WT]), sb("tpm", [P, 2, NK // 2, WT])
        neg, ypre, ym = sb("neg", [P, 3, WT]), sb("ypre", [P, 3, WT]), sb("ym", [P, 3, WT])
        x2_a, x2_b = sb("x2_a", [P, 2, GT]), sb("x2_b", [HALF, 2, GT])
        xa_a, xa_b = sb("xa_a", [P, GT]), sb("xa_b", [HALF, GT])
        xs, xt2 = sb("xs", [P, 2, GT], F32R), sb("xt2", [P, GT], F32R)
        h1, hs = sb("h1", [P, 2, GT]), sb("hs", [P, 2, NM, GT], F32R)
        o_a, o_b = sb("o_a", [P, 2, GT]), sb("o_b", [HALF, 2, GT])
        wps = ps("wps", [P, 3, BANK])
        fill = ps("fill5", [P, 5, BANK])

        TURNS = {2: (0,), 3: (1,), 4: (2, 3), 5: (4, 5), 6: (6, 7)}
        turns = lambda g: TURNS.get(g, ())
        SLOTS = range(1, NG + 1)

        def windows_of(n, g):
            if g < NG:
                return (n, g) if on("E", n) else None
            return (n.shift(1), 0) if on("H", n) else None

        def done_in(i, g):
            return i if g else i.shift(-1)

        def group_before(i, g):
            if g:
                return i, g - 1
            return (i.shift(-1), NG - 1) if on("E", i.shift(-1)) else None

        uses, groups = [], []
        for g in SLOTS:
            m = g - 1
            if m >= 0:
                uses += [f"projM{m}a", f"projM{m}b"]
                groups.append(f"M{m}")
            uses += [f"backH{q}{h}" for q in turns(g - 1)[:1] for h in "ab"]
            if m >= 0:
                uses += [f"turnM{m}a", f"turnM{m}b"]
            uses += [f"backH{q}{h}" for q in turns(g - 1)[1:] for h in "ab"]
            if m >= 0:
                uses += [f"backM{m}a", f"backM{m}b"]
            uses += [f"turnH{q}{h}" for q in turns(g) for h in "ab"]
            groups += [f"H{q}" for q in turns(g)]
            if m >= 0:
                uses += [f"fcoM{m}{j}" for j in range(NM)] + [f"fctM{m}a", f"fctM{m}b"]
        NBANK = 5
        bank_of = {u: i % NBANK for i, u in enumerate(uses)}
        order = {u: i for i, u in enumerate(groups)}
        ab = lambda names: [f"{n}{h}" for n in names for h in "ab"]
        gs = [f"{g}" for g in range(NG)]

        cloaded = sem("cloaded")
        wloaded, wset, wready, wcut = sem("wloaded"), sem("wset"), sem("wready"), sem("wcut")
        filled = count("filled1", None, uses)
        fn_in, xp_in = count("fn_in", "H", ["x"], 32), count("xp_in", "H", ["x"], 32)
        fst_set = count("fst_set", "H", [f"{h}{c}" for h in "ab" for c in range(NCH)])
        fmv_set, fve, frs_set = count("fmv_set", "H", "ab"), count("fve", "H", ["x"]), count("frs_set", "H", ["x"])
        fnm, fnb = count("fnm", "H", ["x"]), count("fnb", "H", ["x"])
        spread = count("spread1", "H", [f"{h}{r}" for r in range(WIN) for h in "ab"])
        x1_set = count("x1_set", "H", ab(gs))
        turned = count("turned", None, ab(groups))
        tst_set = count("tst_set", None, [f"{q}.{j}" for q in groups for j in range(NB)])
        tmv_set, tve, trs_set = count("tmv_set", None, groups), count("tve", None, groups), count("trs_set", None, groups)
        normed = count("normed1", None, [f"{q}.{j}" for q in groups for j in range(NB)])
        xm_set, tpp_set = count("xm_set", "H", gs), count("tpp_set", "H", [f"{g}{h}" for g in gs for h in "01"])
        tpm_set = count("tpm_set", "H", ["x"])
        wgroups = [*gs[1:], "0"]

        def of_windows(name, events):
            return Count(sem(name), when, [(e, "H" if e[0] == "0" else "E", 1) for e in events])

        wtile = [f"{g}.{t}" for g in wgroups for t in range(3)]
        wdone, neg_set, ypre_set = of_windows("wdone", wtile), of_windows("neg_set", wtile), of_windows("ypre_set", wtile)
        ym_set = of_windows("ym_set", wgroups)
        x2_set, xa_set, xs_set = count("x2_set", "E", ab(gs)), count("xa_set", "E", ab(gs)), count("xs_set", "E", ab(gs))
        hhigh_set = count("hhigh_set", "E", [f"{g}{m}" for g in gs for m in range(1, NM, 2)])
        hs_set = count("hs_set", "E", [f"{g}{m}" for g in gs for m in range(NM)])
        h1_set = count("h1_set", "E", [f"{g}{m}" for g in gs for m in range(NM)])
        tail_set = count("tail_set", "E", gs)
        o_set = count("o_set", "E", ab(gs))
        o_out = [count(f"o_out{par}", "E", [g for g in gs if int(g) % 2 == par], 32) for par in range(2)]

        def reader(use):
            what, rest = use[:4], use[4:]
            g = rest[1:-1]
            if what == "turn":
                return turned, rest
            if what == "back":
                if rest[0] == "M":
                    return xa_set, rest[1:]
                return (xm_set, g) if rest[-1] == "a" else (tpp_set, g + "1")
            return {"proj": (x2_set, rest[1:]), "fcoM": (h1_set, use[4:]), "fctM": (o_set, use[4:])}[what if what == "proj" else use[:4]]

        def on(kind, n):
            return n.reg is not None or when[kind][0] <= n.off <= when[kind][1]

        def more(kind, n):
            return n.reg is not None or n.off > when[kind][0]

        def before_it(n, name, names, ring):
            i = names.index(name)
            for back in range(3):
                step = n.shift(-back)
                for k in reversed(range(i if back == 0 else len(names))):
                    if k % ring == i % ring and on("H" if "H" in names[k] else "E", step):
                        return step, names[k]
            return None

        def prior(c, n):
            return c.after(n.shift(-1), c.events[-1][0])

        block = ctx.enter_context(nc.Block())

        def images(eng, emit):
            emit(At(-1), 1)
            emit(At(0), 0)
            with eng.Fori(0, (nimg - 2) // 2) as b:
                emit(At(1, b, 2), 1)
                emit(At(2, b, 2), 0)
            emit(At(nimg - 1), (nimg - 1) % 2)

        raw = xm[:, 1].rearrange("p k w -> p (k w)")
        raw1, raw2, raw1t = raw[:, 0:HID], raw[:, HID:HID + NM * CH], tpp[:, 1].rearrange("p k w -> p (k w)")[:, 0:HID]
        consts = [(sgn, d["sgn"]), (idn, d["ident"]), (b1, d["b1"]), (vec[:, :, 0:1], d["vec"][:, 0:P].rearrange("v (p o) -> p v o", o=1)),
                  (vec[0:HALF, :, 1:2], d["vec"][:, P:CH].rearrange("v (p o) -> p v o", o=1))]
        CONSTS = 16 * len(consts)
        loads = [(wmm, d["wmm"]), (wkt, d["wkt"]), (wmt[:, 0], d["wmt"]), (wtt[:, 0], d["wtt"]),
                 (pw_a, d["pw"][0:P]), (pw_b[0:HALF, 0], d["pw"][P:CH]), (pw_b[HALF:P, 1], d["pw"][P:CH]),
                 (raw1, d["f1"][0:P]), (raw1t[0:HALF], d["f1"][P:CH]), (raw1t[HALF:P], d["f1"][P:CH]),
                 (raw2.rearrange("p (j c) -> p j c", j=NM), d["f2"])]

        @block.sync
        def _(sp):
            for dst, src in consts:
                with nc.allow_non_contiguous_dma(reason="a few hundred numbers, once"):
                    sp.dma_start(dst if isinstance(dst, bass.AP) else dst[:], src).then_inc(cloaded, 16)

            def emit(n, par):
                if not on("H", n):
                    return
                if more("H", n):
                    fn_value, x1_value = held(sp, prior(fn_in, n)), held(sp, prior(x1_set, n))
                    sp.wait_ge(cloaded, CONSTS)
                    sp.wait_ge(fn_in.sem, fn_value)
                    sp.wait_ge(x1_set.sem, x1_value)
                src = d["fz"][bass.ds(n.linear(NCH, NCH), NCH)]
                sp.dma_start(fn_a[:].rearrange("p (c t) -> p c t", c=NCH), src[:, 0:P, :].rearrange("c p t -> p c t")).then_inc(fn_in.sem, 16)
                sp.dma_start(fn_b[:].rearrange("p (c t) -> p c t", c=NCH), src[:, P:CH, :].rearrange("c p t -> p c t")).then_inc(fn_in.sem, 16)
                if on("E", n) and more("E", n):
                    xp_value, x2_value = held(sp, prior(xp_in, n)), held(sp, prior(x2_set, n))
                    sp.wait_ge(cloaded, CONSTS)
                    sp.wait_ge(xp_in.sem, xp_value)
                    sp.wait_ge(x2_set.sem, x2_value)
                sp.dma_start(x1_a[:, 1 - par, :], d["xperm"][n.linear(1, 1), 0:P, :]).then_inc(xp_in.sem, 16)
                sp.dma_start(x1_b[:, 1 - par, :], d["xperm"][n.linear(1, 1), P:CH, :]).then_inc(xp_in.sem, 16)
                if not more("H", n):
                    for dst, src in loads:
                        sp.dma_start(dst if isinstance(dst, bass.AP) else dst[:], src).then_inc(wloaded, 16)

            images(sp, emit)

        @block.gpsimd
        def _(pool):
            for i, (dst, value) in enumerate([(half[:], -0.5), (fmv[:], 1.0), (pw_b[HALF:P, 0], 0.0), (pw_b[0:HALF, 1], 0.0)]):
                nc.gpsimd.memset(dst, value).then_inc(wset, 1)
                pool.wait_ge(wset, i + 1)

            def rstd(n, q):
                r = order[q] % 2
                tmv_set_value = held(pool, tmv_set.after(n, q))
                pool.wait_ge(cloaded, CONSTS)
                pool.wait_ge(tmv_set.sem, tmv_set_value)
                nc.gpsimd.tensor_scalar(trs[:, r, 0], tmv[:, r, :, 1], EPS, 1.0, ALU.add, ALU.mult).then_inc(tve.sem, 1)
                pool.wait_ge(tve.sem, tve.after(n, q))
                nc.gpsimd.tensor_tensor(trs[:, r, 1], trs[:, r, 0], half[0:BL], ALU.pow).then_inc(trs_set.sem, 1)

            def store(n, g):
                pool.wait_ge(o_set.sem, o_set.after(n, f"{g}b"))
                c = o_out[g % 2]
                for dst, lo, hi in ((o_a, 0, P), (o_b, P, CH)):
                    pool.dma_start(d["out"][n.linear(1, 0), lo:hi, bass.ts(g, GT)], dst[:, g % 2, :]).then_inc(c.sem, 16)

            def emit(n, par):
                for g in SLOTS:
                    if on("E", n):
                        rstd(n, f"M{g - 1}")
                    if on("H", n) and g == 1:
                        if more("H", n):
                            pool.wait_ge(spread.sem, prior(spread, n))
                        fmv_value = held(pool, fmv_set.after(n, "b"))
                        pool.wait_ge(cloaded, CONSTS)
                        pool.wait_ge(fmv_set.sem, fmv_value)
                        nc.gpsimd.tensor_scalar(frs[:, 0], fmv[:, :, 1], EPS, 1.0, ALU.add, ALU.mult).then_inc(fve.sem, 1)
                        pool.wait_ge(fve.sem, fve.after(n, "x"))
                        nc.gpsimd.tensor_tensor(frs[:, 1], frs[:, 0], half[:, 0:2], ALU.pow).then_inc(frs_set.sem, 1)
                        pool.wait_ge(frs_set.sem, frs_set.after(n, "x"))
                        nc.gpsimd.tensor_tensor(frs[:, 2], frs[:, 1], fmv[:, :, 0], ALU.mult).then_inc(fnm.sem, 1)
                        fnm_value = held(pool, fnm.after(n, "x"))
                        pool.wait_ge(cloaded, CONSTS)
                        pool.wait_ge(fnm.sem, fnm_value)
                        nc.gpsimd.tensor_scalar(frs[:, 3], frs[:, 2], -1.0, 1.0, ALU.mult, ALU.mult).then_inc(fnb.sem, 1)
                    if on("H", n):
                        for q in turns(g):
                            rstd(n, f"H{q}")
                    if on("E", n):
                        store(n, g - 1)

            images(pool, emit)
            for c in o_out:
                pool.wait_ge(c.sem, 32 * NG // 2 * nimg)

        @block.tensor
        def _(pe):
            pe.wait_ge(cloaded, CONSTS)

            def use(n, name):
                earlier = before_it(n, name, uses, NBANK)
                if earlier is not None:
                    step, user = earlier
                    c, event = reader(user)
                    value = c.after(step, event)
                    if name[:4] in ("turn", "back") and name[-1] == "b":
                        value = held(pe, value)
                        pe.wait_ge(cloaded, CONSTS)
                    pe.wait_ge(c.sem, value)
                return fill[:, bank_of[name], :]

            def turn(n, q, src_a, src_b):
                o = use(n, f"turn{q}a")
                for j in range(NB):
                    last = nc.tensor.transpose(o[0:BL, bass.ts(j, P)], src_a[:, bass.ts(j, BL)], idn[:])
                last.then_inc(filled.sem, 1)
                o = use(n, f"turn{q}b")
                for j in range(NB):
                    last = nc.tensor.transpose(o[0:BL, bass.ts(j, HALF)], src_b[:, bass.ts(j, BL)], idn[0:HALF, 0:HALF])
                last.then_inc(filled.sem, 1)

            def back(n, q):
                pe.wait_ge(normed.sem, normed.after(n, f"{q}.{NB - 1}"))
                r = order[q] % TURN
                o = use(n, f"back{q}a")
                for j in range(NB):
                    last = nc.tensor.transpose(o[:, bass.ts(j, BL)], xt[:, r, j, 0:P], idn[0:BL, 0:BL])
                last.then_inc(filled.sem, 1)
                o = use(n, f"back{q}b")
                for j in range(NB):
                    last = nc.tensor.transpose(o[0:HALF, bass.ts(j, BL)], xt[:, r, j, P:CH], idn[0:BL, 0:BL])
                last.then_inc(filled.sem, 1)

            def window(n, g, t, par):
                earlier = group_before(n, g)
                if earlier is not None:
                    pe.wait_ge(ypre_set.sem, ypre_set.after(done_in(*earlier), f"{earlier[1]}.{t}"))
                plus, minus = [], []
                k0, k1 = 2 * g, 2 * g + 1
                for i in range(NK):
                    k = k1 if t == 1 else k0
                    w = wmm[:, i ^ k, :] if t < 2 else wmt[:, (1 - sign[i][k0] * sign[i][k1]) // 2, i ^ k0, :]
                    (plus if sign[i][k] > 0 else minus).append((w, xm[:, par, i, :]))
                for p in pairs:
                    k = k1 if t == 1 else k0
                    a, b = sign[2 * p][k], sign[2 * p + 1][k]
                    if t < 2:
                        w = wkt[:, (2 * p) ^ k, :]
                    else:
                        w = wtt[:, tails.index((a * sign[2 * p][k1], b * sign[2 * p + 1][k1])), ((2 * p) ^ k0) // 2, :]
                    (plus if a > 0 else minus).append((w, (tpp if a * b > 0 else tpm)[:, par, p, :]))
                for part, terms in enumerate([plus, minus]):
                    for e, (w, x) in enumerate(terms):
                        last = nc.tensor.matmul(wps[:, t, part * WT:(part + 1) * WT], w, x, start=(e == 0), stop=(e == len(terms) - 1))
                last.then_inc(wdone.sem, 1)

            def proj(n, g):
                pe.wait_ge(ym_set.sem, ym_set.after(done_in(n, g), f"{g}"))
                for h, lo, m in (("a", 0, P), ("b", P, HALF)):
                    o = use(n, f"projM{g}{h}")
                    nc.tensor.matmul(o[0:m, 0:GT], pw_a[:, lo:lo + m], ym[:, 0:2, :].rearrange("p a w -> p (a w)"), start=True, stop=False)
                    nc.tensor.matmul(o[0:m, 0:WT], pw_b[:, 0, lo:lo + m], ym[:, 2, :], start=False, stop=False)
                    nc.tensor.matmul(o[0:m, WT:GT], pw_b[:, 1, lo:lo + m], ym[:, 2, :], start=False, stop=True).then_inc(filled.sem, 1)

            def emit(n, par):
                H, E = on("H", n), on("E", n)
                for g in SLOTS:
                    m, w, wpar = g - 1, windows_of(n, g), par if g < NG else 1 - par
                    if E:
                        proj(n, m)
                    if H:
                        for q in turns(g - 1)[:1]:
                            back(n, f"H{q}")
                    if w and g == NG:
                        pe.wait_ge(xm_set.sem, xm_set.after(n, f"{NG - 1}"))
                        pe.wait_ge(tpm_set.sem, tpm_set.after(n, "x"))
                        if not more("H", n):
                            pe.wait_ge(wset, 4)
                            pe.wait_ge(wready, 4)
                            pe.wait_ge(wloaded, 16 * len(loads))
                    if w:
                        window(*w, 0, wpar)
                    if E:
                        pe.wait_ge(x2_set.sem, x2_set.after(n, f"{m}b"))
                        turn(n, f"M{m}", x2_a[:, m % 2, :], x2_b[:, m % 2, :])
                    if H:
                        for q in turns(g - 1)[1:]:
                            back(n, f"H{q}")
                    if w:
                        window(*w, 1, wpar)
                    if E:
                        back(n, f"M{m}")
                    if w:
                        window(*w, 2, wpar)
                    if H:
                        for q in turns(g):
                            pe.wait_ge(x1_set.sem, x1_set.after(n, f"{q}b"))
                            turn(n, f"H{q}", x1_a[:, 1 - par, bass.ts(q, GT)], x1_b[:, 1 - par, bass.ts(q, GT)])
                    if E:
                        pe.wait_ge(xs_set.sem, xs_set.after(n, f"{m}b"))
                        for j in range(NM):
                            o = use(n, f"fcoM{m}{j}")[:, 0:GT]
                            cols = bass.ts(j, P)
                            nc.tensor.matmul(o, f1w[:, 0, cols], xs[:, 0, :], start=True, stop=False)
                            nc.tensor.matmul(o, f1w[:, 1, cols], xs[:, 0, :], start=False, stop=False)
                            nc.tensor.matmul(o, f1w[:, 0, cols], xs[:, 1, :], start=False, stop=False)
                            nc.tensor.matmul(o, f1t[:, cols], xt2[:], start=False, stop=False)
                            nc.tensor.matmul(o, f1l[:, cols], xt2[0:HALF], start=False, stop=True).then_inc(filled.sem, 1)
                        terms = {"a": ((f2w[:, 0], 0), (f2w[:, 1], 0), (f2w[:, 0], 1)), "b": ((f2t, 0), (f2t, 1))}
                        for h in "ab":
                            o = use(n, f"fctM{m}{h}")[:, 0:GT]
                            for j in range(NM):
                                pe.wait_ge(hs_set.sem, hs_set.after(n, f"{m}{j}"))
                                for k, (weights, part) in enumerate(terms[h]):
                                    last = nc.tensor.matmul(o, weights[:, j, :], hs[:, part, j, :], start=(j + k == 0),
                                                            stop=(j == NM - 1 and k == len(terms[h]) - 1))
                            last.then_inc(filled.sem, 1)

            images(pe, emit)

        @block.scalar
        def _(act):
            act.wait_ge(cloaded, CONSTS)

            def filled_by(n, name):
                act.wait_ge(filled.sem, filled.after(n, name))
                return fill[:, bank_of[name], :]

            def take_turn(n, q):
                r = order[q] % TURN
                o = filled_by(n, f"turn{q}a")
                earlier = before_it(n, q, groups, TURN)
                if earlier is not None:
                    act.wait_ge(filled.sem, filled.after(earlier[0], f"back{earlier[1]}b"))
                nc.scalar.activation(xt[:, r, :, 0:P], o[0:BL, 0:NB * P].rearrange("p (j c) -> p j c", j=NB), ACT.Copy).then_inc(turned.sem, 1)
                o = filled_by(n, f"turn{q}b")
                nc.scalar.activation(xt[:, r, :, P:CH], o[0:BL, 0:NB * HALF].rearrange("p (j c) -> p j c", j=NB), ACT.Copy).then_inc(turned.sem, 1)

            def negative(n, g, t):
                act.wait_ge(wdone.sem, wdone.after(done_in(n, g), f"{g}.{t}"))
                earlier = group_before(n, g)
                if t == 0 and earlier is not None:
                    act.wait_ge(ypre_set.sem, ypre_set.after(done_in(*earlier), f"{earlier[1]}.2"))
                nc.scalar.activation(neg[:, t, :], wps[:, t, WT:2 * WT], ACT.Copy).then_inc(neg_set.sem, 1)

            def finish_layer0(n):
                act.wait_ge(frs_set.sem, frs_set.after(n, "x"))
                act.wait_ge(fnb.sem, fnb.after(n, "x"))
                for r in range(WIN):
                    for h, (buf, rows) in enumerate([(fn_a, P), (fn_b, HALF)]):
                        rowsof = buf[:].rearrange("p (wh r x) -> p r wh x", r=WIN, wh=NW)[:, r]
                        nc.scalar.activation(rowsof, rowsof, ACT.Identity, bias=frs[0:rows, 3, h:h + 1],
                                             scale=frs[0:rows, 1, h:h + 1]).then_inc(spread.sem, 1)

            def take_windows(n, g, nxt):
                o = filled_by(n, f"backH{g}a")
                if g == 0 and on("E", n) and more("E", n):
                    act.wait_ge(wdone.sem, prior(wdone, n))
                nc.scalar.activation(xm[:, nxt, 2 * g:2 * g + 2, :].rearrange("p a w -> p (a w)"), o[:, 0:GT], ACT.Identity,
                                     bias=vec[:, 1, 0:1], scale=vec[:, 0, 0:1]).then_inc(xm_set.sem, 1)
                o = filled_by(n, f"backH{g}b")
                for h in range(2):
                    nc.scalar.activation(tpp[h * HALF:(h + 1) * HALF, nxt, g, :], o[0:HALF, h * WT:(h + 1) * WT], ACT.Identity,
                                         bias=vec[0:HALF, 1, 1:2], scale=vec[0:HALF, 0, 1:2]).then_inc(tpp_set.sem, 1)

            def emit(n, par):
                H, E = on("H", n), on("E", n)
                for g in SLOTS:
                    m, w = g - 1, windows_of(n, g)
                    if H:
                        for q in turns(g - 1)[:1]:
                            take_windows(n, q, 1 - par)
                    if w:
                        negative(*w, 0)
                    if E:
                        take_turn(n, f"M{m}")
                    if H:
                        for q in turns(g - 1)[1:]:
                            take_windows(n, q, 1 - par)
                    if w:
                        negative(*w, 1)
                    if E:
                        for c, (h, high, dst, rows) in enumerate([("a", xs[:, 0, :], xa_a, P), ("b", xt2[0:HALF], xa_b, HALF)]):
                            o = filled_by(n, f"backM{m}{h}")[0:rows, 0:GT]
                            g2, b2 = vec[0:rows, 3, c:c + 1], vec[0:rows, 4, c:c + 1]
                            nc.scalar.activation(high, o, ACT.Identity, bias=b2, scale=g2)
                            nc.scalar.activation(dst[:], o, ACT.Identity, bias=b2, scale=g2).then_inc(xa_set.sem, 1)
                    if w:
                        negative(*w, 2)
                    if H:
                        for q in turns(g):
                            take_turn(n, f"H{q}")
                    if E:
                        for j in range(NM):
                            o = filled_by(n, f"fcoM{m}{j}")
                            if j == 0:
                                if m:
                                    act.wait_ge(filled.sem, filled.after(n, f"fctM{m - 1}b"))
                                elif more("E", n):
                                    act.wait_ge(filled.sem, prior(filled, n))
                            if j % 2 == 0:
                                nc.scalar.activation(hs[:, 0, j, :], o[:, 0:GT], ACT.Gelu, bias=b1[:, j:j + 1])
                            if m or j >= 2:
                                act.wait_ge(hs_set.sem, hs_set.before(n, f"{m}{j}") - 1)
                            elif more("E", n):
                                act.wait_ge(hs_set.sem, hs_set.after(n.shift(-1), f"{NG - 1}{NM - 2 + j}"))
                            nc.scalar.activation(h1[:, j % 2, :], o[:, 0:GT], ACT.Gelu, bias=b1[:, j:j + 1]).then_inc(h1_set.sem, 1)
                    if w:
                        act.wait_ge(ypre_set.sem, ypre_set.after(done_in(*w), f"{w[1]}.2"))
                        nc.scalar.activation(ym[:], ypre[:], ACT.Gelu).then_inc(ym_set.sem, 1)
                    if H and g == 1:
                        finish_layer0(n)

            images(act, emit)

        @block.vector
        def _(dve):
            dve.wait_ge(cloaded, CONSTS)
            dve.wait_ge(wset, 4)

            def prepare_weights():
                dve.wait_ge(wloaded, 16 * len(loads))
                nc.vector.tensor_copy(wmt[:, 1, :, 0:HALF], wmt[:, 0, :, 0:HALF])
                nc.vector.tensor_scalar(wmt[:, 1, :, HALF:P], wmt[:, 0, :, HALF:P], -1.0, None, ALU.mult).then_inc(wready, 1)
                for v in range(1, len(tails)):
                    nc.vector.tensor_copy(wtt[:, v, :, 0:HALF], wtt[:, 0, :, 0:HALF])
                for v in reversed(range(len(tails))):
                    col = [(1, 1), (1, -1), (-1, 1), (-1, -1)].index(tails[v])
                    if v == 0:
                        last.then_inc(wready, 1)
                        dve.wait_ge(wready, 2)
                    last = nc.vector.tensor_scalar(wtt[:, v, :, HALF:P], wtt[:, 0, :, HALF:P], sgn[:, col:col + 1], None, ALU.mult)
                last.then_inc(wready, 1)
                nc.vector.tensor_copy(f1w[:, 0, :], raw1)
                nc.vector.tensor_copy(f1t[:], raw1t)
                raw2v = raw2.rearrange("p (j c) -> p j c", j=NM)
                nc.vector.tensor_copy(f2w[:, 0], raw2v[:, :, 0:P])
                nc.vector.tensor_copy(f2t[:, :, 0:HALF], raw2v[:, :, P:CH]).then_inc(wcut, 1)
                dve.wait_ge(wcut, 1)
                nc.vector.tensor_tensor(f1w[:, 1, :], raw1, f1w[:, 0, :], ALU.subtract)
                nc.vector.tensor_tensor(f1l[:], raw1t[0:HALF], f1t[0:HALF], ALU.subtract)
                nc.vector.tensor_tensor(f2w[:, 1], raw2v[:, :, 0:P], f2w[:, 0], ALU.subtract)
                nc.vector.tensor_tensor(f2t[:, :, HALF:P], raw2v[:, :, P:CH], f2t[:, :, 0:HALF], ALU.subtract).then_inc(wready, 1)

            def statistics(n, q):
                r, r2 = order[q] % TURN, order[q] % 2
                dve.wait_ge(turned.sem, turned.after(n, f"{q}b"))
                if q != "H0" or more("H", n):
                    dve.wait_ge(normed.sem, normed.before(n, f"{q}.0"))
                for j in range(NB):
                    nc.vector.bn_stats(tst[:, j, :], xt[:, r, j, :]).then_inc(tst_set.sem, 1)
                tst_set_value = held(dve, tst_set.after(n, f"{q}.{NB - 1}"))
                dve.wait_ge(cloaded, CONSTS)
                dve.wait_ge(tst_set.sem, tst_set_value)
                for j in range(NB):
                    last = nc.vector.bn_aggr(tmv[:, r2, j, :], tst[:, j, :])
                last.then_inc(tmv_set.sem, 1)

            def normalise(n, q):
                r, r2 = order[q] % TURN, order[q] % 2
                dve.wait_ge(trs_set.sem, trs_set.after(n, q))
                for j in range(NB):
                    nc.vector.tensor_scalar(xt[:, r, j, :], xt[:, r, j, :], tmv[:, r2, j, 0:1], trs[:, r2, 1, j:j + 1],
                                            ALU.subtract, ALU.mult).then_inc(normed.sem, 1)

            def subtract(n, g, t):
                dve.wait_ge(neg_set.sem, neg_set.after(done_in(n, g), f"{g}.{t}"))
                earlier = group_before(n, g)
                if t == 0 and earlier is not None:
                    dve.wait_ge(ym_set.sem, ym_set.after(done_in(*earlier), f"{earlier[1]}"))
                nc.vector.tensor_tensor(ypre[:, t, :], wps[:, t, 0:WT], neg[:, t, :], ALU.subtract).then_inc(ypre_set.sem, 1)

            def layer0_statistics(n):
                dve.wait_ge(fn_in.sem, fn_in.after(n, "x"))
                if more("H", n):
                    dve.wait_ge(fnm.sem, prior(fnm, n))
                for h, (src, rows) in enumerate([(fn_a, P), (fn_b, HALF)]):
                    for c in range(NCH):
                        nc.vector.bn_stats(fst[0:rows, h, c, :], src[:, bass.ts(c, TC)]).then_inc(fst_set.sem, 1)
                    fst_set_value = held(dve, fst_set.after(n, f"{'ab'[h]}{NCH - 1}"))
                    dve.wait_ge(cloaded, CONSTS)
                    dve.wait_ge(fst_set.sem, fst_set_value)
                    nc.vector.bn_aggr(fmv[0:rows, h, :], fst[0:rows, h, :, :].rearrange("p c s -> p (c s)")).then_inc(fmv_set.sem, 1)

            def add_input(n, q, nxt):
                r, c0 = 2 * q // WIN, 2 * q % WIN
                if q == 0:
                    dve.wait_ge(xp_in.sem, xp_in.after(n, "x"))
                for h, dst, src in (("a", x1_a, fn_a), ("b", x1_b, fn_b)):
                    dve.wait_ge(spread.sem, spread.after(n, f"{h}{r}"))
                    o = dst[:, nxt, bass.ts(q, GT)].rearrange("p (c wh ww) -> p c wh ww", c=2, wh=NW)
                    i = src[:].rearrange("p (wh r ww c) -> p r c wh ww", r=WIN, ww=NW, c=WIN)[:, r, c0:c0 + 2]
                    nc.vector.tensor_tensor(o, o, i, ALU.add).then_inc(x1_set.sem, 1)

            def emit(n, par):
                H, E = on("H", n), on("E", n)
                for g in SLOTS:
                    m, w = g - 1, windows_of(n, g)
                    if E:
                        for c, (h, dst, x1, rows) in enumerate([("a", x2_a, x1_a, P), ("b", x2_b, x1_b, HALF)]):
                            use = f"projM{m}{h}"
                            dve.wait_ge(filled.sem, filled.after(n, use))
                            if m >= 2:
                                dve.wait_ge(turned.sem, turned.after(n, f"M{m - 2}b"))
                                dve.wait_ge(o_set.sem, o_set.after(n, f"{m - 2}b"))
                            elif more("E", n):
                                dve.wait_ge(o_set.sem, prior(o_set, n))
                            nc.vector.scalar_tensor_tensor(dst[:, m % 2, :], fill[0:rows, bank_of[use], 0:GT], vec[0:rows, 2, c:c + 1],
                                                           x1[:, par, bass.ts(m, GT)], ALU.add, ALU.add).then_inc(x2_set.sem, 1)
                    if w:
                        subtract(*w, 0)
                    if E:
                        statistics(n, f"M{m}")
                        normalise(n, f"M{m}")
                    if w:
                        subtract(*w, 1)
                    if E:
                        dve.wait_ge(xa_set.sem, xa_set.after(n, f"{m}a"))
                        nc.vector.tensor_tensor(xs[:, 1, :], xa_a[:], xs[:, 0, :], ALU.subtract).then_inc(xs_set.sem, 1)
                        dve.wait_ge(xa_set.sem, xa_set.after(n, f"{m}b"))
                        nc.vector.tensor_tensor(xt2[HALF:P], xa_b[:], xt2[0:HALF], ALU.subtract).then_inc(xs_set.sem, 1)
                    if H and g == 1:
                        layer0_statistics(n)
                    if H and g == 4 and not more("H", n):
                        prepare_weights()
                    if H:
                        for q in turns(g):
                            add_input(n, q, 1 - par)
                    if w:
                        subtract(*w, 2)
                    if H and turns(g):
                        statistics(n, f"H{turns(g)[0]}")
                    if H and g == NG - 1:
                        dve.wait_ge(tpp_set.sem, tpp_set.after(n, f"{NG - 1}1"))
                        nc.vector.tensor_scalar(tpm[:, 1 - par].rearrange("p a w -> p (a w)"), tpp[:, 1 - par].rearrange("p a w -> p (a w)"),
                                                sgn[:, 1:2], None, ALU.mult).then_inc(tpm_set.sem, 1)
                    if E:
                        for j in range(NM):
                            dve.wait_ge(h1_set.sem, h1_set.after(n, f"{m}{j}"))
                            if j % 2:
                                nc.vector.tensor_copy(hs[:, 0, j, :], h1[:, 1, :]).then_inc(hhigh_set.sem, 1)
                                dve.wait_ge(hhigh_set.sem, hhigh_set.after(n, f"{m}{j}"))
                            nc.vector.tensor_tensor(hs[:, 1, j, :], h1[:, j % 2, :], hs[:, 0, j, :], ALU.subtract).then_inc(hs_set.sem, 1)
                    if H and turns(g):
                        normalise(n, f"H{turns(g)[0]}")
                    if E:
                        for h, dst, x2, rows in (("a", o_a, x2_a, P), ("b", o_b, x2_b, HALF)):
                            use = f"fctM{m}{h}"
                            dve.wait_ge(filled.sem, filled.after(n, use))
                            c = o_out[m % 2]
                            if m >= 2:
                                dve.wait_ge(c.sem, c.after(n, f"{m - 2}"))
                            elif more("E", n):
                                dve.wait_ge(c.sem, prior(c, n))
                            col, bank = "ab".index(h), fill[:, bank_of[use], 0:GT]
                            end = nc.vector.scalar_tensor_tensor(dst[:, m % 2, :], bank[0:rows], vec[0:rows, 5, col:col + 1],
                                                                 x2[:, m % 2, :], ALU.add, ALU.add)
                            if h == "b":
                                end.then_inc(tail_set.sem, 1)
                                dve.wait_ge(tail_set.sem, tail_set.after(n, f"{m}"))
                                end = nc.vector.tensor_tensor(dst[:, m % 2, :], bank[HALF:P], dst[:, m % 2, :], ALU.add)
                            end.then_inc(o_set.sem, 1)
                    if H:
                        for q in turns(g)[1:]:
                            statistics(n, f"H{q}")
                            normalise(n, f"H{q}")

            images(dve, emit)


def layers(nc, d):
    d = dict(d)
    d["fz"] = nc.dram_tensor("fused_dram", (IMG * NCH, CH, TC), F32, kind="Internal").ap()
    layer0(nc, d, IMG)
    layer1(nc, d, IMG)


def layouts(a):
    def tiles(v):
        return v.reshape((ND, P) + v.shape[1:]).swapaxes(0, 1)

    x = a["x"]
    padded = np.zeros((IMG, CH, SIDE + 2, SIDE), x.dtype)
    padded[:, :, 1:SIDE + 1] = x
    keep = np.ones((P, IMG * NCH, ND), np.float32)
    keep[:, NCH - 1::NCH] = 0
    xw = a["L0_conv_x_proj_w"]
    dtw, parts = np.zeros((P, DI), np.float32), np.zeros((P, 2), np.float32)
    for half in range(2):
        for part in range(2):
            rows = slice(half * LOW + 2 * ST + part * RANK, half * LOW + 2 * ST + (part + 1) * RANK)
            dtw[rows] = a["L0_conv_dt_proj_w"].T
            parts[rows, part] = 1
    w = a["L1_conv_w_sed"]
    other = np.arange(NK) ^ 1
    mm, mt, tm, tt = w[:, :P, :P], w[:, :P, P:], w[:, P:, :P], w[:, P:, P:]
    even = np.arange(0, NK, 2)
    sgn = np.ones((P, 4), np.float32)
    sgn[HALF:, 1] = sgn[:HALF, 2] = sgn[:, 3] = -1
    return dict(
        xch=np.stack([padded[:, :, ROWS * c:ROWS * (c + 1) + 2].reshape(IMG, CH, TH) for c in range(NCH)], 1).reshape(-1, CH, TH),
        win=a["L0_conv_in_proj_w"].T,
        cw=tiles(a["L0_conv_conv_w"].reshape(DI, 9)),
        xpw=tiles(np.concatenate([xw[RANK:], xw[:RANK], xw[:RANK], np.zeros((LOW - 2 * ST - 2 * RANK, DI), xw.dtype)]).T),
        dtw=dtw, parts=parts,
        opw=a["L0_conv_out_proj_w"],
        fuw=a["L0_conv_fuse_w"][:, :, 0, 0].T,
        vecs=np.stack([tiles(a["L0_conv_" + k]) for k in ("conv_b", "dt_proj_b", "D_param", "ln_g", "ln_b")], 1),
        alog=tiles(a["L0_conv_A_log"]),
        ident=np.eye(P, dtype=np.float32),
        pick=np.tile(np.eye(LOW, 2 * ST, dtype=np.float32), (2, 1)),
        keep=keep.reshape(P, -1),
        fub=a["L0_conv_fuse_b"].reshape(CH, 1),
        xperm=x.reshape(IMG, CH, NW, WIN, NW, WIN).transpose(0, 1, 3, 5, 2, 4).reshape(IMG, CH, TOK),
        wmm=mm.transpose(1, 0, 2),
        wkt=np.concatenate([tm, tm[other]], 1).transpose(1, 0, 2),
        wmt=np.concatenate([mt, mt[other]], 2).transpose(1, 0, 2),
        wtt=np.concatenate([np.concatenate([tt[even], tt[even + 1]], 2), np.concatenate([tt[even + 1], tt[even]], 2)], 1).transpose(1, 0, 2),
        pw=a["L1_conv_proj_w"], f1=a["L1_conv_fc1_w"],
        f2=a["L1_conv_fc2_w"].reshape(NM, P, CH).transpose(1, 0, 2),
        vec=np.stack([a["L1_conv_" + k] for k in ("norm1_g", "norm1_b", "proj_b", "norm2_g", "norm2_b", "fc2_b")]),
        b1=a["L1_conv_fc1_b"].reshape(NM, P).T,
        sgn=sgn)


def kernel(**inputs):
    import concourse.bacc as bacc
    from concourse.bass_utils import run_bass_kernel_spmd

    nc = bacc.Bacc("TRN2", target_bir_lowering=False, num_devices=1)
    arrays, d = {}, {}
    for name, a in layouts({k: np.asarray(v) for k, v in inputs.items()}).items():
        arrays[f"{name}_dram"] = np.ascontiguousarray(a)
        d[name] = nc.dram_tensor(f"{name}_dram", a.shape, F32, kind="ExternalInput").ap()
    d["out"] = nc.dram_tensor("out_dram", (IMG, CH, TOK), F32, kind="ExternalOutput").ap()
    layers(nc, d)
    got = run_bass_kernel_spmd(nc, [arrays], core_ids=[0]).results[0]["out_dram"]
    return got.reshape(IMG, CH, WIN, WIN, NW, NW).transpose(0, 1, 4, 2, 5, 3).reshape(IMG, CH, SIDE, SIDE)
```
